# Optimizing a Trainium2 kernel written in Bass

```python
import numpy as np
import jax
import jax.numpy as jnp

def _softmax(x, axis=-1):
    return jax.nn.softmax(x, axis=axis)

def _gelu(x):
    return jax.nn.gelu(x, approximate=True)

def _silu(x):
    return jax.nn.silu(x)

def _sigmoid(x):
    return jax.nn.sigmoid(x)

def _layernorm(x, axis=-1, eps=1e-05):
    m = jnp.mean(x, axis=axis, keepdims=True)
    v = jnp.var(x, axis=axis, keepdims=True)
    return (x - m) / jnp.sqrt(v + eps)

def _scatter_add(tgt, idx, src, axis=0):
    return tgt.at[idx].add(src)

def _segment_sum(src, seg, n):
    return jax.ops.segment_sum(src, seg, n)
kernel_name = 'mk_xattn_seq_d4_seqx_r4_6c9fbd'

def setup_inputs(seed: int=0):
    np.random.seed(seed)
    _w = jnp.asarray

    def _rec_inputs():
        import jax
        import jax.numpy as jnp
        _rk = jax.random.key(seed)
        x = -0.0002928 + 1 * jax.random.normal(jax.random.fold_in(_rk, 1), (16, 128, 512), jnp.float32)
        _lenS = 128 - jax.random.randint(jax.random.fold_in(_rk, 7), (16,), 0, max(1, 128 // 4) + 1, jnp.int32)
        _lenS2 = 128 - jax.random.randint(jax.random.fold_in(_rk, 8), (16,), 0, max(1, 128 // 4) + 1, jnp.int32)
        _ctx_2048P = jax.random.normal(jax.random.fold_in(_rk, 11), (16, 16, 512), jnp.float32)
        _ctx_2048c = jax.random.dirichlet(jax.random.fold_in(_rk, 511), 0.3 * jnp.ones((16,), jnp.float32), (16, 128))
        _ctx_2048t = jnp.einsum('bsk,bkd->bsd', _ctx_2048c, _ctx_2048P)
        _ctx_2048t = _ctx_2048t * jax.lax.rsqrt(jnp.mean(jnp.square(_ctx_2048t)) + 1e-12) * 0.953939
        ctx_2048 = -1.39393e-06 + 0.999914 * (_ctx_2048t + 0.3 * jax.random.normal(jax.random.fold_in(_rk, 611), (16, 128, 512), jnp.float32))
        _validS = jnp.arange(128)[None, :] < _lenS[:, None]
        _validS2 = jnp.arange(128)[None, :] < _lenS2[:, None]
        _causal = jnp.tril(jnp.ones((128, 128), dtype=bool))
        mask_1x1xSxS2_fc1 = jnp.where(jnp.broadcast_to(_validS2[0:1, None, None, :], (1, 1, 128, 128)), 1.0, 0.0).astype(jnp.float32)
        mask_Bx1xSxS2_ff1 = jnp.where(jnp.ones((16, 1, 128, 128), dtype=bool), 1.0, 0.0).astype(jnp.float32)
        mask_Bx1xSxS2_ff0 = jnp.where(jnp.ones((16, 1, 128, 128), dtype=bool), 0.0, -1000000000.0).astype(jnp.float32)
        mask_BxS2_ik0 = jnp.where(jnp.broadcast_to(_validS2[:, :], (16, 128)), 0, 1).astype(jnp.int32)
        return (x, ctx_2048, mask_1x1xSxS2_fc1, mask_Bx1xSxS2_ff1, mask_Bx1xSxS2_ff0, mask_BxS2_ik0)
    x, ctx_2048, mask_1x1xSxS2_fc1, mask_Bx1xSxS2_ff1, mask_Bx1xSxS2_ff0, mask_BxS2_ik0 = _rec_inputs()

    def _L0_xattn_setup():
        import jax, jax.numpy as jnp
        import numpy as np
        H = 512
        NH = 16
        HD = H // NH
        EPS = 1e-05

        def gelu(x):
            return 0.5 * x * (1.0 + jnp.tanh(0.7978845608028654 * x * (1.0 + 0.044715 * x * x)))

        def layernorm(x, scale, bias):
            m = jnp.mean(x, axis=-1, keepdims=True)
            v = jnp.mean(jnp.square(x - m), axis=-1, keepdims=True)
            return (x - m) * jax.lax.rsqrt(v + EPS) * scale + bias

        def split_heads(x):
            b, s, _ = x.shape
            return x.reshape(b, s, NH, HD).transpose(0, 2, 1, 3)

        def merge_heads(x):
            b, nh, s, hd = x.shape
            return x.transpose(0, 2, 1, 3).reshape(b, s, nh * hd)

        def attention(q, k, v, mask):
            scores = jnp.einsum('bhqd,bhkd->bhqk', q, k) / jnp.sqrt(jnp.float32(HD))
            scores = scores * mask - 10000.0 * (1.0 - mask)
            probs = jax.nn.softmax(scores, axis=-1)
            return jnp.einsum('bhqk,bhkd->bhqd', probs, v)
        key = jax.random.key(seed)
        ks = jax.random.split(key, 16)
        b, s, t = (2, 256, 256)
        w = lambda k, i, o: jax.random.normal(k, (i, o), jnp.float32) * 0.02
        inp = {'hidden_states': jax.random.normal(ks[0], (b, s, H), jnp.float32), 'encoder_states': jax.random.normal(ks[1], (b, t, H), jnp.float32), 'ltor_mask': jnp.tril(jnp.ones((1, 1, s, s), jnp.float32)), 'cross_mask': jnp.ones((b, 1, s, t), jnp.float32), 'ln1_s': jnp.ones((H,), jnp.float32), 'ln1_b': jnp.zeros((H,), jnp.float32), 'w_qkv': w(ks[2], H, 3 * H), 'b_qkv': jnp.zeros((3 * H,), jnp.float32), 'w_ao': w(ks[3], H, H), 'b_ao': jnp.zeros((H,), jnp.float32), 'ln2_s': jnp.ones((H,), jnp.float32), 'ln2_b': jnp.zeros((H,), jnp.float32), 'w_q': w(ks[4], H, H), 'b_q': jnp.zeros((H,), jnp.float32), 'w_kv': w(ks[5], H, 2 * H), 'b_kv': jnp.zeros((2 * H,), jnp.float32), 'w_co': w(ks[6], H, H), 'b_co': jnp.zeros((H,), jnp.float32), 'ln3_s': jnp.ones((H,), jnp.float32), 'ln3_b': jnp.zeros((H,), jnp.float32), 'w1': w(ks[7], H, 4 * H), 'b1': jnp.zeros((4 * H,), jnp.float32), 'w2': w(ks[8], 4 * H, H), 'b2': jnp.zeros((H,), jnp.float32)}
        return inp
    _L0_xattn_all = _L0_xattn_setup()
    _L0_xattn_in = {k: v for k, v in _L0_xattn_all.items() if k in ('ln1_s', 'ln1_b', 'w_qkv', 'b_qkv', 'w_ao', 'b_ao', 'ln2_s', 'ln2_b', 'w_q', 'b_q', 'w_kv', 'b_kv', 'w_co', 'b_co', 'ln3_s', 'ln3_b', 'w1', 'b1', 'w2', 'b2')}
    del _L0_xattn_all

    def _L1_xattn_setup():
        import jax, jax.numpy as jnp
        import numpy as np
        H = 512
        NH = 32
        KVH = 8
        HD = H // NH
        GROUPS = NH // KVH
        EPS = 1e-06
        B, L, S = (4, 256, 256)

        def _gqa_forward(hidden_state, encoder_hidden_state, encoder_attention_mask, Wq, bq, Wk, bk, Wv, bv, Wo, bo, gamma, beta):
            b, l, _ = hidden_state.shape
            s = encoder_hidden_state.shape[1]
            q = hidden_state @ Wq + bq
            k = encoder_hidden_state @ Wk + bk
            v = encoder_hidden_state @ Wv + bv
            q = q.reshape(b, l, KVH, GROUPS, HD).transpose(0, 2, 3, 1, 4)
            k = k.reshape(b, s, KVH, HD).transpose(0, 2, 1, 3)
            v = v.reshape(b, s, KVH, HD).transpose(0, 2, 1, 3)
            scale = 1.0 / jnp.sqrt(jnp.asarray(HD, q.dtype))
            scores = jnp.einsum('bkgld,bksd->bkgls', q, k) * scale
            scores = scores + encoder_attention_mask[:, :, None, :, :]
            attn = jax.nn.softmax(scores, axis=-1)
            out = jnp.einsum('bkgls,bksd->bkgld', attn, v)
            out = out.transpose(0, 3, 1, 2, 4).reshape(b, l, H)
            out = out @ Wo + bo
            x = out + hidden_state
            mu = jnp.mean(x, axis=-1, keepdims=True)
            var = jnp.var(x, axis=-1, keepdims=True)
            return (x - mu) * jax.lax.rsqrt(var + EPS) * gamma + beta
        key = jax.random.key(seed)
        ks = jax.random.split(key, 12)
        sd = 0.02
        return {'hidden_state': jax.random.normal(ks[0], (B, L, H), jnp.float32), 'encoder_hidden_state': jax.random.normal(ks[1], (B, S, H), jnp.float32), 'encoder_attention_mask': jnp.zeros((B, 1, L, S), jnp.float32), 'Wq': jax.random.normal(ks[2], (H, H), jnp.float32) * sd, 'bq': jnp.zeros((H,), jnp.float32), 'Wk': jax.random.normal(ks[3], (H, KVH * HD), jnp.float32) * sd, 'bk': jnp.zeros((KVH * HD,), jnp.float32), 'Wv': jax.random.normal(ks[4], (H, KVH * HD), jnp.float32) * sd, 'bv': jnp.zeros((KVH * HD,), jnp.float32), 'Wo': jax.random.normal(ks[5], (H, H), jnp.float32) * sd, 'bo': jnp.zeros((H,), jnp.float32), 'gamma': jnp.ones((H,), jnp.float32), 'beta': jnp.zeros((H,), jnp.float32)}
    _L1_xattn_all = _L1_xattn_setup()
    _L1_xattn_in = {k: v for k, v in _L1_xattn_all.items() if k in ('Wq', 'bq', 'Wk', 'bk', 'Wv', 'bv', 'Wo', 'bo', 'gamma', 'beta')}
    del _L1_xattn_all

    def _L2_xattn_setup():
        import jax, jax.numpy as jnp
        import numpy as np
        E, H, L, B = (512, 32, 256, 4)
        S = E // H
        DM, DD = (32, 64)

        def _ln(x, w, b, eps=1e-05):
            m = x.mean(-1, keepdims=True)
            v = ((x - m) ** 2).mean(-1, keepdims=True)
            return (x - m) / jnp.sqrt(v + eps) * w + b

        def _block(x, state, ln1_w, ln1_b, ln2_w, ln2_b, maa_x, maa_w1, maa_w2, maa_stack, time_decay, td_w1, td_w2, u, Wr, Wk, Wv, Wg, Wo, gn_w, gn_b, ffn_maa_k, ffn_maa_r, Wfk, Wfr, Wfv):
            b, l, e = x.shape
            h = u.shape[0]
            s_ = e // h
            xa = _ln(x, ln1_w, ln1_b)
            sx = jnp.concatenate([state[:, 1:2] - xa[:, :1], xa[:, :-1] - xa[:, 1:]], axis=1)
            xxx = jnp.tanh((xa + sx * maa_x) @ maa_w1).reshape(b, l, 5, DM)
            xxx = jnp.einsum('blfd,fde->blfe', xxx, maa_w2)
            xm = xa[:, :, None] + sx[:, :, None] * (maa_stack + xxx)
            xk, xw, xv, xr, xg = (xm[:, :, j] for j in range(5))
            w = jnp.exp(-jnp.exp(time_decay + jnp.tanh(xw @ td_w1) @ td_w2)).reshape(b, l, h, s_)
            r = (xr @ Wr.T).reshape(b, l, h, s_)
            k = (xk @ Wk.T).reshape(b, l, h, s_)
            v = (xv @ Wv.T).reshape(b, l, h, s_)
            g = jax.nn.silu(xg @ Wg.T)
            s0 = state[:, 2:2 + s_].reshape(b, h, s_, s_)

            def step(s, rkvw):
                r_t, k_t, v_t, w_t = rkvw
                a = k_t[..., :, None] * v_t[..., None, :]
                out = jnp.einsum('bhi,bhij->bhj', r_t, u * a + s)
                s = a + w_t[..., :, None] * s
                return (s, out)
            rkvw = tuple((jnp.moveaxis(t, 1, 0) for t in (r, k, v, w)))
            _, out = jax.lax.scan(step, s0, rkvw)
            out = jnp.moveaxis(out, 0, 1).reshape(b, l, e)
            og = out.reshape(b, l, h, s_)
            m = og.mean(-1, keepdims=True)
            va = ((og - m) ** 2).mean(-1, keepdims=True)
            og = ((og - m) / jnp.sqrt(va + 1e-05)).reshape(b, l, e) * gn_w + gn_b
            x1 = x + og * g @ Wo.T
            xc = _ln(x1, ln2_w, ln2_b)
            sx2 = jnp.concatenate([state[:, 0:1] - xc[:, :1], xc[:, :-1] - xc[:, 1:]], axis=1)
            xk2 = xc + sx2 * ffn_maa_k
            xr2 = xc + sx2 * ffn_maa_r
            rr = jax.nn.sigmoid(xr2 @ Wfr.T)
            kk = jnp.square(jax.nn.relu(xk2 @ Wfk.T))
            return x1 + rr * (kk @ Wfv.T)
        key = jax.random.key(seed)
        ks = jax.random.split(key, 24)
        sc = 0.02
        d = {'x': jax.random.normal(ks[0], (B, L, E), jnp.float32), 'state': jax.random.normal(ks[1], (B, 2 + S, E), jnp.float32) * 0.1, 'ln1_w': jnp.ones((E,), jnp.float32), 'ln1_b': jnp.zeros((E,), jnp.float32), 'ln2_w': jnp.ones((E,), jnp.float32), 'ln2_b': jnp.zeros((E,), jnp.float32), 'maa_x': jax.random.normal(ks[2], (E,), jnp.float32) * 0.1, 'maa_w1': jax.random.normal(ks[3], (E, 5 * DM), jnp.float32) * sc, 'maa_w2': jax.random.normal(ks[4], (5, DM, E), jnp.float32) * sc, 'maa_stack': jax.random.normal(ks[5], (1, 5, E), jnp.float32) * 0.1, 'time_decay': jax.random.normal(ks[6], (E,), jnp.float32) * 0.5, 'td_w1': jax.random.normal(ks[7], (E, DD), jnp.float32) * sc, 'td_w2': jax.random.normal(ks[8], (DD, E), jnp.float32) * sc, 'u': jax.random.normal(ks[9], (H, S, 1), jnp.float32) * 0.1, 'Wr': jax.random.normal(ks[10], (E, E), jnp.float32) * sc, 'Wk': jax.random.normal(ks[11], (E, E), jnp.float32) * sc, 'Wv': jax.random.normal(ks[12], (E, E), jnp.float32) * sc, 'Wg': jax.random.normal(ks[13], (E, E), jnp.float32) * sc, 'Wo': jax.random.normal(ks[14], (E, E), jnp.float32) * sc, 'gn_w': jnp.ones((E,), jnp.float32), 'gn_b': jnp.zeros((E,), jnp.float32), 'ffn_maa_k': jax.random.normal(ks[15], (E,), jnp.float32) * 0.1, 'ffn_maa_r': jax.random.normal(ks[16], (E,), jnp.float32) * 0.1, 'Wfk': jax.random.normal(ks[17], (E, E), jnp.float32) * sc, 'Wfr': jax.random.normal(ks[18], (E, E), jnp.float32) * sc, 'Wfv': jax.random.normal(ks[19], (E, E), jnp.float32) * sc}
        return d
    _L2_xattn_all = _L2_xattn_setup()
    _L2_xattn_in = {k: v for k, v in _L2_xattn_all.items() if k in ('ln1_w', 'ln1_b', 'ln2_w', 'ln2_b', 'maa_x', 'maa_w1', 'maa_w2', 'maa_stack', 'time_decay', 'td_w1', 'td_w2', 'u', 'Wr', 'Wk', 'Wv', 'Wg', 'Wo', 'gn_w', 'gn_b', 'ffn_maa_k', 'ffn_maa_r', 'Wfk', 'Wfr', 'Wfv')}
    del _L2_xattn_all

    def _L3_xattn_setup():
        import jax, jax.numpy as jnp
        import numpy as np
        B, P, K, H, NH = (4, 512, 64, 512, 16)
        DH = H // NH
        EPS = 1e-06

        def rmsnorm(x, w):
            var = jnp.mean(jnp.square(x), axis=-1, keepdims=True)
            return x * jax.lax.rsqrt(var + EPS) * w
        key = jax.random.key(seed)
        ks = jax.random.split(key, 12)
        s = 0.02
        return {'x': jax.random.normal(ks[0], (B, P, H), jnp.float32), 'latents': jax.random.normal(ks[1], (B, K, H), jnp.float32), 'attention_mask': jax.random.randint(ks[2], (B, P), 0, 2, jnp.int32), 'q_w': s * jax.random.normal(ks[3], (H, H), jnp.float32), 'q_b': jnp.zeros((H,), jnp.float32), 'kv_w': s * jax.random.normal(ks[4], (H, 2 * H), jnp.float32), 'kv_b': jnp.zeros((2 * H,), jnp.float32), 'out_w': s * jax.random.normal(ks[5], (H, H), jnp.float32), 'out_b': jnp.zeros((H,), jnp.float32), 'postnorm_w': jnp.ones((H,), jnp.float32), 'mlp_w1': s * jax.random.normal(ks[6], (H, 4 * H), jnp.float32), 'mlp_b1': jnp.zeros((4 * H,), jnp.float32), 'mlp_w2': s * jax.random.normal(ks[7], (4 * H, H), jnp.float32), 'mlp_b2': jnp.zeros((H,), jnp.float32)}
    _L3_xattn_all = _L3_xattn_setup()
    _L3_xattn_in = {k: v for k, v in _L3_xattn_all.items() if k in ('q_w', 'q_b', 'kv_w', 'kv_b', 'out_w', 'out_b', 'postnorm_w', 'mlp_w1', 'mlp_b1', 'mlp_w2', 'mlp_b2')}
    del _L3_xattn_all
    return {'x': x, 'ctx_2048': ctx_2048, 'mask_1x1xSxS2_fc1': mask_1x1xSxS2_fc1, 'mask_Bx1xSxS2_ff1': mask_Bx1xSxS2_ff1, 'mask_Bx1xSxS2_ff0': mask_Bx1xSxS2_ff0, 'mask_BxS2_ik0': mask_BxS2_ik0, 'L0_xattn_ln1_s': _L0_xattn_in['ln1_s'], 'L0_xattn_ln1_b': _L0_xattn_in['ln1_b'], 'L0_xattn_w_qkv': _L0_xattn_in['w_qkv'], 'L0_xattn_b_qkv': _L0_xattn_in['b_qkv'], 'L0_xattn_w_ao': _L0_xattn_in['w_ao'], 'L0_xattn_b_ao': _L0_xattn_in['b_ao'], 'L0_xattn_ln2_s': _L0_xattn_in['ln2_s'], 'L0_xattn_ln2_b': _L0_xattn_in['ln2_b'], 'L0_xattn_w_q': _L0_xattn_in['w_q'], 'L0_xattn_b_q': _L0_xattn_in['b_q'], 'L0_xattn_w_kv': _L0_xattn_in['w_kv'], 'L0_xattn_b_kv': _L0_xattn_in['b_kv'], 'L0_xattn_w_co': _L0_xattn_in['w_co'], 'L0_xattn_b_co': _L0_xattn_in['b_co'], 'L0_xattn_ln3_s': _L0_xattn_in['ln3_s'], 'L0_xattn_ln3_b': _L0_xattn_in['ln3_b'], 'L0_xattn_w1': _L0_xattn_in['w1'], 'L0_xattn_b1': _L0_xattn_in['b1'], 'L0_xattn_w2': _L0_xattn_in['w2'], 'L0_xattn_b2': _L0_xattn_in['b2'], 'L1_xattn_Wq': _L1_xattn_in['Wq'], 'L1_xattn_bq': _L1_xattn_in['bq'], 'L1_xattn_Wk': _L1_xattn_in['Wk'], 'L1_xattn_bk': _L1_xattn_in['bk'], 'L1_xattn_Wv': _L1_xattn_in['Wv'], 'L1_xattn_bv': _L1_xattn_in['bv'], 'L1_xattn_Wo': _L1_xattn_in['Wo'], 'L1_xattn_bo': _L1_xattn_in['bo'], 'L1_xattn_gamma': _L1_xattn_in['gamma'], 'L1_xattn_beta': _L1_xattn_in['beta'], 'L2_xattn_ln1_w': _L2_xattn_in['ln1_w'], 'L2_xattn_ln1_b': _L2_xattn_in['ln1_b'], 'L2_xattn_ln2_w': _L2_xattn_in['ln2_w'], 'L2_xattn_ln2_b': _L2_xattn_in['ln2_b'], 'L2_xattn_maa_x': _L2_xattn_in['maa_x'], 'L2_xattn_maa_w1': _L2_xattn_in['maa_w1'], 'L2_xattn_maa_w2': _L2_xattn_in['maa_w2'], 'L2_xattn_maa_stack': _L2_xattn_in['maa_stack'], 'L2_xattn_time_decay': _L2_xattn_in['time_decay'], 'L2_xattn_td_w1': _L2_xattn_in['td_w1'], 'L2_xattn_td_w2': _L2_xattn_in['td_w2'], 'L2_xattn_u': _L2_xattn_in['u'], 'L2_xattn_Wr': _L2_xattn_in['Wr'], 'L2_xattn_Wk': _L2_xattn_in['Wk'], 'L2_xattn_Wv': _L2_xattn_in['Wv'], 'L2_xattn_Wg': _L2_xattn_in['Wg'], 'L2_xattn_Wo': _L2_xattn_in['Wo'], 'L2_xattn_gn_w': _L2_xattn_in['gn_w'], 'L2_xattn_gn_b': _L2_xattn_in['gn_b'], 'L2_xattn_ffn_maa_k': _L2_xattn_in['ffn_maa_k'], 'L2_xattn_ffn_maa_r': _L2_xattn_in['ffn_maa_r'], 'L2_xattn_Wfk': _L2_xattn_in['Wfk'], 'L2_xattn_Wfr': _L2_xattn_in['Wfr'], 'L2_xattn_Wfv': _L2_xattn_in['Wfv'], 'L3_xattn_q_w': _L3_xattn_in['q_w'], 'L3_xattn_q_b': _L3_xattn_in['q_b'], 'L3_xattn_kv_w': _L3_xattn_in['kv_w'], 'L3_xattn_kv_b': _L3_xattn_in['kv_b'], 'L3_xattn_out_w': _L3_xattn_in['out_w'], 'L3_xattn_out_b': _L3_xattn_in['out_b'], 'L3_xattn_postnorm_w': _L3_xattn_in['postnorm_w'], 'L3_xattn_mlp_w1': _L3_xattn_in['mlp_w1'], 'L3_xattn_mlp_b1': _L3_xattn_in['mlp_b1'], 'L3_xattn_mlp_w2': _L3_xattn_in['mlp_w2'], 'L3_xattn_mlp_b2': _L3_xattn_in['mlp_b2']}

def reference(x, ctx_2048, mask_1x1xSxS2_fc1, mask_Bx1xSxS2_ff1, mask_Bx1xSxS2_ff0, mask_BxS2_ik0, L0_xattn_ln1_s, L0_xattn_ln1_b, L0_xattn_w_qkv, L0_xattn_b_qkv, L0_xattn_w_ao, L0_xattn_b_ao, L0_xattn_ln2_s, L0_xattn_ln2_b, L0_xattn_w_q, L0_xattn_b_q, L0_xattn_w_kv, L0_xattn_b_kv, L0_xattn_w_co, L0_xattn_b_co, L0_xattn_ln3_s, L0_xattn_ln3_b, L0_xattn_w1, L0_xattn_b1, L0_xattn_w2, L0_xattn_b2, L1_xattn_Wq, L1_xattn_bq, L1_xattn_Wk, L1_xattn_bk, L1_xattn_Wv, L1_xattn_bv, L1_xattn_Wo, L1_xattn_bo, L1_xattn_gamma, L1_xattn_beta, L2_xattn_ln1_w, L2_xattn_ln1_b, L2_xattn_ln2_w, L2_xattn_ln2_b, L2_xattn_maa_x, L2_xattn_maa_w1, L2_xattn_maa_w2, L2_xattn_maa_stack, L2_xattn_time_decay, L2_xattn_td_w1, L2_xattn_td_w2, L2_xattn_u, L2_xattn_Wr, L2_xattn_Wk, L2_xattn_Wv, L2_xattn_Wg, L2_xattn_Wo, L2_xattn_gn_w, L2_xattn_gn_b, L2_xattn_ffn_maa_k, L2_xattn_ffn_maa_r, L2_xattn_Wfk, L2_xattn_Wfr, L2_xattn_Wfv, L3_xattn_q_w, L3_xattn_q_b, L3_xattn_kv_w, L3_xattn_kv_b, L3_xattn_out_w, L3_xattn_out_b, L3_xattn_postnorm_w, L3_xattn_mlp_w1, L3_xattn_mlp_b1, L3_xattn_mlp_w2, L3_xattn_mlp_b2):
    import jax
    import jax.numpy as jnp

    def _L0_xattn_ref(hidden_states, encoder_states, ltor_mask, cross_mask, ln1_s, ln1_b, w_qkv, b_qkv, w_ao, b_ao, ln2_s, ln2_b, w_q, b_q, w_kv, b_kv, w_co, b_co, ln3_s, ln3_b, w1, b1, w2, b2):
        import jax, jax.numpy as jnp
        import numpy as np
        H = 512
        NH = 16
        HD = H // NH
        EPS = 1e-05

        def gelu(x):
            return 0.5 * x * (1.0 + jnp.tanh(0.7978845608028654 * x * (1.0 + 0.044715 * x * x)))

        def layernorm(x, scale, bias):
            m = jnp.mean(x, axis=-1, keepdims=True)
            v = jnp.mean(jnp.square(x - m), axis=-1, keepdims=True)
            return (x - m) * jax.lax.rsqrt(v + EPS) * scale + bias

        def split_heads(x):
            b, s, _ = x.shape
            return x.reshape(b, s, NH, HD).transpose(0, 2, 1, 3)

        def merge_heads(x):
            b, nh, s, hd = x.shape
            return x.transpose(0, 2, 1, 3).reshape(b, s, nh * hd)

        def attention(q, k, v, mask):
            scores = jnp.einsum('bhqd,bhkd->bhqk', q, k) / jnp.sqrt(jnp.float32(HD))
            scores = scores * mask - 10000.0 * (1.0 - mask)
            probs = jax.nn.softmax(scores, axis=-1)
            return jnp.einsum('bhqk,bhkd->bhqd', probs, v)
        ln_out = layernorm(hidden_states, ln1_s, ln1_b)
        qkv = ln_out @ w_qkv + b_qkv
        q, k, v = jnp.split(qkv, 3, axis=-1)
        ctx = merge_heads(attention(split_heads(q), split_heads(k), split_heads(v), ltor_mask))
        attn_out = ctx @ w_ao + b_ao
        x = hidden_states + attn_out
        ln_out = layernorm(x, ln2_s, ln2_b)
        q = ln_out @ w_q + b_q
        kv = encoder_states @ w_kv + b_kv
        k, v = jnp.split(kv, 2, axis=-1)
        ctx = merge_heads(attention(split_heads(q), split_heads(k), split_heads(v), cross_mask))
        cross_out = ctx @ w_co + b_co
        x = x + cross_out
        ln_out = layernorm(x, ln3_s, ln3_b)
        mlp_out = gelu(ln_out @ w1 + b1) @ w2 + b2
        return x + mlp_out

    def _L1_xattn_ref(hidden_state, encoder_hidden_state, encoder_attention_mask, Wq, bq, Wk, bk, Wv, bv, Wo, bo, gamma, beta):
        import jax, jax.numpy as jnp
        import numpy as np
        H = 512
        NH = 32
        KVH = 8
        HD = H // NH
        GROUPS = NH // KVH
        EPS = 1e-06
        B, L, S = (4, 256, 256)

        def _gqa_forward(hidden_state, encoder_hidden_state, encoder_attention_mask, Wq, bq, Wk, bk, Wv, bv, Wo, bo, gamma, beta):
            b, l, _ = hidden_state.shape
            s = encoder_hidden_state.shape[1]
            q = hidden_state @ Wq + bq
            k = encoder_hidden_state @ Wk + bk
            v = encoder_hidden_state @ Wv + bv
            q = q.reshape(b, l, KVH, GROUPS, HD).transpose(0, 2, 3, 1, 4)
            k = k.reshape(b, s, KVH, HD).transpose(0, 2, 1, 3)
            v = v.reshape(b, s, KVH, HD).transpose(0, 2, 1, 3)
            scale = 1.0 / jnp.sqrt(jnp.asarray(HD, q.dtype))
            scores = jnp.einsum('bkgld,bksd->bkgls', q, k) * scale
            scores = scores + encoder_attention_mask[:, :, None, :, :]
            attn = jax.nn.softmax(scores, axis=-1)
            out = jnp.einsum('bkgls,bksd->bkgld', attn, v)
            out = out.transpose(0, 3, 1, 2, 4).reshape(b, l, H)
            out = out @ Wo + bo
            x = out + hidden_state
            mu = jnp.mean(x, axis=-1, keepdims=True)
            var = jnp.var(x, axis=-1, keepdims=True)
            return (x - mu) * jax.lax.rsqrt(var + EPS) * gamma + beta
        return _gqa_forward(hidden_state, encoder_hidden_state, encoder_attention_mask, Wq, bq, Wk, bk, Wv, bv, Wo, bo, gamma, beta)

    def _L2_xattn_ref(x, state, ln1_w, ln1_b, ln2_w, ln2_b, maa_x, maa_w1, maa_w2, maa_stack, time_decay, td_w1, td_w2, u, Wr, Wk, Wv, Wg, Wo, gn_w, gn_b, ffn_maa_k, ffn_maa_r, Wfk, Wfr, Wfv):
        import jax, jax.numpy as jnp
        import numpy as np
        E, H, L, B = (512, 32, 256, 4)
        S = E // H
        DM, DD = (32, 64)

        def _ln(x, w, b, eps=1e-05):
            m = x.mean(-1, keepdims=True)
            v = ((x - m) ** 2).mean(-1, keepdims=True)
            return (x - m) / jnp.sqrt(v + eps) * w + b

        def _block(x, state, ln1_w, ln1_b, ln2_w, ln2_b, maa_x, maa_w1, maa_w2, maa_stack, time_decay, td_w1, td_w2, u, Wr, Wk, Wv, Wg, Wo, gn_w, gn_b, ffn_maa_k, ffn_maa_r, Wfk, Wfr, Wfv):
            b, l, e = x.shape
            h = u.shape[0]
            s_ = e // h
            xa = _ln(x, ln1_w, ln1_b)
            sx = jnp.concatenate([state[:, 1:2] - xa[:, :1], xa[:, :-1] - xa[:, 1:]], axis=1)
            xxx = jnp.tanh((xa + sx * maa_x) @ maa_w1).reshape(b, l, 5, DM)
            xxx = jnp.einsum('blfd,fde->blfe', xxx, maa_w2)
            xm = xa[:, :, None] + sx[:, :, None] * (maa_stack + xxx)
            xk, xw, xv, xr, xg = (xm[:, :, j] for j in range(5))
            w = jnp.exp(-jnp.exp(time_decay + jnp.tanh(xw @ td_w1) @ td_w2)).reshape(b, l, h, s_)
            r = (xr @ Wr.T).reshape(b, l, h, s_)
            k = (xk @ Wk.T).reshape(b, l, h, s_)
            v = (xv @ Wv.T).reshape(b, l, h, s_)
            g = jax.nn.silu(xg @ Wg.T)
            s0 = state[:, 2:2 + s_].reshape(b, h, s_, s_)

            def step(s, rkvw):
                r_t, k_t, v_t, w_t = rkvw
                a = k_t[..., :, None] * v_t[..., None, :]
                out = jnp.einsum('bhi,bhij->bhj', r_t, u * a + s)
                s = a + w_t[..., :, None] * s
                return (s, out)
            rkvw = tuple((jnp.moveaxis(t, 1, 0) for t in (r, k, v, w)))
            _, out = jax.lax.scan(step, s0, rkvw)
            out = jnp.moveaxis(out, 0, 1).reshape(b, l, e)
            og = out.reshape(b, l, h, s_)
            m = og.mean(-1, keepdims=True)
            va = ((og - m) ** 2).mean(-1, keepdims=True)
            og = ((og - m) / jnp.sqrt(va + 1e-05)).reshape(b, l, e) * gn_w + gn_b
            x1 = x + og * g @ Wo.T
            xc = _ln(x1, ln2_w, ln2_b)
            sx2 = jnp.concatenate([state[:, 0:1] - xc[:, :1], xc[:, :-1] - xc[:, 1:]], axis=1)
            xk2 = xc + sx2 * ffn_maa_k
            xr2 = xc + sx2 * ffn_maa_r
            rr = jax.nn.sigmoid(xr2 @ Wfr.T)
            kk = jnp.square(jax.nn.relu(xk2 @ Wfk.T))
            return x1 + rr * (kk @ Wfv.T)
        return _block(x, state, ln1_w, ln1_b, ln2_w, ln2_b, maa_x, maa_w1, maa_w2, maa_stack, time_decay, td_w1, td_w2, u, Wr, Wk, Wv, Wg, Wo, gn_w, gn_b, ffn_maa_k, ffn_maa_r, Wfk, Wfr, Wfv)

    def _L3_xattn_ref(x, latents, attention_mask, q_w, q_b, kv_w, kv_b, out_w, out_b, postnorm_w, mlp_w1, mlp_b1, mlp_w2, mlp_b2):
        import jax, jax.numpy as jnp
        import numpy as np
        B, P, K, H, NH = (4, 512, 64, 512, 16)
        DH = H // NH
        EPS = 1e-06

        def rmsnorm(x, w):
            var = jnp.mean(jnp.square(x), axis=-1, keepdims=True)
            return x * jax.lax.rsqrt(var + EPS) * w
        b, p, _ = x.shape
        k_len = latents.shape[1]
        residual = latents
        h = jnp.concatenate([x, latents], axis=1)
        q = (latents @ q_w + q_b).reshape(b, k_len, NH, DH)
        kv = (h @ kv_w + kv_b).reshape(b, p + k_len, NH, DH, 2)
        kmat, v = (kv[..., 0], kv[..., 1])
        attn = jnp.einsum('bkhd,bnhd->bhkn', q, kmat) / DH
        full_mask = jnp.concatenate([attention_mask.astype(bool), jnp.ones((b, k_len), bool)], axis=-1)
        attn = jnp.where(full_mask[:, None, None, :], attn, -jnp.inf)
        attn = jax.nn.softmax(attn.astype(jnp.float32), axis=-1).astype(q.dtype)
        attn_out = jnp.einsum('bhkn,bnhd->bkhd', attn, v).reshape(b, k_len, H)
        attn_out = attn_out @ out_w + out_b + residual
        out = rmsnorm(attn_out, postnorm_w)
        out = jax.nn.gelu(out @ mlp_w1 + mlp_b1) @ mlp_w2 + mlp_b2
        return out + residual
    x = _L0_xattn_ref(x, ctx_2048, mask_1x1xSxS2_fc1, mask_Bx1xSxS2_ff1, L0_xattn_ln1_s, L0_xattn_ln1_b, L0_xattn_w_qkv, L0_xattn_b_qkv, L0_xattn_w_ao, L0_xattn_b_ao, L0_xattn_ln2_s, L0_xattn_ln2_b, L0_xattn_w_q, L0_xattn_b_q, L0_xattn_w_kv, L0_xattn_b_kv, L0_xattn_w_co, L0_xattn_b_co, L0_xattn_ln3_s, L0_xattn_ln3_b, L0_xattn_w1, L0_xattn_b1, L0_xattn_w2, L0_xattn_b2)
    x = _L1_xattn_ref(x, ctx_2048, mask_Bx1xSxS2_ff0, L1_xattn_Wq, L1_xattn_bq, L1_xattn_Wk, L1_xattn_bk, L1_xattn_Wv, L1_xattn_bv, L1_xattn_Wo, L1_xattn_bo, L1_xattn_gamma, L1_xattn_beta)
    x = _L2_xattn_ref(x, ctx_2048, L2_xattn_ln1_w, L2_xattn_ln1_b, L2_xattn_ln2_w, L2_xattn_ln2_b, L2_xattn_maa_x, L2_xattn_maa_w1, L2_xattn_maa_w2, L2_xattn_maa_stack, L2_xattn_time_decay, L2_xattn_td_w1, L2_xattn_td_w2, L2_xattn_u, L2_xattn_Wr, L2_xattn_Wk, L2_xattn_Wv, L2_xattn_Wg, L2_xattn_Wo, L2_xattn_gn_w, L2_xattn_gn_b, L2_xattn_ffn_maa_k, L2_xattn_ffn_maa_r, L2_xattn_Wfk, L2_xattn_Wfr, L2_xattn_Wfv)
    x = _L3_xattn_ref(ctx_2048, x, mask_BxS2_ik0, L3_xattn_q_w, L3_xattn_q_b, L3_xattn_kv_w, L3_xattn_kv_b, L3_xattn_out_w, L3_xattn_out_b, L3_xattn_postnorm_w, L3_xattn_mlp_w1, L3_xattn_mlp_b1, L3_xattn_mlp_w2, L3_xattn_mlp_b2)
    return x

_drawn_inputs = setup_inputs


def setup_inputs(seed=0):
    import zlib

    import numpy as np

    out = dict(_drawn_inputs(seed))
    spreads = {'L0_xattn_ln1_s': (1.0, 0.6),
     'L0_xattn_ln1_b': (0.0, 0.379),
     'L0_xattn_b_qkv': (0.0, 0.1),
     'L0_xattn_b_ao': (0.0, 0.1),
     'L0_xattn_ln2_s': (1.0, 0.6),
     'L0_xattn_ln2_b': (0.0, 0.8),
     'L0_xattn_b_q': (0.0, 2.0),
     'L0_xattn_b_kv': (0.0, 0.1),
     'L0_xattn_b_co': (0.0, 0.1),
     'L0_xattn_ln3_s': (1.0, 0.2),
     'L0_xattn_ln3_b': (0.0, 0.316),
     'L0_xattn_b1': (0.0, 0.1),
     'L0_xattn_b2': (0.0, 0.1),
     'L1_xattn_bq': (0.0, 0.8),
     'L1_xattn_bk': (0.0, 2.0),
     'L1_xattn_bv': (0.0, 0.1),
     'L1_xattn_bo': (0.0, 0.1),
     'L1_xattn_gamma': (1.0, 0.2),
     'L1_xattn_beta': (0.0, 0.1),
     'L2_xattn_ln1_w': (1.0, 0.2),
     'L2_xattn_ln1_b': (0.0, 0.288),
     'L2_xattn_ln2_w': (1.0, 0.6),
     'L2_xattn_ln2_b': (0.0, 0.8),
     'L2_xattn_gn_w': (1.0, 0.6),
     'L2_xattn_gn_b': (0.0, 0.692),
     'L3_xattn_q_b': (0.0, 2.0),
     'L3_xattn_kv_b': (0.0, 0.8),
     'L3_xattn_out_b': (0.0, 0.367),
     'L3_xattn_postnorm_w': (1.0, 0.2),
     'L3_xattn_mlp_b1': (0.0, 0.1),
     'L3_xattn_mlp_b2': (0.0, 0.1)}
    factors = {'L0_xattn_w_q': 6.833,
     'L1_xattn_Wq': 7.071,
     'L1_xattn_Wk': 6.876,
     'L2_xattn_maa_x': 8.0,
     'L2_xattn_maa_w1': 3.095,
     'L2_xattn_maa_w2': 3.089,
     'L2_xattn_td_w1': 8.0,
     'L2_xattn_td_w2': 8.0,
     'L2_xattn_u': 3.08,
     'L2_xattn_ffn_maa_k': 5.815,
     'L2_xattn_ffn_maa_r': 8.0,
     'L2_xattn_Wfr': 4.117,
     'L3_xattn_q_w': 8.0,
     'L3_xattn_kv_w': 4.423,
     'L3_xattn_out_w': 3.41}
    for name, (base, spread) in spreads.items():
        noise = np.random.default_rng([zlib.crc32(name.encode()), seed]).standard_normal(out[name].shape)
        drawn = base * np.exp(spread * noise) if base else spread * noise
        out[name] = jnp.asarray(drawn.astype(out[name].dtype))
    for name, factor in factors.items():
        out[name] = (out[name] * factor).astype(out[name].dtype)
    return out
```

```python
from contextlib import ExitStack

import numpy as np
import concourse.bass as bass
from concourse import mybir

F32 = mybir.dt.float32
I32 = mybir.dt.int32
ALU = mybir.AluOpType
ACT = mybir.ActivationFunctionType
AX = mybir.AxisListType

B = 16
T = 128
D = 512
C = D // 128
SL = 2
NIT = B // SL
TT = SL * T
BANK = 512
HID = 4 * D
HC = HID // 128
DM = 32
NMIX = 5
DD = 64
HS = 16
NHR = D // HS
HPT = 128 // HS

VECTORS = [("ln1_s", 4), ("ln1_b", 4), ("b_q0", 4), ("b_k0", 4), ("b_v0", 4),
           ("ln2_s", 4), ("ln2_b", 4), ("b_q1", 4), ("b_k1", 4), ("b_v1", 4),
           ("ln3_s", 4), ("ln3_b", 4), ("b1", 16),
           ("g_bq", 4), ("g_bk", 1), ("g_bv", 4),
           ("r_ln1_w", 4), ("r_ln1_b", 4), ("r_ln2_w", 4), ("r_ln2_b", 4), ("maa_x", 4),
           ("maa_stack", 20), ("time_decay", 4), ("u", 4), ("ffn_k", 4), ("ffn_r", 4),
           ("p_bq", 4), ("p_bk", 4), ("p_bv", 4), ("p_norm", 4), ("p_b1", 16)]
ROWS = ["b_ao", "b_co", "b2", "g_bo", "g_gamma", "g_beta", "gn_w", "gn_b", "p_bo", "p_b2"]


class Ring:

    def __init__(self, name, sem, banks, items):
        assert len(items) % len(banks) == 0
        self.banks, self.items = banks, {item: n for n, item in enumerate(items)}
        self.per_bank = len(items) // len(banks)
        self.full = [sem(f"{name}_full{b}") for b in range(len(banks))]
        self.free = [sem(f"{name}_free{b}") for b in range(len(banks))]

    def index(self, item):
        return self.items[item] % len(self.banks)

    def bank(self, item):
        return self.banks[self.index(item)]

    def full_sem(self, item):
        return self.full[self.index(item)]

    def free_sem(self, item):
        return self.free[self.index(item)]

    def latest(self, items):
        return list({self.index(item): item for item in sorted(items, key=self.items.get)}.values())

    def uses_before(self, it, item):
        return it * self.per_bank + self.items[item] // len(self.banks)

    def uses_of_iterations(self, it):
        return it * self.per_bank

    def uses_with(self, it, item):
        return it * self.per_bank + self.items[item] // len(self.banks) + 1


    def wait_free(self, engine, it, start=None, read=()):
        need = {}
        for item in read:
            need[self.index(item)] = max(need.get(self.index(item), 0), self.items[item] // len(self.banks) + 1)
        if start is not None:
            need[self.index(start)] = max(need.get(self.index(start), 0), self.items[start] // len(self.banks))
        for bank, uses in need.items():
            engine.wait_ge(self.free[bank], it * self.per_bank + uses)


class Semaphores:

    def __init__(self, nc, prefix, stack):
        self.nc, self.prefix, self.stack, self.held = nc, prefix, stack, []

    def __call__(self, name):
        held = self.stack.enter_context(self.nc.semaphore(f"{self.prefix}_{name}"))
        self.held.append(held)
        return held

    def clear(self):
        with self.nc.Block() as block:
            @block.gpsimd
            def _(pool):
                numbers = sorted(held.num for held in self.held)
                start = numbers[0]
                for n, after in zip(numbers, numbers[1:] + [None]):
                    if after != n + 1:
                        pool.sem_clear(range(start, n + 1))
                        start = after


def bcast(ap, shape, axis):
    return ap.unsqueeze(axis).to_broadcast(shape)


def sequences(engine, it):
    return [it * SL + k if isinstance(it, int) else engine.snap(it * SL + k) for k in range(SL)]


def row_stats(nc, dve, rows, stats, touched, sems, it, eps, mean_square=False):
    stat_done, aggr_done, var_done = sems
    for k in range(SL):
        nc.vector.bn_stats(stats[:, k, 0:6], rows[k]).then_inc(stat_done, 1)
    dve.wait_ge(stat_done, it * 2 + 2)
    nc.vector.tensor_copy(touched[:, 0:1], stats[:, 0, 0:1])
    for k in range(SL):
        nc.vector.bn_aggr(stats[:, k, 6:8], stats[:, k, 0:6]).then_inc(aggr_done, 1)
    dve.wait_ge(aggr_done, it * 2 + 2)
    if mean_square:
        nc.vector.tensor_tensor(stats[:, :, 8:9], stats[:, :, 6:7], stats[:, :, 6:7], ALU.mult).then_inc(var_done, 1)
        dve.wait_ge(var_done, it * 2 + 1)
        nc.vector.scalar_tensor_tensor(stats[:, :, 9:10], stats[:, :, 8:9], eps, stats[:, :, 7:8],
                                       ALU.add, ALU.add).then_inc(var_done, 1)
    else:
        nc.vector.tensor_scalar(stats[:, :, 9:10], stats[:, :, 7:8], eps, None, ALU.add).then_inc(var_done, 2)


def rstd_on_pool(nc, pool, stats, rstd, minus_half, var_done, rstd_done, it):
    pool.wait_ge(var_done, it * 2 + 2)
    nc.gpsimd.tensor_tensor(rstd[:, :, 0:1], stats[:, :, 9:10], minus_half[:, 0:SL].unsqueeze(2), ALU.pow)\
        .then_inc(rstd_done, 1)


def attention_phase(nc, cfg, const, x_in, x_out, ctx_t, mask, weights, own_weights, next_weights):
    kind = cfg["kind"]
    normed = kind in ("self", "cross")
    grouped, latent = kind == "group", kind == "latent"
    NK = 2 * T if latent else T
    KB = NK // 128
    NH = 32 if grouped else 16
    HD = D // NH
    U = 2 * SL if grouped or latent else SL
    UPS = U // SL
    HU = NH // UPS
    scale = cfg["scale"]
    Wq, Wk, Wv, Wo = weights
    ident, minus_half = const["ident"], const["minus_half"]
    vec, row = const["vec"], const["row"]

    def blocks(u):
        out = []
        for r in range(4):
            for i in range(4):
                if grouped:
                    out.append(((4 * (r % 2) + i) * 4 + 2 * (u % 2) + r // 2, 0))
                elif latent:
                    out.append((4 * (2 * (u % 2) + i // 2) + r, i % 2))
                else:
                    out.append((4 * i + r, 0))
        return out

    with ExitStack() as stack:
        def sb(name, shape, dt=F32):
            return stack.enter_context(nc.sbuf_tensor(f"{kind}_{name}", shape, dt))

        def ps(name, shape):
            return stack.enter_context(nc.psum_tensor(f"{kind}_{name}", shape, F32))

        sem = Semaphores(nc, kind, stack)

        x = sb("x", [128, SL, D])
        xres = sb("xres", [128, SL, D])
        xn = sb("xn", [128, SL, D]) if normed else None
        stats = sb("stats", [128, SL, 10])
        rstd = sb("rstd", [128, SL, 1])
        touched = sb("touched", [128, 1])
        src_t = sb("src_t", [128, C, SL, NK])
        ctx_sb = sb("ctx_t", [128, C, SL, T]) if kind in ("cross", "group") else None
        q_t = sb("q_t", [128, C, TT])
        k_t = sb("k_t", [128, 1 if grouped else C, SL * NK])
        k_diag = sb("k_diag", [128, SL, 8, T]) if grouped else None
        vw = 128 if grouped else D
        v = sb("v", [128, SL, KB, vw])
        msk = sb("mask", [128, SL, NK]) if not latent else None
        bias = sb("bias", [128, SL, NK]) if not grouped else None
        key_mask = sb("key_mask", [128, SL, T], I32) if latent else None
        S = sb("scores", [128, 2, 16, 128])
        negmax = sb("negmax", [128, 2, HU])
        rowsum = sb("rowsum", [128, SL, NH])
        rinv = sb("rinv", [128, SL, NH])
        PT = sb("probs_t", [128, 4, 4, 128])
        o = sb("o", [128, SL, D])
        o_t = sb("o_t", [128, SL, C, T])

        sc = ps("sc", [128, 4, BANK])
        pj_banks = [ps(f"pj{i}", [128, BANK]) for i in range(2)]
        pt_banks = [ps(f"pt{i}", [128, BANK]) for i in range(2)]
        k_items = 1 if grouped else 4 if latent else 2
        v_items = 1 if grouped else 4 if latent else 2
        order = [("x", 0), ("x", 1), ("q", 0), ("q", 1)] + [("k", n) for n in range(k_items)]
        order += [("v", n) for n in range(v_items)]
        order += [(w, k) for w in ("pv", "ot", "out") for k in range(SL)]
        pj = Ring("pj", sem, pj_banks, order)
        pt = Ring("pt", sem, pt_banks, [(u, r) for u in range(U) for r in range(4)])

        x_loaded = [sem(f"x_loaded{k}") for k in range(SL)]
        ctx_loaded = [sem(f"ctx_loaded{k}") for k in range(SL)]
        mask_loaded = [sem(f"mask_loaded{k}") for k in range(SL)]
        stored = sem("stored")
        norm_sems = (sem("stat_done"), sem("aggr_done"), sem("var_done"))
        rstd_done = sem("rstd_done")
        xn_done = sem("xn_done")
        xres_done = sem("xres_done")
        bias_done = sem("bias_done")
        diag_done = sem("diag_done")
        scores_ready = sem("scores_ready")
        scores_read = sem("scores_read")
        bias_added = sem("bias_added")
        max_done = sem("max_done")
        exp_done = sem("exp_done")
        rinv_done = sem("rinv_done")
        y_steps = sem("y_steps")
        y_done = sem("y_done")
        stack.callback(sem.clear)
        block = stack.enter_context(nc.Block())

        @block.sync
        def _(sp):
            def load(it, after=None):
                seq = sequences(sp, it)
                for k in range(SL):
                    if after is not None:
                        if normed:
                            sp.wait_ge(xn_done, after * 2 + 2)
                        elif k == 0:
                            sp.wait_ge(pj.full_sem(("x", 0)), pj.uses_with(after, ("x", 0)))
                            sp.wait_ge(pj.full_sem(("x", 1)), pj.uses_with(after, ("x", 1)))
                        sp.wait_ge(xres_done, after * 2 + 2)
                    sp.dma_start(x[:, k, :], x_in[seq[k]]).then_inc(x_loaded[k], 16)
                for k in range(SL):
                    if kind == "cross" or grouped or latent:
                        if after is not None:
                            for item in pj.latest([("k", i) for i in range(k_items)]
                                                  + [("v", i) for i in range(v_items)]):
                                sp.wait_ge(pj.full_sem(item), pj.uses_with(after, item))
                        dst = src_t[:, :, k, 0:T] if latent else ctx_sb[:, :, k, :]
                        sp.dma_start(dst, ctx_t[seq[k]]).then_inc(ctx_loaded[k], 16)
                    if after is not None:
                        if not grouped:
                            sp.wait_ge(bias_done, after * 2 + 2)
                        if not latent:
                            sp.wait_ge(scores_read, after * U + U)
                    if latent:
                        sp.dma_start(key_mask[:, k, :], mask[seq[k]].to_broadcast([128, T]))\
                            .then_inc(mask_loaded[k], 16)
                    elif kind == "self":
                        sp.dma_start(msk[:, k, :], mask[0]).then_inc(mask_loaded[k], 16)
                    else:
                        sp.dma_start(msk[:, k, :], mask[seq[k]]).then_inc(mask_loaded[k], 16)

            def store(it):
                seq = sequences(sp, it)
                for k in range(SL):
                    if grouped:
                        sp.wait_ge(y_done, it * SL + k + 1)
                    else:
                        sp.wait_ge(pj.free_sem(("out", k)), pj.uses_with(it, ("out", k)))
                    sp.dma_start(x_out[seq[k]], o[:, k, :]).then_inc(stored, 16)

            load(0)
            with sp.Fori(0, NIT - 1) as it:
                load(it + 1, after=it)
                store(it)
            store(NIT - 1)
            sp.wait_ge(stored, 16 * B)

        @block.gpsimd
        def _(pool):
            with pool.Fori(0, NIT) as it:
                for k in range(SL):
                    pool.wait_ge(x_loaded[k], it * 16 + 16)
                    if grouped:
                        pool.wait_ge(y_done, it * 2)
                    else:
                        pool.wait_ge(pj.free_sem(("out", k)), pj.uses_of_iterations(it))
                    nc.gpsimd.tensor_tensor(xres[:, k, :], x[:, k, :], row(cfg["bo"]), ALU.add)\
                        .then_inc(xres_done, 1)
                if normed:
                    rstd_on_pool(nc, pool, stats, rstd, minus_half, norm_sems[2], rstd_done, it)
                    for u in range(U):
                        pool.wait_ge(bias_done, it * 2 + u + 1)
                        pool.wait_ge(scores_read, it * U + u + 1)
                        nc.gpsimd.tensor_tensor(S[:, u, :, :], S[:, u, :, :], bcast(bias[:, u, :], [128, 16, T], 1),
                                                ALU.add).then_inc(bias_added, 1)
                if grouped:
                    rstd_on_pool(nc, pool, stats, rstd, minus_half, norm_sems[2], rstd_done, it)

        @block.scalar
        def _(act):
            if next_weights:
                next_weights.start(act)
            with act.Fori(0, NIT) as it:
                for k in range(SL):
                    act.wait_ge(pj.full_sem(("x", k)), pj.uses_with(it, ("x", k)))
                    bank = pj.bank(("x", k))
                    if normed:
                        for c in range(C):
                            last = nc.scalar.activation(src_t[:, c, k, :], bank[:, c * 128:c * 128 + 128],
                                                        ACT.Identity, scale=vec(cfg["ln_s"], c),
                                                        bias=vec(cfg["ln_b"], c))
                    else:
                        last = nc.scalar.copy(src_t[:, :, k, NK - T:NK], bank[:, :].rearrange("p (c t) -> p c t", c=C))
                    last.then_inc(pj.free_sem(("x", k)), 1)
                for w, n_items, bias_name in (("q", 2, cfg["bq"]), ("k", k_items, cfg["bk"])):
                    for n in range(n_items):
                        act.wait_ge(pj.full_sem((w, n)), pj.uses_with(it, (w, n)))
                        bank = pj.bank((w, n))
                        per = 1 if w == "k" and k_items != 2 else 2
                        width = (TT if w == "q" else SL * NK)
                        dst = q_t if w == "q" else k_t
                        for i in range(per):
                            last = nc.scalar.activation(dst[:, n * per + i, :], bank[:, i * width:(i + 1) * width],
                                                        ACT.Identity, bias=vec(bias_name, n * per + i))
                        last.then_inc(pj.free_sem((w, n)), 1)
                for step in range(U + 1):
                    if step < U:
                        u = step
                        act.wait_ge(max_done, it * U + u + 1)
                        if u % UPS == 0:
                            act.wait_ge(rinv_done, it * 2)
                        w = NK // 128
                        heads = [h for h, kb in blocks(u) if kb == 0]
                        for j, h in enumerate(heads):
                            nc.scalar.activation(S[:, u % 2, j * w:(j + 1) * w, :], S[:, u % 2, j * w:(j + 1) * w, :],
                                                 ACT.Exp, bias=negmax[:, u % 2, j:j + 1],
                                                 accum_out=rowsum[:, u // UPS, h:h + 1]).then_inc(exp_done, 1)
                    if step > 0:
                        u = step - 1
                        for r in (1, 3):
                            act.wait_ge(pt.full_sem((u, r)), pt.uses_with(it, (u, r)))
                            nc.scalar.copy(PT[:, r, :, :], pt.bank((u, r))[:, :].rearrange("p (i t) -> p i t", i=4))\
                                .then_inc(pt.free_sem((u, r)), 1)
                for k in range(SL):
                    act.wait_ge(pj.full_sem(("ot", k)), pj.uses_with(it, ("ot", k)))
                    for c in range(C):
                        last = nc.scalar.activation(o_t[:, k, c, :], pj.bank(("ot", k))[:, c * 128:c * 128 + 128],
                                                    ACT.Identity, bias=vec(cfg["bv"], c))
                    last.then_inc(pj.free_sem(("ot", k)), 1)

        @block.vector
        def _(dve):
            if latent:
                nc.vector.memset(bias[:, :, T:NK], 0.0).then_inc(y_steps, 1)
                dve.wait_ge(y_steps, 1)
            with dve.Fori(0, NIT) as it:
                if normed:
                    for k in range(SL):
                        dve.wait_ge(x_loaded[k], it * 16 + 16)
                    row_stats(nc, dve, [x[:, k, :] for k in range(SL)], stats, touched, norm_sems, it, cfg["eps"])
                    dve.wait_ge(rstd_done, it + 1)
                    dve.wait_ge(scores_ready, it * U)
                    for k in range(SL):
                        nc.vector.tensor_scalar(xn[:, k, :], x[:, k, :], stats[:, k, 6:7], rstd[:, k, :],
                                                ALU.subtract, ALU.mult).then_inc(xn_done, 1)
                if grouped:
                    for k in range(SL):
                        dve.wait_ge(pj.free_sem(("k", 0)), pj.uses_with(it, ("k", 0)))
                        dve.wait_ge(scores_ready, it * U)
                        nc.vector.tensor_tensor(k_diag[:, k, :, :], bcast(k_t[:, 0, k * T:k * T + T], [128, 8, T], 1),
                                                bcast(const["head_mask"], [128, 8, T], 2), ALU.mult)\
                            .then_inc(diag_done, 1)
                else:
                    for k in range(SL):
                        dve.wait_ge(mask_loaded[k], it * 16 + 16)
                        if latent:
                            dve.wait_ge(scores_read, it * U)
                            nc.vector.tensor_scalar(bias[:, k, 0:T], key_mask[:, k, :], 0.0, -3.0e38,
                                                    ALU.is_equal, ALU.mult).then_inc(bias_done, 1)
                        else:
                            dve.wait_ge(bias_added, it * U)
                            nc.vector.tensor_scalar(bias[:, k, :], msk[:, k, :], 1.0, 10000.0,
                                                    ALU.subtract, ALU.mult).then_inc(bias_done, 1)

                def values(n):
                    dve.wait_ge(pj.full_sem(("v", n)), pj.uses_with(it, ("v", n)))
                    bank = pj.bank(("v", n))
                    if grouped:
                        dst, src = v[:, :, 0, :], bank[:, 0:SL * 128].rearrange("p (k n) -> p k n", k=SL)
                    else:
                        dst, src = v[:, n // KB, n % KB, :], bank[:, :]
                    nc.vector.tensor_copy(dst, src).then_inc(pj.free_sem(("v", n)), 1)

                def scale_and_mask(u):
                    k = u // UPS
                    dve.wait_ge(scores_ready, it * U + u + 1)
                    out, src = S[:, u % 2, :, :], sc[:, :, :].rearrange("p r (i t) -> p (r i) t", i=4)
                    if latent:
                        dve.wait_ge(bias_done, it * 2 + k + 1)
                        out = out.rearrange("p (a kb) t -> p a (kb t)", kb=2)
                        src = sc[:, :, :].rearrange("p r (i t) -> p (r i) t", i=2)
                        nc.vector.scalar_tensor_tensor(out, src, scale, bcast(bias[:, k, :], [128, 8, NK], 1),
                                                       ALU.mult, ALU.add).then_inc(scores_read, 1)
                    else:
                        dve.wait_ge(mask_loaded[k], it * 16 + 16)
                        nc.vector.scalar_tensor_tensor(out, src, scale, bcast(msk[:, k, :], [128, 16, T], 1),
                                                       ALU.mult, ALU.add if grouped else ALU.mult)\
                            .then_inc(scores_read, 1)

                def row_max(u):
                    if normed:
                        dve.wait_ge(bias_added, it * U + u + 1)
                    else:
                        dve.wait_ge(scores_read, it * U + u + 1)
                    nc.vector.tensor_reduce(out=negmax[:, u % 2, :],
                                            in_=S[:, u % 2, :, :].rearrange("p (h b) t -> p h (b t)", b=KB),
                                            op=ALU.max, axis=AX.X, negate=True).then_inc(max_done, 1)

                def copy_probs(u):
                    for r in (0, 2):
                        dve.wait_ge(pt.full_sem((u, r)), pt.uses_with(it, (u, r)))
                        nc.vector.tensor_copy(PT[:, r, :, :], pt.bank((u, r))[:, :].rearrange("p (i t) -> p i t", i=4))\
                            .then_inc(pt.free_sem((u, r)), 1)

                def normalise(k):
                    dve.wait_ge(exp_done, it * U * HU + (k + 1) * UPS * HU)
                    nc.vector.reciprocal(rinv[:, k, :], rowsum[:, k, :]).then_inc(rinv_done, 1)
                    dve.wait_ge(rinv_done, it * 2 + k + 1)
                    dve.wait_ge(pj.full_sem(("pv", k)), pj.uses_with(it, ("pv", k)))
                    dve.wait_ge(stored, it * 32)
                    nc.vector.tensor_tensor(o[:, k, :].rearrange("p (h d) -> p h d", h=NH),
                                            pj.bank(("pv", k))[:, :].rearrange("p (h d) -> p h d", h=NH),
                                            bcast(rinv[:, k, :], [128, NH, HD], 2), ALU.mult)\
                        .then_inc(pj.free_sem(("pv", k)), 1)

                for u in range(U):
                    scale_and_mask(u)
                    if u == 0:
                        for n in range(v_items):
                            values(n)
                    row_max(u)
                    if u > 0:
                        copy_probs(u - 1)
                        if u % UPS == 0:
                            normalise(u // UPS - 1)
                copy_probs(U - 1)
                normalise(SL - 1)
                for k in range(SL):
                    dve.wait_ge(pj.full_sem(("out", k)), pj.uses_with(it, ("out", k)))
                    dve.wait_ge(xres_done, it * 2 + k + 1)
                    if grouped:
                        nc.vector.tensor_tensor(xres[:, k, :], pj.bank(("out", k))[:, :], xres[:, k, :], ALU.add)\
                            .then_inc(pj.free_sem(("out", k)), 1)
                    else:
                        nc.vector.tensor_tensor(o[:, k, :], pj.bank(("out", k))[:, :], xres[:, k, :], ALU.add)\
                            .then_inc(pj.free_sem(("out", k)), 1)
                if grouped:
                    for k in range(SL):
                        dve.wait_ge(pj.free_sem(("out", k)), pj.uses_with(it, ("out", k)))
                    row_stats(nc, dve, [xres[:, k, :] for k in range(SL)], stats, touched, norm_sems, it, cfg["eps"])
                    dve.wait_ge(rstd_done, it + 1)
                    for k in range(SL):
                        nc.vector.tensor_scalar(xres[:, k, :], xres[:, k, :], stats[:, k, 6:7], rstd[:, k, :],
                                                ALU.subtract, ALU.mult).then_inc(y_steps, 1)
                        dve.wait_ge(y_steps, it * 4 + 2 * k + 1)
                        nc.vector.tensor_tensor(xres[:, k, :], xres[:, k, :], row("g_gamma"), ALU.mult)\
                            .then_inc(y_steps, 1)
                        dve.wait_ge(y_steps, it * 4 + 2 * k + 2)
                        nc.vector.tensor_tensor(o[:, k, :], xres[:, k, :], row("g_beta"), ALU.add)\
                            .then_inc(y_done, 1)

        @block.tensor
        def _(pe):
            own_weights.wait(pe)
            with pe.Fori(0, NIT) as it:
                def begin(item):
                    pe.wait_ge(pj.free_sem(item), pj.uses_before(it, item))

                def project_features(item, W, f0, n_chunks, moving, width):
                    begin(item)
                    for i in range(n_chunks):
                        for c in range(C):
                            last = nc.tensor.matmul(pj.bank(item)[:, i * width:(i + 1) * width],
                                                    W[:, c, f0 + i * 128:f0 + i * 128 + 128], moving(c),
                                                    start=c == 0, stop=c == C - 1)
                    last.then_inc(pj.full_sem(item), 1)

                for k in range(SL):
                    begin(("x", k))
                    if normed:
                        pe.wait_ge(xn_done, it * 2 + k + 1)
                    else:
                        pe.wait_ge(x_loaded[k], it * 16 + 16)
                    rows = xn if normed else x
                    for c in range(C):
                        last = nc.tensor.transpose(pj.bank(("x", k))[:, c * 128:c * 128 + 128],
                                                   rows[:, k, c * 128:c * 128 + 128], ident)
                    last.then_inc(pj.full_sem(("x", k)), 1)
                for k in range(SL):
                    pe.wait_ge(pj.free_sem(("x", k)), pj.uses_with(it, ("x", k)))
                for n in range(2):
                    project_features(("q", n), Wq, n * 256, 2, lambda c: src_t[:, c, :, NK - T:NK], TT)
                if kind != "self":
                    for k in range(SL):
                        pe.wait_ge(ctx_loaded[k], it * 16 + 16)
                if latent:
                    for n in range(4):
                        project_features(("k", n), Wk, n * 128, 1, lambda c: src_t[:, c, :, :], SL * NK)
                elif grouped:
                    project_features(("k", 0), Wk, 0, 1, lambda c: ctx_sb[:, c, :, :], TT)
                else:
                    kv = src_t if kind == "self" else ctx_sb
                    for n in range(2):
                        project_features(("k", n), Wk, n * 256, 2, lambda c: kv[:, c, :, :], TT)

                def project_values():
                    kv = ctx_sb if kind in ("cross", "group") else src_t
                    for n in range(v_items):
                        begin(("v", n))
                        for k, kb in ([(0, 0), (1, 0)] if grouped else [(n // KB, n % KB)]):
                            out = pj.bank(("v", n))[:, k * 128:k * 128 + 128] if grouped else pj.bank(("v", n))[:, :]
                            for c in range(C):
                                last = nc.tensor.matmul(out, kv[:, c, k, kb * 128:kb * 128 + 128], Wv[:, c, :],
                                                        start=c == 0, stop=c == C - 1)
                        last.then_inc(pj.full_sem(("v", n)), 1)

                def scores(u):
                    k = u // UPS
                    for item in pj.latest([("q", 0), ("q", 1)] + [("k", i) for i in range(k_items)]):
                        pe.wait_ge(pj.free_sem(item), pj.uses_with(it, item))
                    if grouped:
                        pe.wait_ge(diag_done, it * 2 + k + 1)
                    pe.wait_ge(scores_read, it * U + u)
                    if grouped:
                        for r in range(4):
                            j, half = 2 * (u % 2) + r // 2, r % 2
                            last = nc.tensor.matmul(sc[:, r, :], q_t[:, j, k * T:k * T + T],
                                                    k_diag[:, k, 4 * half:4 * half + 4, :], start=True, stop=True)
                    else:
                        for i in range(4 // KB):
                            for r in range(4):
                                m = i + (4 // KB) * (u % UPS)
                                last = nc.tensor.matmul(sc[:, r, i * NK:(i + 1) * NK],
                                                        q_t[32 * r:32 * r + 32, m, k * T:k * T + T],
                                                        k_t[32 * r:32 * r + 32, m, k * NK:(k + 1) * NK],
                                                        start=True, stop=True)
                    last.then_inc(scores_ready, 1)

                def transpose_probs(u, r):
                    pe.wait_ge(pt.free_sem((u, r)), pt.uses_before(it, (u, r)))
                    pe.wait_ge(exp_done, it * U * HU + u * HU + (r + 1) * HU // 4)
                    for i in range(4):
                        last = nc.tensor.transpose(pt.bank((u, r))[:, i * 128:i * 128 + 128],
                                                   S[:, u % 2, 4 * r + i, :], ident)
                    last.then_inc(pt.full_sem((u, r)), 1)

                def weigh_values(u, r):
                    k = u // UPS
                    pe.wait_ge(pt.free_sem((u, r)), pt.uses_with(it, (u, r)))
                    if r == 0:
                        if u % UPS == 0:
                            begin(("pv", k))
                        for item in pj.latest([("v", n) for n in range(v_items)]):
                            pe.wait_ge(pj.free_sem(item), pj.uses_with(it, item))
                    for i, (h, kb) in enumerate(blocks(u)[4 * r:4 * r + 4]):
                        f = (h // 4) * HD if grouped else h * HD
                        last = nc.tensor.matmul(pj.bank(("pv", k))[:, h * HD:(h + 1) * HD], PT[:, r, i, :],
                                                v[:, k, kb, f:f + HD], start=kb == 0, stop=kb == KB - 1)
                    if u % UPS == UPS - 1 and r == 3:
                        last.then_inc(pj.full_sem(("pv", k)), 1)

                scores(0)
                project_values()
                for u in range(U):
                    if u + 1 < U:
                        scores(u + 1)
                    for r in range(4):
                        transpose_probs(u, r)
                        if r > 0:
                            weigh_values(u, r - 1)
                    weigh_values(u, 3)
                for k in range(SL):
                    begin(("ot", k))
                    pe.wait_ge(pj.free_sem(("pv", k)), pj.uses_with(it, ("pv", k)))
                    for c in range(C):
                        last = nc.tensor.transpose(pj.bank(("ot", k))[:, c * 128:c * 128 + 128],
                                                   o[:, k, c * 128:c * 128 + 128], ident)
                    last.then_inc(pj.full_sem(("ot", k)), 1)
                for k in range(SL):
                    begin(("out", k))
                    pe.wait_ge(pj.free_sem(("ot", k)), pj.uses_with(it, ("ot", k)))
                    for c in range(C):
                        last = nc.tensor.matmul(pj.bank(("out", k))[:, :], o_t[:, k, c, :], Wo[:, c, :],
                                                start=c == 0, stop=c == C - 1)
                    last.then_inc(pj.full_sem(("out", k)), 1)


def mlp_phase(nc, cfg, const, x_in, x_out, x_res, weights, own_weights, next_weights):
    name, rms = cfg["name"], cfg["rms"]
    W1, W2 = weights
    ident, minus_half, vec, row = const["ident"], const["minus_half"], const["vec"], const["row"]
    with ExitStack() as stack:
        def sb(n, shape):
            return stack.enter_context(nc.sbuf_tensor(f"{name}_{n}", shape, F32))

        sem = Semaphores(nc, name, stack)

        x = sb("x", [128, SL, D])
        xr = sb("x_res", [128, SL, D]) if rms else x
        xres = sb("xres", [128, SL, D])
        xn = sb("xn", [128, SL, D])
        y = sb("y", [128, SL, D])
        stats = sb("stats", [128, SL, 10])
        rstd = sb("rstd", [128, SL, 1])
        touched = sb("touched", [128, 1])
        src_t = sb("src_t", [128, C, SL, T])
        h_t = sb("h_t", [128, HC, TT])
        banks = [stack.enter_context(nc.psum_tensor(f"{name}_bank{i}", [128, BANK], F32)) for i in range(6)]
        HI = HC // 2
        pj = Ring(f"{name}_pj", sem, banks, [("x", 0), ("x", 1)] + [("h", n) for n in range(HI)]
                  + [("out", 0), ("out", 1)])
        x_loaded = [sem(f"x_loaded{k}") for k in range(SL)]
        r_loaded = [sem(f"r_loaded{k}") for k in range(SL)]
        stored = sem("stored")
        norm_sems = (sem("stat_done"), sem("aggr_done"), sem("var_done"))
        rstd_done, xn_done, xres_done = sem("rstd_done"), sem("xn_done"), sem("xres_done")
        stack.callback(sem.clear)
        block = stack.enter_context(nc.Block())

        @block.sync
        def _(sp):
            def load(it, after=None):
                seq = sequences(sp, it)
                for k in range(SL):
                    if after is not None:
                        sp.wait_ge(xn_done, after * 2 + 2)
                        sp.wait_ge(xres_done, after * 2 + 2)
                    sp.dma_start(x[:, k, :], x_in[seq[k]]).then_inc(x_loaded[k], 16)
                    if rms:
                        sp.dma_start(xr[:, k, :], x_res[seq[k]]).then_inc(r_loaded[k], 16)

            def store(it):
                seq = sequences(sp, it)
                for k in range(SL):
                    sp.wait_ge(pj.free_sem(("out", k)), pj.uses_with(it, ("out", k)))
                    sp.dma_start(x_out[seq[k]], y[:, k, :]).then_inc(stored, 16)

            load(0)
            with sp.Fori(0, NIT - 1) as it:
                load(it + 1, after=it)
                store(it)
            store(NIT - 1)
            sp.wait_ge(stored, 16 * B)

        @block.gpsimd
        def _(pool):
            with pool.Fori(0, NIT) as it:
                rstd_on_pool(nc, pool, stats, rstd, minus_half, norm_sems[2], rstd_done, it)
                for k in range(SL):
                    pool.wait_ge((r_loaded if rms else x_loaded)[k], it * 16 + 16)
                    pool.wait_ge(pj.free_sem(("out", k)), pj.uses_of_iterations(it))
                    nc.gpsimd.tensor_tensor(xres[:, k, :], xr[:, k, :], row(cfg["b2"]), ALU.add)\
                        .then_inc(xres_done, 1)

        @block.scalar
        def _(act):
            if next_weights:
                next_weights.start(act)
            with act.Fori(0, NIT) as it:
                for k in range(SL):
                    act.wait_ge(pj.full_sem(("x", k)), pj.uses_with(it, ("x", k)))
                    for c in range(C):
                        last = nc.scalar.activation(src_t[:, c, k, :], pj.bank(("x", k))[:, c * 128:c * 128 + 128],
                                                    ACT.Identity, scale=vec(cfg["ln_s"], c),
                                                    bias=0.0 if rms else vec(cfg["ln_b"], c))
                    last.then_inc(pj.free_sem(("x", k)), 1)
                for n in range(HI):
                    act.wait_ge(pj.full_sem(("h", n)), pj.uses_with(it, ("h", n)))
                    for i in range(2):
                        last = nc.scalar.activation(h_t[:, 2 * n + i, :], pj.bank(("h", n))[:, i * TT:(i + 1) * TT],
                                                    ACT.Gelu_apprx_tanh, bias=vec(cfg["b1"], 2 * n + i))
                    last.then_inc(pj.free_sem(("h", n)), 1)

        @block.vector
        def _(dve):
            with dve.Fori(0, NIT) as it:
                for k in range(SL):
                    dve.wait_ge(x_loaded[k], it * 16 + 16)
                row_stats(nc, dve, [x[:, k, :] for k in range(SL)], stats, touched, norm_sems, it, cfg["eps"],
                          mean_square=rms)
                dve.wait_ge(rstd_done, it + 1)
                for k in range(SL):
                    dve.wait_ge(pj.full_sem(("x", k)), pj.uses_of_iterations(it))
                    if rms:
                        nc.vector.tensor_scalar(xn[:, k, :], x[:, k, :], rstd[:, k, :], None, ALU.mult)\
                            .then_inc(xn_done, 1)
                    else:
                        nc.vector.tensor_scalar(xn[:, k, :], x[:, k, :], stats[:, k, 6:7], rstd[:, k, :],
                                                ALU.subtract, ALU.mult).then_inc(xn_done, 1)
                for k in range(SL):
                    dve.wait_ge(pj.full_sem(("out", k)), pj.uses_with(it, ("out", k)))
                    dve.wait_ge(xres_done, it * 2 + k + 1)
                    dve.wait_ge(stored, it * 32)
                    nc.vector.tensor_tensor(y[:, k, :], pj.bank(("out", k))[:, :], xres[:, k, :], ALU.add)\
                        .then_inc(pj.free_sem(("out", k)), 1)

        @block.tensor
        def _(pe):
            own_weights.wait(pe)
            with pe.Fori(0, NIT) as it:
                for k in range(SL):
                    item = ("x", k)
                    pe.wait_ge(pj.free_sem(item), pj.uses_before(it, item))
                    pe.wait_ge(xn_done, it * 2 + k + 1)
                    for c in range(C):
                        last = nc.tensor.transpose(pj.bank(item)[:, c * 128:c * 128 + 128],
                                                   xn[:, k, c * 128:c * 128 + 128], ident)
                    last.then_inc(pj.full_sem(item), 1)
                for k in range(SL):
                    pe.wait_ge(pj.free_sem(("x", k)), pj.uses_with(it, ("x", k)))
                for n in range(HI):
                    item = ("h", n)
                    pe.wait_ge(pj.free_sem(item), pj.uses_before(it, item))
                    for i in range(2):
                        f = (2 * n + i) * 128
                        for c in range(C):
                            last = nc.tensor.matmul(pj.bank(item)[:, i * TT:(i + 1) * TT], W1[:, c, f:f + 128],
                                                    src_t[:, c, :, :], start=c == 0, stop=c == C - 1)
                    last.then_inc(pj.full_sem(item), 1)
                for k in range(SL):
                    item = ("out", k)
                    pe.wait_ge(pj.free_sem(item), pj.uses_before(it, item))
                    for c in range(HC):
                        if k == 0 and c % 2 == 0:
                            pe.wait_ge(pj.free_sem(("h", c // 2)), pj.uses_with(it, ("h", c // 2)))
                        last = nc.tensor.matmul(pj.bank(item)[:, :], h_t[:, c, k * T:k * T + T], W2[:, c, :],
                                                start=c == 0, stop=c == HC - 1)
                    last.then_inc(pj.full_sem(item), 1)


def recurrence_phase(nc, const, x_in, x_out, ctx, state_t, weights, own_weights, next_weights):
    F32R = mybir.dt.float32r
    W, maa_w1, maa_w2a, maa_w2b, td_w1, td_w2 = weights
    ident, minus_half, vec, row = const["ident"], const["minus_half"], const["vec"], const["row"]
    MIXES = [1, 0, 2, 3, 4]
    JH = HS // 2
    UNITS = [(m, jh) for m in range(C) for jh in range(2)]
    NU = len(UNITS)

    with ExitStack() as stack:
        def sb(n, shape, dt=F32):
            return stack.enter_context(nc.sbuf_tensor(f"rec_{n}", shape, dt))

        def ps(n, shape):
            return stack.enter_context(nc.psum_tensor(f"rec_{n}", shape, F32))

        sem = Semaphores(nc, "rec", stack)

        x = sb("x", [128, SL, D])
        xn = sb("xn", [128, SL, D])
        stats = sb("stats", [128, SL, 10])
        stats2 = sb("stats2", [128, SL, 10])
        rstd = sb("rstd", [128, SL, 1])
        touched = sb("touched", [128, 1])
        st = sb("st", [128, SL, 2, C])
        s0 = sb("s0", [128, SL, C, HS])
        xa_t = sb("xa_t", [128, C, SL, T + 1])
        sx_t = sb("sx_t", [128, C, SL, T])
        base = sb("base", [128, C, SL, T])
        t_a = sb("t_a", [128, TT])
        t_b = sb("t_b", [DM, TT])
        mixtmp = sb("mixtmp", [128, SL, C, T])
        xm = [sb(f"xm{i}", [128, C, SL, T]) for i in range(2)]
        d_t = sb("d_t", [DD, TT])
        e_t = sb("e_t", [128, C, SL, T])
        r_t = sb("r_t", [128, C, SL, T])
        k_t = sb("k_t", [128, C, SL, T])
        v_t = sb("v_t", [128, C, SL, T])
        v_hi = sb("v_hi", [128, C, SL, T], F32R)
        v_lo = sb("v_lo", [128, C, SL, T], F32R)
        v_tok = sb("v_tok", [128, SL, D])
        g2 = sb("g2", [128, SL, D])
        c_sb = sb("c_sb", [128, SL, NHR])
        small = sb("small", [128, SL, 4, NHR])
        decay = sb("decay", [128, JH, SL, T])
        A = sb("A", [128, JH, SL, T])
        S = [sb(f"S{i}", [128, JH, SL, T]) for i in range(2)]
        sel = sb("sel", [128, HS, 128], F32R)

        vb = ps("vb", [128, JH, SL, T])
        rec_out = [ps(f"rec_out{k}", [128, BANK]) for k in range(SL)]
        banks = [ps(f"bank{i}", [128, BANK]) for i in range(2)]
        order = [("x", 0), ("x", 1), ("mx", 0)]
        for f in MIXES:
            order += [("mix", f, k) for k in range(SL)]
            if f == 1:
                order += [("d", 0), ("z", 0), ("z", 1)]
            else:
                name = {0: "k", 2: "v", 3: "r", 4: "g"}[f]
                order += [(name, 0), (name, 1)]
        order += [("vt", 0), ("vt", 1), ("c", 0), ("c", 1)]
        order += [(w, k) for w in ("ogt", "o", "x2", "fk", "fr", "fv") for k in range(SL)]
        pj = Ring("rec_pj", sem, banks, order)

        x_loaded = [sem(f"x_loaded{k}") for k in range(SL)]
        st_loaded = [sem(f"st_loaded{k}") for k in range(SL)]
        s0_loaded = [sem(f"s0_loaded{k}") for k in range(SL)]
        stored = sem("stored")
        sel_loaded = sem("sel_loaded")
        sel_done = sem("sel_done")
        zero_done = sem("zero_done")
        norm_sems = (sem("stat_done"), sem("aggr_done"), sem("var_done"))
        norm2_sems = (sem("stat2_done"), sem("aggr2_done"), sem("var2_done"))
        rstd_done, rstd2_done = sem("rstd_done"), sem("rstd2_done")
        xn_done, xn2_done = sem("xn_done"), sem("xn2_done")
        first_done = sem("first_done")
        first2_done = sem("first2_done")
        sx_done, sx2_done = sem("sx_done"), sem("sx2_done")
        base_done = sem("base_done")
        tanh_done = sem("tanh_done")
        xm_done = sem("xm_done")
        dt_done = sem("dt_done")
        vsplit_done = sem("vsplit_done")
        gate_tanh = sem("gate_tanh")
        ruk_steps = sem("ruk_steps")
        decay_done = sem("decay_done")
        a_steps = sem("a_steps")
        vb_full = sem("vb_full")
        scan_done = sem("scan_done")
        prod_done = sem("prod_done")
        reduced = sem("reduced")
        gn_steps = sem("gn_steps")
        gn_red = sem("gn_red")
        gn_rstd = sem("gn_rstd")
        gn_aff = sem("gn_aff")
        og_done = sem("og_done")
        ffn_done = sem("ffn_done")
        kk_done = sem("kk_done")
        y_done = sem("y_done")
        stack.callback(sem.clear)
        block = stack.enter_context(nc.Block())

        @block.sync
        def _(sp):
            sp.dma_start(A[:, :, :, :].rearrange("p a b t -> p (a b t)"), const["sel_dram"]).then_inc(sel_loaded, 16)

            def load(it, after=None):
                seq = sequences(sp, it)
                for k in range(SL):
                    if after is not None:
                        sp.wait_ge(xn_done, after * 2 + 2)
                        sp.wait_ge(pj.free_sem(("o", k)), pj.uses_with(after, ("o", k)))
                        sp.wait_ge(first2_done, after * 2 + 2)
                        sp.wait_ge(a_steps, after * 2 * NU + 2 * NU)
                    sp.dma_start(x[:, k, :], x_in[seq[k]]).then_inc(x_loaded[k], 16)
                    sp.dma_start(st[:, k, :, :], state_t[seq[k]]).then_inc(st_loaded[k], 16)
                    sp.dma_start(s0[:, k, :, :], ctx[seq[k]]).then_inc(s0_loaded[k], 16)

            def store(it):
                seq = sequences(sp, it)
                for k in range(SL):
                    sp.wait_ge(y_done, it * SL + k + 1)
                    sp.dma_start(x_out[seq[k]], g2[:, k, :]).then_inc(stored, 16)

            load(0)
            with sp.Fori(0, NIT - 1) as it:
                load(it + 1, after=it)
                store(it)
            store(NIT - 1)
            sp.wait_ge(stored, 16 * B)

        @block.gpsimd
        def _(pool):
            with pool.Fori(0, NIT) as it:
                rstd_on_pool(nc, pool, stats, rstd, minus_half, norm_sems[2], rstd_done, it)
                for n, f in enumerate(MIXES):
                    for k in range(SL):
                        pool.wait_ge(pj.free_sem(("mix", f, k)), pj.uses_with(it, ("mix", f, k)))
                        if n >= 2:
                            w = {1: ("d", 0), 0: ("k", 1), 2: ("v", 1), 3: ("r", 1)}[MIXES[n - 2]]
                            pool.wait_ge(pj.full_sem(w), pj.uses_with(it, w))
                        nc.gpsimd.tensor_tensor(xm[n % 2][:, :, k, :], mixtmp[:, k, :, :], xa_t[:, :, k, 1:T + 1],
                                                ALU.add).then_inc(xm_done, 1)
                for n in range(NU):
                    pool.wait_ge(scan_done, it * NU + n + 1)
                    m = UNITS[n][0]
                    nc.gpsimd.tensor_tensor(S[n % 2][:, :, :, :], S[n % 2][:, :, :, :],
                                            bcast(r_t[:, m, :, :], [128, JH, SL, T], 1), ALU.mult)\
                        .then_inc(prod_done, 1)
                for k in range(SL):
                    pool.wait_ge(gn_steps, it * 16 + 8 * k + 6)
                    nc.gpsimd.tensor_tensor(small[:, k, 3, :], small[:, k, 2, :], minus_half[:, 0:NHR], ALU.pow)\
                        .then_inc(gn_rstd, 1)
                rstd_on_pool(nc, pool, stats2, rstd, minus_half, norm2_sems[2], rstd2_done, it)
                for n in range(2):
                    pool.wait_ge(pj.free_sem(("fk", n)), pj.uses_with(it, ("fk", n)))
                    nc.gpsimd.tensor_tensor(xm[1][:, 2 * n:2 * n + 2, :, :], xm[1][:, 2 * n:2 * n + 2, :, :],
                                            xm[1][:, 2 * n:2 * n + 2, :, :], ALU.mult).then_inc(kk_done, 1)

        @block.scalar
        def _(act):
            act.wait_ge(sel_loaded, 16)
            nc.scalar.copy(sel[:, :, :].rearrange("p j q -> p (j q)"), A[:, :, :, :].rearrange("p a b t -> p (a b t)"))\
                .then_inc(sel_done, 1)
            with act.Fori(0, NIT) as it:
                for k in range(SL):
                    act.wait_ge(st_loaded[k], it * 16 + 16)
                    act.wait_ge(y_done, it * 2)
                    nc.scalar.copy(xa_t[:, :, k, 0:1], st[:, k, 1, :].unsqueeze(2)).then_inc(first_done, 1)
                for k in range(SL):
                    act.wait_ge(pj.full_sem(("x", k)), pj.uses_with(it, ("x", k)))
                    for c in range(C):
                        last = nc.scalar.activation(xa_t[:, c, k, 1:T + 1], pj.bank(("x", k))[:, c * 128:c * 128 + 128],
                                                    ACT.Identity, scale=vec("r_ln1_w", c), bias=vec("r_ln1_b", c))
                    last.then_inc(pj.free_sem(("x", k)), 1)
                item = ("mx", 0)
                act.wait_ge(pj.full_sem(item), pj.uses_with(it, item))
                nc.scalar.activation(t_a[:, :], pj.bank(item)[:, 0:TT], ACT.Tanh).then_inc(tanh_done, 1)
                nc.scalar.activation(t_b[:, :], pj.bank(item)[0:DM, TT:2 * TT], ACT.Tanh).then_inc(pj.free_sem(item), 1)
                for f in MIXES:
                    if f == 1:
                        item = ("d", 0)
                        act.wait_ge(pj.full_sem(item), pj.uses_with(it, item))
                        nc.scalar.activation(d_t[:, :], pj.bank(item)[0:DD, 0:TT], ACT.Tanh).then_inc(pj.free_sem(item), 1)
                        for n in range(2):
                            item = ("z", n)
                            act.wait_ge(pj.full_sem(item), pj.uses_with(it, item))
                            for i in range(2):
                                last = nc.scalar.activation(e_t[:, 2 * n + i, :, :].rearrange("p k t -> p (k t)"),
                                                            pj.bank(item)[:, i * TT:(i + 1) * TT],
                                                            ACT.Exp, bias=vec("time_decay", 2 * n + i))
                            last.then_inc(pj.free_sem(item), 1)
                    elif f == 4:
                        for k in range(SL):
                            item = ("g", k)
                            act.wait_ge(pj.full_sem(item), pj.uses_with(it, item))
                            act.wait_ge(xm_done, it * 10 + 10)
                            nc.scalar.activation(mixtmp[:, k, :, :].rearrange("p c t -> p (c t)"), pj.bank(item)[:, :],
                                                 ACT.Tanh, scale=0.5).then_inc(gate_tanh, 1)
                    else:
                        name, dst = {0: ("k", k_t), 2: ("v", v_t), 3: ("r", r_t)}[f]
                        for n in range(2):
                            item = (name, n)
                            act.wait_ge(pj.full_sem(item), pj.uses_with(it, item))
                            nc.scalar.copy(dst[:, 2 * n:2 * n + 2, :, :],
                                           pj.bank(item)[:, :].rearrange("p (c k t) -> p c k t", c=2, k=SL))\
                                .then_inc(pj.free_sem(item), 1)
                for k in range(SL):
                    item = ("vt", k)
                    act.wait_ge(pj.full_sem(item), pj.uses_with(it, item))
                    nc.scalar.copy(v_tok[:, k, :], pj.bank(item)[:, :]).then_inc(pj.free_sem(item), 1)
                for k in range(SL):
                    item = ("c", k)
                    act.wait_ge(pj.full_sem(item), pj.uses_with(it, item))
                    nc.scalar.copy(c_sb[:, k, :], pj.bank(item)[:, 0:NHR]).then_inc(pj.free_sem(item), 1)
                for m in range(C):
                    act.wait_ge(scan_done, it * NU + 2 * m)
                    if m == 0:
                        for n in range(2):
                            act.wait_ge(pj.free_sem(("z", n)), pj.uses_with(it, ("z", n)))
                    nc.scalar.activation(decay[:, :, :, 1:T], bcast(e_t[:, m, :, 0:T - 1], [128, JH, SL, T - 1], 1),
                                         ACT.Exp, scale=-1.0).then_inc(decay_done, 1)
                for k in range(SL):
                    item = ("ogt", k)
                    act.wait_ge(pj.full_sem(item), pj.uses_with(it, item))
                    nc.scalar.copy(k_t[:, :, k, :], pj.bank(item)[:, :].rearrange("p (c t) -> p c t", c=C))\
                        .then_inc(pj.free_sem(item), 1)
                for k in range(SL):
                    act.wait_ge(sx_done, it * 2 + 2)
                    nc.scalar.copy(xa_t[:, :, k, 0:1], st[:, k, 0, :].unsqueeze(2)).then_inc(first2_done, 1)
                for k in range(SL):
                    item = ("x2", k)
                    act.wait_ge(pj.full_sem(item), pj.uses_with(it, item))
                    for c in range(C):
                        last = nc.scalar.activation(xa_t[:, c, k, 1:T + 1], pj.bank(item)[:, c * 128:c * 128 + 128],
                                                    ACT.Identity, scale=vec("r_ln2_w", c), bias=vec("r_ln2_b", c))
                    last.then_inc(pj.free_sem(item), 1)
                for n in range(2):
                    item = ("fk", n)
                    act.wait_ge(pj.full_sem(item), pj.uses_with(it, item))
                    nc.scalar.activation(xm[1][:, 2 * n:2 * n + 2, :, :],
                                         pj.bank(item)[:, :].rearrange("p (c k t) -> p c k t", c=2, k=SL), ACT.Relu)\
                        .then_inc(pj.free_sem(item), 1)
                for k in range(SL):
                    item = ("fr", k)
                    act.wait_ge(pj.full_sem(item), pj.uses_with(it, item))
                    nc.scalar.activation(mixtmp[:, k, :, :].rearrange("p c t -> p (c t)"), pj.bank(item)[:, :],
                                         ACT.Tanh, scale=0.5).then_inc(pj.free_sem(item), 1)

        @block.vector
        def _(dve):
            def freed(item, it):
                dve.wait_ge(pj.free_sem(item), pj.uses_with(it, item))

            def shift_mix(out, coef, sem_out):
                for c in range(C):
                    last = nc.vector.scalar_tensor_tensor(out[:, c, :, :], sx_t[:, c, :, :], vec(coef, c),
                                                          xa_t[:, c, :, 1:T + 1], ALU.mult, ALU.add)
                last.then_inc(sem_out, 1)

            nc.vector.memset(decay[:, :, :, 0:1], 0.0).then_inc(zero_done, 1)
            for tile in S:
                nc.vector.memset(tile[:, :, :, :], 0.0).then_inc(zero_done, 1)
            with dve.Fori(0, NIT) as it:
                for k in range(SL):
                    dve.wait_ge(x_loaded[k], it * 16 + 16)
                row_stats(nc, dve, [x[:, k, :] for k in range(SL)], stats, touched, norm_sems, it, 1e-5)
                dve.wait_ge(rstd_done, it + 1)
                for k in range(SL):
                    nc.vector.tensor_scalar(xn[:, k, :], x[:, k, :], stats[:, k, 6:7], rstd[:, k, :],
                                            ALU.subtract, ALU.mult).then_inc(xn_done, 1)
                for k in range(SL):
                    freed(("x", k), it)
                    dve.wait_ge(first_done, it * 2 + k + 1)
                    nc.vector.tensor_tensor(sx_t[:, :, k, :], xa_t[:, :, k, 0:T], xa_t[:, :, k, 1:T + 1],
                                            ALU.subtract).then_inc(sx_done, 1)
                dve.wait_ge(sx_done, it * 2 + 2)
                shift_mix(base, "maa_x", base_done)
                for n, f in enumerate(MIXES):
                    for k in range(SL):
                        item = ("mix", f, k)
                        dve.wait_ge(pj.full_sem(item), pj.uses_with(it, item))
                        dve.wait_ge(xm_done, it * 10 + (2 * n + k - 1 if n else 0))
                        for c in range(C):
                            last = nc.vector.scalar_tensor_tensor(mixtmp[:, k, c, :],
                                                                  pj.bank(item)[:, c * 128:c * 128 + 128],
                                                                  vec("maa_stack", 4 * f + c), sx_t[:, c, k, :],
                                                                  ALU.add, ALU.mult)
                        last.then_inc(pj.free_sem(item), 1)
                for k in range(SL):
                    dve.wait_ge(gate_tanh, it * 2 + k + 1)
                    dve.wait_ge(stored, it * 32)
                    nc.vector.scalar_tensor_tensor(g2[:, k, :], mixtmp[:, k, :, :].rearrange("p c t -> p (c t)"), 1.0,
                                                   pj.bank(("g", k))[:, :], ALU.add, ALU.mult)\
                        .then_inc(pj.free_sem(("g", k)), 1)
                for n in range(2):
                    freed(("v", n), it)
                nc.vector.tensor_copy(v_hi[:, :, :, :], v_t[:, :, :, :]).then_inc(vsplit_done, 1)
                dve.wait_ge(vsplit_done, it * 2 + 1)
                nc.vector.tensor_tensor(v_lo[:, :, :, :], v_t[:, :, :, :], v_hi[:, :, :, :], ALU.subtract)\
                    .then_inc(vsplit_done, 1)
                for item in pj.latest([(w, n) for w in "kr" for n in range(2)]):
                    freed(item, it)
                for c in range(C):
                    nc.vector.scalar_tensor_tensor(base[:, c, :, :], k_t[:, c, :, :], vec("u", c), r_t[:, c, :, :],
                                                   ALU.mult, ALU.mult).then_inc(ruk_steps, 1)
                for n, (m, jh) in enumerate(UNITS):
                    dve.wait_ge(vb_full, it * NU + n + 1)
                    if n == 0:
                        for k in range(SL):
                            dve.wait_ge(s0_loaded[k], it * 16 + 16)
                        dve.wait_ge(sel_done, 1)
                    dve.wait_ge(scan_done, it * NU + n)
                    nc.vector.tensor_tensor(A[:, :, :, 1:T], vb[:, :, :, 0:T - 1],
                                            bcast(k_t[:, m, :, 0:T - 1], [128, JH, SL, T - 1], 1), ALU.mult)\
                        .then_inc(a_steps, 1)
                    nc.vector.tensor_copy(A[:, :, :, 0:1].rearrange("p j k o -> p k j o"),
                                          s0[:, :, m, jh * JH:(jh + 1) * JH].unsqueeze(3)).then_inc(a_steps, 1)
                    dve.wait_ge(a_steps, it * 2 * NU + 2 * n + 2)
                    dve.wait_ge(decay_done, it * C + m + 1)
                    if n < 2:
                        dve.wait_ge(zero_done, 3)
                        dve.wait_ge(reduced, it * NU)
                    else:
                        dve.wait_ge(reduced, it * NU + n - 1)
                    nc.vector.tensor_tensor_scan(S[n % 2][:, :, :, :].rearrange("p j k t -> p (j k t)"),
                                                 decay[:, :, :, :].rearrange("p j k t -> p (j k t)"),
                                                 A[:, :, :, :].rearrange("p j k t -> p (j k t)"), 0.0,
                                                 ALU.mult, ALU.add).then_inc(scan_done, 1)
                og = mixtmp[:, :, :, :].rearrange("p k c t -> p k (c t)")
                tmp = base[:, :, :, :].rearrange("p c k t -> p (c k t)").rearrange("p (k f) -> p k f", k=SL)
                heads = "p (h j) -> p h j"
                for k in range(SL):
                    at = it * 16 + 8 * k
                    pj.wait_free(dve, it, read=[("c", 0), ("c", 1), ("vt", k)])
                    nc.vector.tensor_tensor(tmp[:, k, :].rearrange(heads, h=NHR), v_tok[:, k, :].rearrange(heads, h=NHR),
                                            bcast(c_sb[:, k, :], [128, NHR, HS], 2), ALU.mult).then_inc(gn_steps, 1)
                    dve.wait_ge(gn_steps, at + 1)
                    dve.wait_ge(reduced, it * NU + NU)
                    nc.vector.tensor_tensor(og[:, k, :].rearrange("p (m h j) -> p m h j", m=C, h=HPT),
                                            rec_out[k][:, :].rearrange("p (m j h) -> p m h j", m=C, j=HS),
                                            tmp[:, k, :].rearrange("p (m h j) -> p m h j", m=C, h=HPT), ALU.add)\
                        .then_inc(gn_steps, 1)
                    dve.wait_ge(gn_steps, at + 2)
                    nc.vector.tensor_reduce(out=small[:, k, 0, :], in_=og[:, k, :].rearrange(heads, h=NHR),
                                            op=ALU.add, axis=AX.X).then_inc(gn_steps, 1)
                    dve.wait_ge(gn_steps, at + 3)
                    nc.vector.scalar_tensor_tensor(og[:, k, :].rearrange(heads, h=NHR),
                                                   bcast(small[:, k, 0, :], [128, NHR, HS], 2), -1.0 / HS,
                                                   og[:, k, :].rearrange(heads, h=NHR), ALU.mult, ALU.add)\
                        .then_inc(gn_steps, 1)
                    dve.wait_ge(gn_steps, at + 4)
                    nc.vector.tensor_tensor(tmp[:, k, :], og[:, k, :], og[:, k, :], ALU.mult).then_inc(gn_steps, 1)
                    dve.wait_ge(gn_steps, at + 5)
                    nc.vector.tensor_reduce(out=small[:, k, 1, :], in_=tmp[:, k, :].rearrange(heads, h=NHR),
                                            op=ALU.add, axis=AX.X).then_inc(gn_red, 1)
                    dve.wait_ge(gn_red, it * 2 + k + 1)
                    nc.vector.tensor_scalar(small[:, k, 2, :], small[:, k, 1, :], 1.0 / HS, 1e-5, ALU.mult, ALU.add)\
                        .then_inc(gn_steps, 1)
                    dve.wait_ge(gn_rstd, it * 2 + k + 1)
                    nc.vector.tensor_tensor(tmp[:, k, :].rearrange(heads, h=NHR), og[:, k, :].rearrange(heads, h=NHR),
                                            bcast(small[:, k, 3, :], [128, NHR, HS], 2), ALU.mult).then_inc(gn_steps, 1)
                    dve.wait_ge(gn_steps, at + 7)
                    nc.vector.tensor_tensor(tmp[:, k, :], tmp[:, k, :], row("gn_w"), ALU.mult).then_inc(gn_steps, 1)
                    dve.wait_ge(gn_steps, at + 8)
                    nc.vector.tensor_tensor(tmp[:, k, :], tmp[:, k, :], row("gn_b"), ALU.add).then_inc(gn_aff, 1)
                    dve.wait_ge(gn_aff, it * 2 + k + 1)
                    for i in range(SL):
                        freed(("g", i), it)
                    nc.vector.scalar_tensor_tensor(og[:, k, :], tmp[:, k, :], 0.5, g2[:, k, :], ALU.mult, ALU.mult)\
                        .then_inc(og_done, 1)
                x1 = v_t[:, :, :, :].rearrange("p c k t -> p (c k t)").rearrange("p (k f) -> p k f", k=SL)
                for k in range(SL):
                    item = ("o", k)
                    dve.wait_ge(pj.full_sem(item), pj.uses_with(it, item))
                    nc.vector.tensor_tensor(x1[:, k, :], pj.bank(item)[:, :], x[:, k, :], ALU.add)\
                        .then_inc(pj.free_sem(item), 1)
                for k in range(SL):
                    freed(("o", k), it)
                row_stats(nc, dve, [x1[:, k, :] for k in range(SL)], stats2, touched, norm2_sems, it, 1e-5)
                dve.wait_ge(rstd2_done, it + 1)
                for k in range(SL):
                    nc.vector.tensor_scalar(xn[:, k, :], x1[:, k, :], stats2[:, k, 6:7], rstd[:, k, :],
                                            ALU.subtract, ALU.mult).then_inc(xn2_done, 1)
                for k in range(SL):
                    freed(("x2", k), it)
                    dve.wait_ge(first2_done, it * 2 + k + 1)
                    nc.vector.tensor_tensor(sx_t[:, :, k, :], xa_t[:, :, k, 0:T], xa_t[:, :, k, 1:T + 1],
                                            ALU.subtract).then_inc(sx2_done, 1)
                dve.wait_ge(sx2_done, it * 2 + 2)
                shift_mix(base, "ffn_k", ffn_done)
                shift_mix(xm[0], "ffn_r", ffn_done)
                for k in range(SL):
                    item = ("fv", k)
                    dve.wait_ge(pj.full_sem(item), pj.uses_with(it, item))
                    freed(("fr", k), it)
                    nc.vector.scalar_tensor_tensor(og[:, k, :], og[:, k, :], 1.0, pj.bank(item)[:, :], ALU.add, ALU.mult)\
                        .then_inc(pj.free_sem(item), 1)
                    freed(item, it)
                    nc.vector.scalar_tensor_tensor(g2[:, k, :], og[:, k, :], 0.5, x1[:, k, :], ALU.mult, ALU.add)\
                        .then_inc(y_done, 1)

        @block.tensor
        def _(pe):
            own_weights.wait(pe)
            with pe.Fori(0, NIT) as it:
                def begin(item, read=()):
                    pj.wait_free(pe, it, item, read)

                def done(item, last):
                    last.then_inc(pj.full_sem(item), 1)

                def transpose(item, src):
                    for c in range(C):
                        last = nc.tensor.transpose(pj.bank(item)[:, c * 128:c * 128 + 128], src(c), ident)
                    done(item, last)

                def features(name, Wm, src):
                    for n in range(2):
                        begin((name, n))
                        for i in range(2):
                            f = (2 * n + i) * 128
                            for c in range(C):
                                last = nc.tensor.matmul(pj.bank((name, n))[:, i * TT:(i + 1) * TT],
                                                        Wm[:, c, f:f + 128], src[:, c, :, :],
                                                        start=c == 0, stop=c == C - 1)
                        done((name, n), last)

                def rows(item, Wm, src, k):
                    for c in range(C):
                        last = nc.tensor.matmul(pj.bank(item)[:, :], src[:, c, k, :], Wm[:, c, :],
                                                start=c == 0, stop=c == C - 1)
                    done(item, last)

                for k in range(SL):
                    begin(("x", k))
                    pe.wait_ge(xn_done, it * 2 + k + 1)
                    transpose(("x", k), lambda c: xn[:, k, c * 128:c * 128 + 128])
                item = ("mx", 0)
                begin(item)
                pe.wait_ge(base_done, it + 1)
                for lo, hi in ((0, 128), (128, 160)):
                    for c in range(C):
                        last = nc.tensor.matmul(pj.bank(item)[0:hi - lo, (TT if lo else 0):(TT if lo else 0) + TT],
                                                maa_w1[:, c, lo:hi], base[:, c, :, :], start=c == 0, stop=c == C - 1)
                done(item, last)
                for n, f in enumerate(MIXES):
                    for k in range(SL):
                        item = ("mix", f, k)
                        begin(item, [("mx", 0)])
                        pe.wait_ge(tanh_done, it + 1)
                        w2, p0, tt = (maa_w2a, 32 * f, t_a) if f < 4 else (maa_w2b, 0, t_b)
                        for c in range(C):
                            last = nc.tensor.matmul(pj.bank(item)[:, c * 128:c * 128 + 128],
                                                    w2[p0:p0 + DM, c * 128:c * 128 + 128],
                                                    tt[p0:p0 + DM, k * T:k * T + T], start=True, stop=True)
                        done(item, last)
                    pe.wait_ge(xm_done, it * 10 + 2 * n + 2)
                    src = xm[n % 2]
                    if f == 1:
                        begin(("d", 0))
                        for c in range(C):
                            last = nc.tensor.matmul(pj.bank(("d", 0))[0:DD, 0:TT], td_w1[:, c, :], src[:, c, :, :],
                                                    start=c == 0, stop=c == C - 1)
                        done(("d", 0), last)
                        for n2 in range(2):
                            begin(("z", n2), [("d", 0)])
                            for i in range(2):
                                f0 = (2 * n2 + i) * 128
                                last = nc.tensor.matmul(pj.bank(("z", n2))[:, i * TT:(i + 1) * TT],
                                                        td_w2[0:DD, f0:f0 + 128], d_t[:, :], start=True, stop=True)
                            done(("z", n2), last)
                    elif f == 4:
                        for k in range(SL):
                            begin(("g", k))
                            rows(("g", k), W["g"], src, k)
                    else:
                        name = {0: "k", 2: "v", 3: "r"}[f]
                        features(name, W[name], src)
                for k in range(SL):
                    begin(("vt", k), [("v", 0), ("v", 1)])
                    transpose(("vt", k), lambda c: v_t[:, c, k, :])
                for k in range(SL):
                    begin(("c", k))
                    pe.wait_ge(ruk_steps, it * C + C)
                    for m in range(C):
                        last = nc.tensor.matmul(pj.bank(("c", k))[:, m * HPT:(m + 1) * HPT], base[:, m, k, :],
                                                const["head_mask"], start=True, stop=True)
                    done(("c", k), last)

                def spread_v(n):
                    m, jh = UNITS[n]
                    pe.wait_ge(vsplit_done, it * 2 + 2)
                    pe.wait_ge(sel_done, 1)
                    pe.wait_ge(a_steps, it * 2 * NU + 2 * n)
                    for j in range(JH):
                        for part, v_part in enumerate((v_hi, v_lo)):
                            last = nc.tensor.matmul(vb[:, j, :, :], sel[:, jh * JH + j, :], v_part[:, m, :, :],
                                                    start=part == 0, stop=part == 1)
                    last.then_inc(vb_full, 1)

                def sum_heads(n):
                    m, jh = UNITS[n]
                    pe.wait_ge(prod_done, it * NU + n + 1)
                    if n == 0:
                        pe.wait_ge(gn_steps, it * 16)
                    for k in range(SL):
                        for j in range(JH):
                            col = m * 128 + (jh * JH + j) * HPT
                            last = nc.tensor.matmul(rec_out[k][:, col:col + HPT], S[n % 2][:, j, k, :],
                                                    const["head_mask"], start=True, stop=True)
                    last.then_inc(reduced, 1)

                spread_v(0)
                for n in range(NU):
                    if n + 1 < NU:
                        spread_v(n + 1)
                    sum_heads(n)
                for k in range(SL):
                    begin(("ogt", k))
                    pe.wait_ge(og_done, it * 2 + k + 1)
                    transpose(("ogt", k), lambda c: mixtmp[:, k, c, :])
                for k in range(SL):
                    begin(("o", k), [("ogt", k)])
                    rows(("o", k), W["o"], k_t, k)
                for k in range(SL):
                    begin(("x2", k))
                    pe.wait_ge(xn2_done, it * 2 + k + 1)
                    transpose(("x2", k), lambda c: xn[:, k, c * 128:c * 128 + 128])
                pe.wait_ge(ffn_done, it * 2 + 1)
                features("fk", W["fk"], base)
                pe.wait_ge(ffn_done, it * 2 + 2)
                for k in range(SL):
                    begin(("fr", k))
                    rows(("fr", k), W["fr"], xm[0], k)
                for k in range(SL):
                    begin(("fv", k))
                    pe.wait_ge(kk_done, it * 2 + 2)
                    rows(("fv", k), W["fv"], xm[1], k)


class WeightLoad:

    def __init__(self, sem, pairs):
        self.sem, self.pairs = sem, pairs

    def start(self, engine):
        for dst, src in self.pairs:
            engine.dma_start(dst, src).then_inc(self.sem, 16)

    def wait(self, engine):
        engine.wait_ge(self.sem, 16 * len(self.pairs))


def build(nc, a, out):
    with ExitStack() as stack:
        def sb(name, shape, dt=F32):
            return stack.enter_context(nc.sbuf_tensor(name, shape, dt))

        def sem(name):
            return stack.enter_context(nc.semaphore(name))

        rows_between = [nc.dram_tensor(f"rows_{n}", (B, T, D), F32, kind="Internal").ap() for n in "ABCDEF"]
        offsets, width = {}, 0
        for name, n in VECTORS:
            offsets[name] = width
            width += n
        vectors = sb("vectors", [128, width])
        rows = sb("rows", [128, len(ROWS), D])
        ident = sb("ident", [128, 128])
        head_mask = sb("head_mask", [128, HPT])
        minus_half = sb("minus_half", [128, NHR])
        region_a = sb("region_a", [128, 8 * C * D + C * (NMIX * DM + DD) + 3 * D])

        const = {
            "ident": ident[:, :], "minus_half": minus_half, "head_mask": head_mask[:, :],
            "vec": lambda name, c: vectors[:, offsets[name] + c:offsets[name] + c + 1],
            "row": lambda name: rows[:, ROWS.index(name), :],
            "sel_dram": a["sel"],
        }

        def view(region, parts):
            at, out = 0, []
            for n, m in parts:
                out.append(region[:, at:at + n * m].rearrange("p (n m) -> p n m", n=n))
                at += n * m
            return out

        def load(name, region, parts, sources):
            views = view(region, parts)
            return views, WeightLoad(sem(f"weights_{name}"), list(zip(views, sources)))

        square = [(C, D)] * 4
        mlp = [(C, HID), (HC, D)]
        rec_names = ["k", "v", "r", "g", "o", "fk", "fr", "fv"]
        A_w, A_load = load("A", region_a, square, [a[f"A_w{i}"] for i in "qkvo"])
        C_w, C_load = load("C", region_a, mlp, [a["C_w1"], a["C_w2"]])
        E_w, E_load = load("E", region_a, [(C, D)] * 8 + [(C, NMIX * DM), (C, DD), (1, D), (1, D), (1, D)], [])
        E_sources = [a[f"E_w{n}"] for n in rec_names] + [a["maa_w1"], a["td_w1"]]
        E_load.pairs = list(zip(E_w[:10], E_sources))
        maa_w2a, maa_w2b, td_w2 = E_w[10][:, 0, :], E_w[11][0:DM, 0, :], E_w[12][0:DD, 0, :]
        E_load.pairs += [(maa_w2a, a["maa_w2"][0:128, :]), (maa_w2b, a["maa_w2"][128:160, :]), (td_w2, a["td_w2"])]
        G_w, G_load = load("G", region_a, mlp, [a["G_w1"], a["G_w2"]])
        setup = sem("setup")
        memset_done = sem("memset_done")

        with nc.Block() as block:
            @block.sync
            def _(sp):
                pairs = [(vectors[:, :], a["vectors"]), (ident[:, :], a["ident"]), (head_mask[:, :], a["head_mask"]),
                         (rows[:, :, :].rearrange("p n m -> p (n m)"), a["rows"].to_broadcast([128, len(ROWS) * D]))]
                for dst, src in pairs:
                    sp.dma_start(dst, src).then_inc(setup, 16)
                sp.wait_ge(setup, 16 * len(pairs))

            @block.scalar
            def _(act):
                A_load.start(act)

            @block.gpsimd
            def _(pool):
                nc.gpsimd.memset(minus_half[:, :], -0.5).then_inc(memset_done, 1)

        SELF = dict(kind="self", scale=32 ** -0.5, eps=1e-5, ln_s="ln1_s", ln_b="ln1_b", bq="b_q0", bk="b_k0",
                    bv="b_v0", bo="b_ao")
        CROSS = dict(kind="cross", scale=32 ** -0.5, eps=1e-5, ln_s="ln2_s", ln_b="ln2_b", bq="b_q1", bk="b_k1",
                     bv="b_v1", bo="b_co")
        GROUP = dict(kind="group", scale=16 ** -0.5, eps=1e-6, bq="g_bq", bk="g_bk", bv="g_bv", bo="g_bo")
        LATENT = dict(kind="latent", scale=1.0 / 32, bq="p_bq", bk="p_bk", bv="p_bv", bo="p_bo")
        ctx_t = a["ctx_t"]
        rA, rB, rC, rD, rE, rF = rows_between
        with nc.sbuf_tensor("region_b", [128, 4 * C * D], F32) as region_b:
            B_w, B_load = load("B", region_b, square, [a[f"B_w{i}"] for i in "qkvo"])
            D_w, D_load = load("D", region_b, [(C, D), (C, 128), (C, 128), (C, D)], [a[f"D_w{i}"] for i in "qkvo"])
            attention_phase(nc, SELF, const, a["x"], rA, ctx_t, a["mask_self"], A_w, A_load, B_load)
            attention_phase(nc, CROSS, const, rA, rB, ctx_t, a["mask_cross"], B_w, B_load, C_load)
            mlp_phase(nc, dict(name="mlp", rms=False, eps=1e-5, ln_s="ln3_s", ln_b="ln3_b", b1="b1", b2="b2"),
                      const, rB, rC, None, C_w, C_load, D_load)
            attention_phase(nc, GROUP, const, rC, rD, ctx_t, a["mask_group"], D_w, D_load, E_load)
        W = dict(zip(rec_names, E_w))
        recurrence_phase(nc, const, rD, rE, a["s0"], a["state_t"],
                         (W, E_w[8], maa_w2a, maa_w2b, E_w[9], td_w2), E_load, None)
        with nc.sbuf_tensor("region_b2", [128, 4 * C * D], F32) as region_b:
            F_w, F_load = load("F", region_b, square, [a[f"F_w{i}"] for i in "qkvo"])
            with nc.Block() as block:
                @block.scalar
                def _(act):
                    F_load.start(act)
            attention_phase(nc, LATENT, const, rE, rF, ctx_t, a["key_mask"], F_w, F_load, G_load)
        mlp_phase(nc, dict(name="pmlp", rms=True, eps=1e-6, ln_s="p_norm", b1="p_b1", b2="p_b2"),
                  const, rF, out, rE, G_w, G_load, None)


def layout(i):
    g = {k: np.asarray(v) for k, v in i.items()}

    def w(m):
        return m.reshape(-1, 128, m.shape[1]).transpose(1, 0, 2)

    def cols(v):
        return v.reshape(-1, 128).T

    L0, L1, L2, L3 = (f"L{n}_xattn_" for n in range(4))
    qkv, kv = g[L0 + "w_qkv"], g[L0 + "w_kv"]
    bqkv, bkv = g[L0 + "b_qkv"], g[L0 + "b_kv"]
    pkv, pbkv = g[L3 + "kv_w"], g[L3 + "kv_b"]
    ctx = g["ctx_2048"]
    gq = g[L1 + "Wq"].reshape(D, 8, 4, 16).transpose(0, 2, 1, 3).reshape(D, D)
    gbq = g[L1 + "bq"].reshape(8, 4, 16).transpose(1, 0, 2).reshape(D)
    gbv = np.broadcast_to(g[L1 + "bv"].reshape(8, 1, 16), (8, 4, 16)).reshape(D)
    vec = {
        "ln1_s": g[L0 + "ln1_s"], "ln1_b": g[L0 + "ln1_b"], "b_q0": bqkv[:D], "b_k0": bqkv[D:2 * D], "b_v0": bqkv[2 * D:],
        "ln2_s": g[L0 + "ln2_s"], "ln2_b": g[L0 + "ln2_b"], "b_q1": g[L0 + "b_q"], "b_k1": bkv[:D], "b_v1": bkv[D:],
        "ln3_s": g[L0 + "ln3_s"], "ln3_b": g[L0 + "ln3_b"], "b1": g[L0 + "b1"],
        "g_bq": gbq, "g_bk": g[L1 + "bk"], "g_bv": gbv,
        "r_ln1_w": g[L2 + "ln1_w"], "r_ln1_b": g[L2 + "ln1_b"], "r_ln2_w": g[L2 + "ln2_w"], "r_ln2_b": g[L2 + "ln2_b"],
        "maa_x": g[L2 + "maa_x"], "maa_stack": g[L2 + "maa_stack"].reshape(-1), "time_decay": g[L2 + "time_decay"],
        "u": g[L2 + "u"].reshape(-1), "ffn_k": g[L2 + "ffn_maa_k"], "ffn_r": g[L2 + "ffn_maa_r"],
        "p_bq": g[L3 + "q_b"], "p_bk": pbkv[0::2], "p_bv": pbkv[1::2], "p_norm": g[L3 + "postnorm_w"],
        "p_b1": g[L3 + "mlp_b1"],
    }
    row = {"b_ao": g[L0 + "b_ao"], "b_co": g[L0 + "b_co"], "b2": g[L0 + "b2"], "g_bo": g[L1 + "bo"],
           "g_gamma": g[L1 + "gamma"], "g_beta": g[L1 + "beta"], "gn_w": g[L2 + "gn_w"], "gn_b": g[L2 + "gn_b"],
           "p_bo": g[L3 + "out_b"], "p_b2": g[L3 + "mlp_b2"]}
    p = np.arange(128)
    sel = (p[:, None, None] == (p[None, None, :] // HS) * HS + np.arange(HS)[None, :, None]).astype(np.float32)
    a = {
        "x": g["x"], "ctx_t": ctx.reshape(B, T, C, 128).transpose(0, 3, 2, 1),
        "state_t": ctx[:, 0:2, :].reshape(B, 2, C, 128).transpose(0, 3, 1, 2),
        "s0": ctx[:, 2:2 + HS, :].reshape(B, C, 128, HS).transpose(0, 2, 1, 3),
        "mask_self": g["mask_1x1xSxS2_fc1"].reshape(1, T, T), "mask_cross": g["mask_Bx1xSxS2_ff1"].reshape(B, T, T),
        "mask_group": g["mask_Bx1xSxS2_ff0"].reshape(B, T, T), "key_mask": g["mask_BxS2_ik0"].reshape(B, 1, T),
        "vectors": np.concatenate([cols(vec[n]) for n, _ in VECTORS], axis=1),
        "rows": np.concatenate([row[n] for n in ROWS]).reshape(1, -1),
        "ident": np.eye(128, dtype=np.float32),
        "head_mask": (p[:, None] // HS == np.arange(HPT)[None, :]).astype(np.float32),
        "sel": sel.reshape(128, HS * 128),
        "A_wq": w(qkv[:, :D]), "A_wk": w(qkv[:, D:2 * D]), "A_wv": w(qkv[:, 2 * D:]), "A_wo": w(g[L0 + "w_ao"]),
        "B_wq": w(g[L0 + "w_q"]), "B_wk": w(kv[:, :D]), "B_wv": w(kv[:, D:]), "B_wo": w(g[L0 + "w_co"]),
        "C_w1": w(g[L0 + "w1"]), "C_w2": w(g[L0 + "w2"]),
        "D_wq": w(gq), "D_wk": w(g[L1 + "Wk"]), "D_wv": w(g[L1 + "Wv"]), "D_wo": w(g[L1 + "Wo"]),
        "maa_w1": w(g[L2 + "maa_w1"]), "maa_w2": g[L2 + "maa_w2"].reshape(NMIX * DM, D),
        "td_w1": w(g[L2 + "td_w1"]), "td_w2": g[L2 + "td_w2"],
        "F_wq": w(g[L3 + "q_w"]), "F_wk": w(pkv[:, 0::2]), "F_wv": w(pkv[:, 1::2]), "F_wo": w(g[L3 + "out_w"]),
        "G_w1": w(g[L3 + "mlp_w1"]), "G_w2": w(g[L3 + "mlp_w2"]),
    }
    for name, key in (("k", "Wk"), ("v", "Wv"), ("r", "Wr"), ("g", "Wg"), ("o", "Wo"),
                      ("fk", "Wfk"), ("fr", "Wfr"), ("fv", "Wfv")):
        a["E_w" + name] = w(g[L2 + key].T)
    return {k: np.ascontiguousarray(v) for k, v in a.items()}


def kernel(**inputs):
    import concourse.bacc as bacc
    from concourse.bass_utils import run_bass_kernel_spmd

    nc = bacc.Bacc("TRN2", target_bir_lowering=False, num_devices=1)
    arrays = layout(inputs)
    aps = {k: nc.dram_tensor(f"in_{k}", v.shape, mybir.dt.from_np(v.dtype), kind="ExternalInput").ap()
           for k, v in arrays.items()}
    out = nc.dram_tensor("out", (B, T, D), F32, kind="ExternalOutput").ap()
    build(nc, aps, out)
    result = run_bass_kernel_spmd(nc, [{f"in_{k}": v for k, v in arrays.items()}], core_ids=[0])
    return result.results[0]["out"]
```

```python
from contextlib import ExitStack

import numpy as np
import concourse.bass as bass
from concourse import mybir

F32 = mybir.dt.float32
I32 = mybir.dt.int32
ALU = mybir.AluOpType
ACT = mybir.ActivationFunctionType
AX = mybir.AxisListType

B = 16
T = 128
D = 512
C = D // 128
SL = 2
NIT = B // SL
TT = SL * T
BANK = 512
HID = 4 * D
HC = HID // 128
DM = 32
NMIX = 5
DD = 64
HS = 16
NHR = D // HS
HPT = 128 // HS

VECTORS = [("ln1_s", 4), ("ln1_b", 4), ("b_q0", 4), ("b_k0", 4), ("b_v0", 4),
           ("ln2_s", 4), ("ln2_b", 4), ("b_q1", 4), ("b_k1", 4), ("b_v1", 4),
           ("ln3_s", 4), ("ln3_b", 4), ("b1", 16),
           ("g_bq", 4), ("g_bk", 1), ("g_bv", 4),
           ("r_ln1_w", 4), ("r_ln1_b", 4), ("r_ln2_w", 4), ("r_ln2_b", 4), ("maa_x", 4),
           ("maa_stack", 20), ("time_decay", 4), ("u", 4), ("ffn_k", 4), ("ffn_r", 4),
           ("p_bq", 4), ("p_bk", 4), ("p_bv", 4), ("p_norm", 4), ("p_b1", 16)]
ROWS = ["b_ao", "b_co", "b2", "g_bo", "g_gamma", "g_beta", "gn_w", "gn_b", "p_bo", "p_b2"]


def wait_count(engine, sem, count):
    if not isinstance(count, int) or count > 0:
        engine.wait_ge(sem, count)


class Ring:

    def __init__(self, name, sem, banks, items):
        assert len(items) % len(banks) == 0
        self.banks, self.items = banks, {item: n for n, item in enumerate(items)}
        self.per_bank = len(items) // len(banks)
        self.full = [sem(f"{name}_full{b}") for b in range(len(banks))]
        self.free = [sem(f"{name}_free{b}") for b in range(len(banks))]

    def index(self, item):
        return self.items[item] % len(self.banks)

    def bank(self, item):
        return self.banks[self.index(item)]

    def full_sem(self, item):
        return self.full[self.index(item)]

    def free_sem(self, item):
        return self.free[self.index(item)]

    def latest(self, items):
        return list({self.index(item): item for item in sorted(items, key=self.items.get)}.values())

    def uses_before(self, it, item):
        return it * self.per_bank + self.items[item] // len(self.banks)

    def uses_with(self, it, item):
        return it * self.per_bank + self.items[item] // len(self.banks) + 1


    def wait_free(self, engine, it, start=None, read=()):
        need = {}
        for item in read:
            need[self.index(item)] = max(need.get(self.index(item), 0), self.items[item] // len(self.banks) + 1)
        if start is not None:
            need[self.index(start)] = max(need.get(self.index(start), 0), self.items[start] // len(self.banks))
        for bank, uses in need.items():
            wait_count(engine, self.free[bank], it * self.per_bank + uses)


class AheadRing(Ring):

    def __init__(self, name, sem, banks, before, ahead, after):
        super().__init__(name, sem, banks, before + ahead + after)
        assert len(before) % len(banks) == 0 and len(ahead) % len(banks) == 0
        self.ahead = ahead
        self.ahead_uses, self.before_uses = len(ahead) // len(banks), len(before) // len(banks)

    def uses_before(self, it, item):
        uses = self.items[item] // len(self.banks)
        if item in self.ahead:
            if isinstance(it, int) and it == 0:
                return uses - self.before_uses
            return (it - 1) * self.per_bank + (self.ahead_uses + uses)
        if isinstance(it, int) and it == NIT - 1 and uses >= self.before_uses:
            uses -= self.ahead_uses
        return it * self.per_bank + (self.ahead_uses + uses)

    def uses_with(self, it, item):
        return self.uses_before(it, item) + 1


class Semaphores:

    def __init__(self, nc, prefix, stack):
        self.nc, self.prefix, self.stack, self.held = nc, prefix, stack, []

    def __call__(self, name):
        held = self.stack.enter_context(self.nc.semaphore(f"{self.prefix}_{name}"))
        self.held.append(held)
        return held

    def clear(self):
        with self.nc.Block() as block:
            @block.gpsimd
            def _(pool):
                numbers = sorted(held.num for held in self.held)
                start = numbers[0]
                for n, after in zip(numbers, numbers[1:] + [None]):
                    if after != n + 1:
                        pool.sem_clear(range(start, n + 1))
                        start = after


def run_iterations(engine, body):
    body(0)
    with engine.Fori(1, NIT - 1) as it:
        body(it)
    body(NIT - 1, last=True)


def bcast(ap, shape, axis):
    return ap.unsqueeze(axis).to_broadcast(shape)


def sequences(engine, it):
    return [it * SL + k if isinstance(it, int) else engine.snap(it * SL + k) for k in range(SL)]


def row_stats(nc, dve, rows, stats, touched, sems, it, eps, mean_square=False):
    stat_done, aggr_done, var_done = sems
    for k in range(SL):
        nc.vector.bn_stats(stats[:, k, 0:6], rows[k]).then_inc(stat_done, 1)
    dve.wait_ge(stat_done, it * 2 + 2)
    nc.vector.tensor_copy(touched[:, 0:1], stats[:, 0, 0:1])
    for k in range(SL):
        nc.vector.bn_aggr(stats[:, k, 6:8], stats[:, k, 0:6]).then_inc(aggr_done, 1)
    dve.wait_ge(aggr_done, it * 2 + 2)
    if mean_square:
        nc.vector.tensor_tensor(stats[:, :, 8:9], stats[:, :, 6:7], stats[:, :, 6:7], ALU.mult).then_inc(var_done, 1)
        dve.wait_ge(var_done, it * 2 + 1)
        nc.vector.scalar_tensor_tensor(stats[:, :, 9:10], stats[:, :, 8:9], eps, stats[:, :, 7:8],
                                       ALU.add, ALU.add).then_inc(var_done, 1)
    else:
        nc.vector.tensor_scalar(stats[:, :, 9:10], stats[:, :, 7:8], eps, None, ALU.add).then_inc(var_done, 2)


def rstd_on_pool(nc, pool, stats, rstd, minus_half, var_done, rstd_done, it):
    pool.wait_ge(var_done, it * 2 + 2)
    nc.gpsimd.tensor_tensor(rstd[:, :, 0:1], stats[:, :, 9:10], minus_half[:, 0:SL].unsqueeze(2), ALU.pow)\
        .then_inc(rstd_done, 1)


def attention_phase(nc, cfg, const, x_in, x_out, ctx_t, mask, weights, own_weights, next_weights):
    kind = cfg["kind"]
    normed = kind in ("self", "cross")
    grouped, latent = kind == "group", kind == "latent"
    NK = 2 * T if latent else T
    KB = NK // 128
    NH = 32 if grouped else 16
    HD = D // NH
    U = 2 * SL if grouped or latent else SL
    UPS = U // SL
    HU = NH // UPS
    DVE_COPIES, ACT_COPIES = (0, 1), (2, 3)
    PARTS = 2
    HP = HU // PARTS
    scale = cfg["scale"]
    Wq, Wk, Wv, Wo = weights
    ident, minus_half = const["ident"], const["minus_half"]
    vec, row = const["vec"], const["row"]

    def early_transposes(u):
        return latent or grouped and u > 0

    def blocks(u):
        out = []
        for r in range(4):
            for i in range(4):
                if grouped:
                    out.append(((4 * (r % 2) + i) * 4 + 2 * (u % 2) + r // 2, 0))
                elif latent:
                    out.append((4 * (2 * (u % 2) + i // 2) + r, i % 2))
                else:
                    out.append((4 * i + r, 0))
        return out

    with ExitStack() as stack:
        def sb(name, shape, dt=F32):
            return stack.enter_context(nc.sbuf_tensor(f"{kind}_{name}", shape, dt))

        def ps(name, shape):
            return stack.enter_context(nc.psum_tensor(f"{kind}_{name}", shape, F32))

        sem = Semaphores(nc, kind, stack)

        x = sb("x", [128, SL, D])
        xres = sb("xres", [128, SL, D])
        xn = sb("xn", [128, SL, D]) if normed else None
        stats = sb("stats", [128, SL, 10])
        rstd = sb("rstd", [128, SL, 1])
        touched = sb("touched", [128, 1])
        src_t = sb("src_t", [128, C, SL, NK])
        ctx_sb = sb("ctx_t", [128, C, SL, T]) if kind in ("cross", "group") else None
        q_t = sb("q_t", [128, C, TT])
        k_t = sb("k_t", [128, 1 if grouped else C, SL * NK])
        k_diag = sb("k_diag", [128, SL, 8, T]) if grouped else None
        vw = 128 if grouped else D
        v = sb("v", [128, SL, KB, vw])
        msk = sb("mask", [128, SL, NK]) if not latent else None
        bias = sb("bias", [128, SL, NK]) if not grouped else None
        key_mask = sb("key_mask", [128, SL, T], I32) if latent else None
        S = sb("scores", [128, 2, 16, 128])
        negmax = sb("negmax", [128, 2, HU])
        rowsum = sb("rowsum", [128, SL, NH])
        rinv = sb("rinv", [128, SL, NH])
        PT = sb("probs_t", [128, 4, 4, 128])
        o = sb("o", [128, SL, D])
        o_t = sb("o_t", [128, SL, C, T])

        sc = ps("sc", [128, 4, BANK])
        pj_banks = [ps(f"pj{i}", [128, BANK]) for i in range(2)]
        pt_banks = [ps(f"pt{i}", [128, BANK]) for i in range(2)]
        k_items = v_items = 4 if latent else 2
        early_ot = [("pv", 0), ("ot", 0)] if U == 4 else []
        pj = AheadRing("pj", sem, pj_banks, before=[("v", n) for n in range(v_items)] + early_ot,
                       ahead=[("x", 0), ("x", 1), ("q", 0), ("q", 1)] + [("k", n) for n in range(k_items)],
                       after=[(w, k) for w in ("pv", "ot", "out") for k in range(SL) if (w, k) not in early_ot])
        pt = Ring("pt", sem, pt_banks, [(u, r) for u in range(U) for r in range(4)])

        x_loaded = [sem(f"x_loaded{k}") for k in range(SL)]
        ctx_loaded = [sem(f"ctx_loaded{k}") for k in range(SL)]
        mask_loaded = [sem(f"mask_loaded{k}") for k in range(SL)]
        stored = sem("stored")
        norm_sems = (sem("stat_done"), sem("aggr_done"), sem("var_done"))
        rstd_done = sem("rstd_done")
        xn_done = sem("xn_done")
        xres_done = sem("xres_done")
        bias_done = sem("bias_done")
        diag_done = sem("diag_done")
        scores_ready = sem("scores_ready")
        scores_read = sem("scores_read")
        bias_added = sem("bias_added")
        max_done = sem("max_done")
        exp_done = sem("exp_done")
        rinv_done = sem("rinv_done")
        y_steps = sem("y_steps")
        y_done = sem("y_done")
        stack.callback(sem.clear)
        block = stack.enter_context(nc.Block())

        @block.sync
        def _(sp):
            def load(it, after=None):
                seq = sequences(sp, it)
                for k in range(SL):
                    if after is not None:
                        if normed:
                            sp.wait_ge(xn_done, after * 2 + 2)
                        elif k == 0:
                            sp.wait_ge(pj.full_sem(("x", 0)), pj.uses_with(after, ("x", 0)))
                            sp.wait_ge(pj.full_sem(("x", 1)), pj.uses_with(after, ("x", 1)))
                        sp.wait_ge(xres_done, after * 2 + 2)
                    sp.dma_start(x[:, k, :], x_in[seq[k]]).then_inc(x_loaded[k], 16)
                for k in range(SL):
                    if kind == "cross" or grouped or latent:
                        if after is not None:
                            for item in pj.latest([("v", i) for i in range(v_items)]):
                                sp.wait_ge(pj.full_sem(item), pj.uses_with(after, item))
                        dst = src_t[:, :, k, 0:T] if latent else ctx_sb[:, :, k, :]
                        sp.dma_start(dst, ctx_t[seq[k]]).then_inc(ctx_loaded[k], 16)
                    if after is not None:
                        if not grouped:
                            sp.wait_ge(bias_done, after * 2 + 2)
                        if not latent:
                            sp.wait_ge(scores_read, after * U + U)
                    if latent:
                        sp.dma_start(key_mask[:, k, :], mask[seq[k]].to_broadcast([128, T]))\
                            .then_inc(mask_loaded[k], 16)
                    elif kind == "self":
                        sp.dma_start(msk[:, k, :], mask[0]).then_inc(mask_loaded[k], 16)
                    else:
                        sp.dma_start(msk[:, k, :], mask[seq[k]]).then_inc(mask_loaded[k], 16)

            def store(it):
                seq = sequences(sp, it)
                for k in range(SL):
                    if grouped:
                        sp.wait_ge(y_done, it * SL + k + 1)
                    else:
                        sp.wait_ge(pj.free_sem(("out", k)), pj.uses_with(it, ("out", k)))
                    sp.dma_start(x_out[seq[k]], o[:, k, :]).then_inc(stored, 16)

            load(0)
            load(1, after=0)
            store(0)
            with sp.Fori(1, NIT - 1) as it:
                load(it + 1, after=it)
                store(it)
            store(NIT - 1)
            sp.wait_ge(stored, 16 * B)

        @block.gpsimd
        def _(pool):
            def norm_scale(it):
                rstd_on_pool(nc, pool, stats, rstd, minus_half, norm_sems[2], rstd_done, it)

            def add_bias(it, u, part):
                pool.wait_ge(bias_done, it * 2 + u + 1)
                pool.wait_ge(scores_read, it * U + u + 1)
                at = slice(part * HP, (part + 1) * HP)
                nc.gpsimd.tensor_tensor(S[:, u, at, :], S[:, u, at, :], bcast(bias[:, u, :], [128, HP, T], 1),
                                        ALU.add).then_inc(bias_added, 1)

            def body(it, last=False):
                if grouped and not (isinstance(it, int) and it == 0):
                    norm_scale(it - 1)
                if kind == "self" and isinstance(it, int) and it == 0:
                    const["rows_load"].wait(pool)
                for k in range(SL):
                    pool.wait_ge(x_loaded[k], it * 16 + 16)
                    if grouped:
                        wait_count(pool, y_done, it * 2)
                    elif not isinstance(it, int) or it > 0:
                        pool.wait_ge(pj.free_sem(("out", k)), pj.uses_with(it - 1, ("out", k)))
                    nc.gpsimd.tensor_tensor(xres[:, k, :], x[:, k, :], row(cfg["bo"]), ALU.add)\
                        .then_inc(xres_done, 1)
                if normed:
                    add_bias(it, 0, 0)
                    if not last:
                        norm_scale(it + 1)
                    for part in range(1, PARTS):
                        add_bias(it, 0, part)
                    for part in range(PARTS):
                        add_bias(it, 1, part)

            if normed:
                norm_scale(0)
            run_iterations(pool, body)
            if grouped:
                norm_scale(NIT - 1)

        @block.scalar
        def _(act):
            own_weights.start(act, late=True)
            if kind == "self":
                const["rows_load"].start(act)
            if next_weights:
                next_weights.start(act)

            def rows_features(it):
                for k in range(SL):
                    act.wait_ge(pj.full_sem(("x", k)), pj.uses_with(it, ("x", k)))
                    nc.scalar.copy(src_t[:, :, k, NK - T:NK],
                                   pj.bank(("x", k))[:, :].rearrange("p (c t) -> p c t", c=C))\
                        .then_inc(pj.free_sem(("x", k)), 1)

            def queries_keys(it, part=("q", "k")):
                for w, n_items, bias_name in (("q", 2, cfg["bq"]), ("k", k_items, cfg["bk"])):
                    for n in range(n_items if w in part else 0):
                        act.wait_ge(pj.full_sem((w, n)), pj.uses_with(it, (w, n)))
                        bank = pj.bank((w, n))
                        if w == "k" and grouped:
                            last = nc.scalar.activation(k_t[:, 0, n * T:(n + 1) * T], bank[:, 0:T],
                                                        ACT.Identity, bias=vec(bias_name, 0))
                        else:
                            per = 1 if w == "k" and latent else 2
                            width = TT if w == "q" else SL * NK
                            dst = q_t if w == "q" else k_t
                            for i in range(per):
                                last = nc.scalar.activation(dst[:, n * per + i, :], bank[:, i * width:(i + 1) * width],
                                                            ACT.Identity, bias=vec(bias_name, n * per + i))
                        last.then_inc(pj.free_sem((w, n)), 1)

            def exponentials(it, u):
                if u % UPS == 0:
                    wait_count(act, rinv_done, it * 2)
                for j, h in enumerate([h for h, kb in blocks(u) if kb == 0]):
                    if j % HP == 0:
                        act.wait_ge(max_done, (it * U + u) * PARTS + j // HP + 1)
                    nc.scalar.activation(S[:, u % 2, j * KB:(j + 1) * KB, :], S[:, u % 2, j * KB:(j + 1) * KB, :],
                                         ACT.Exp, bias=negmax[:, u % 2, j:j + 1],
                                         accum_out=rowsum[:, u // UPS, h:h + 1]).then_inc(exp_done, 1)

            def output_features(it, k):
                act.wait_ge(pj.full_sem(("ot", k)), pj.uses_with(it, ("ot", k)))
                for c in range(C):
                    last = nc.scalar.activation(o_t[:, k, c, :], pj.bank(("ot", k))[:, c * 128:c * 128 + 128],
                                                ACT.Identity, bias=vec(cfg["bv"], c))
                last.then_inc(pj.free_sem(("ot", k)), 1)

            def copy_probs(it, u):
                for r in ACT_COPIES:
                    act.wait_ge(pt.full_sem((u, r)), pt.uses_with(it, (u, r)))
                    nc.scalar.copy(PT[:, r, :, :], pt.bank((u, r))[:, :].rearrange("p (i t) -> p i t", i=4))\
                        .then_inc(pt.free_sem((u, r)), 1)

            def body(it, last=False):
                for u in range(U - 1):
                    if not normed and u > 0:
                        copy_probs(it, u - 1)
                    exponentials(it, u)
                if early_ot:
                    output_features(it, 0)
                if not normed and not last:
                    rows_features(it + 1)
                if normed and not last:
                    queries_keys(it + 1, "q")
                if last:
                    copy_probs(it, U - 2)
                exponentials(it, U - 1)
                if not last:
                    queries_keys(it + 1, "k" if normed else "qk")
                if not last:
                    copy_probs(it, U - 2)
                copy_probs(it, U - 1)
                if not early_ot:
                    output_features(it, 0)
                output_features(it, 1)

            if not normed:
                rows_features(0)
            queries_keys(0)
            run_iterations(act, body)

        @block.vector
        def _(dve):
            if latent:
                nc.vector.memset(bias[:, :, T:NK], 0.0).then_inc(y_steps, 1)
                dve.wait_ge(y_steps, 1)

            def norm_stats(it):
                for k in range(SL):
                    dve.wait_ge(x_loaded[k], it * 16 + 16)
                row_stats(nc, dve, [x[:, k, :] for k in range(SL)], stats, touched, norm_sems, it, cfg["eps"])

            def norm_apply(it):
                dve.wait_ge(rstd_done, it + 1)
                if not isinstance(it, int) or it > 0:
                    dve.wait_ge(pj.full_sem(("x", 1)), pj.uses_with(it - 1, ("x", 1)))
                for k in range(SL):
                    nc.vector.tensor_scalar(xn[:, k, :], x[:, k, :], stats[:, k, 6:7], rstd[:, k, :],
                                            ALU.subtract, ALU.mult).then_inc(xn_done, 1)

            def rows_features(it):
                for k in range(SL):
                    dve.wait_ge(pj.full_sem(("x", k)), pj.uses_with(it, ("x", k)))
                    for c in range(C):
                        last = nc.vector.tensor_scalar(src_t[:, c, k, :], pj.bank(("x", k))[:, c * 128:c * 128 + 128],
                                                       vec(cfg["ln_s"], c), vec(cfg["ln_b"], c), ALU.mult, ALU.add)
                    last.then_inc(pj.free_sem(("x", k)), 1)

            def key_blocks(it):
                for k in range(SL):
                    dve.wait_ge(pj.free_sem(("k", k)), pj.uses_with(it, ("k", k)))
                    wait_count(dve, scores_ready, it * U)
                    nc.vector.tensor_tensor(k_diag[:, k, :, :], bcast(k_t[:, 0, k * T:k * T + T], [128, 8, T], 1),
                                            bcast(const["head_mask"], [128, 8, T], 2), ALU.mult)\
                        .then_inc(diag_done, 1)

            def output_stats(it):
                for k in range(SL):
                    dve.wait_ge(pj.free_sem(("out", k)), pj.uses_with(it, ("out", k)))
                row_stats(nc, dve, [xres[:, k, :] for k in range(SL)], stats, touched, norm_sems, it, cfg["eps"])

            def output_norm(it):
                dve.wait_ge(rstd_done, it + 1)
                for k in range(SL):
                    nc.vector.tensor_scalar(xres[:, k, :], xres[:, k, :], stats[:, k, 6:7], rstd[:, k, :],
                                            ALU.subtract, ALU.mult).then_inc(y_steps, 1)
                    dve.wait_ge(y_steps, it * 4 + 2 * k + 1)
                    nc.vector.tensor_tensor(xres[:, k, :], xres[:, k, :], row("g_gamma"), ALU.mult)\
                        .then_inc(y_steps, 1)
                    dve.wait_ge(y_steps, it * 4 + 2 * k + 2)
                    nc.vector.tensor_tensor(o[:, k, :], xres[:, k, :], row("g_beta"), ALU.add)\
                        .then_inc(y_done, 1)

            def body(it, last=False):
                if not grouped:
                    for k in range(SL):
                        dve.wait_ge(mask_loaded[k], it * 16 + 16)
                        if latent:
                            wait_count(dve, scores_read, it * U)
                            nc.vector.tensor_scalar(bias[:, k, 0:T], key_mask[:, k, :], 0.0, -3.0e38,
                                                    ALU.is_equal, ALU.mult).then_inc(bias_done, 1)
                        else:
                            wait_count(dve, bias_added, it * U * PARTS)
                            nc.vector.tensor_scalar(bias[:, k, :], msk[:, k, :], 1.0, 10000.0,
                                                    ALU.subtract, ALU.mult).then_inc(bias_done, 1)

                def values(n):
                    dve.wait_ge(pj.full_sem(("v", n)), pj.uses_with(it, ("v", n)))
                    bank = pj.bank(("v", n))
                    if grouped:
                        dst, src = v[:, n, 0, :], bank[:, 0:128]
                    else:
                        dst, src = v[:, n // KB, n % KB, :], bank[:, :]
                    nc.vector.tensor_copy(dst, src).then_inc(pj.free_sem(("v", n)), 1)

                def scale_and_mask(u):
                    k = u // UPS
                    dve.wait_ge(scores_ready, it * U + u + 1)
                    out, src = S[:, u % 2, :, :], sc[:, :, :].rearrange("p r (i t) -> p (r i) t", i=4)
                    if latent:
                        dve.wait_ge(bias_done, it * 2 + k + 1)
                        out = out.rearrange("p (a kb) t -> p a (kb t)", kb=2)
                        src = sc[:, :, :].rearrange("p r (i t) -> p (r i) t", i=2)
                        nc.vector.scalar_tensor_tensor(out, src, scale, bcast(bias[:, k, :], [128, 8, NK], 1),
                                                       ALU.mult, ALU.add).then_inc(scores_read, 1)
                    else:
                        dve.wait_ge(mask_loaded[k], it * 16 + 16)
                        nc.vector.scalar_tensor_tensor(out, src, scale, bcast(msk[:, k, :], [128, 16, T], 1),
                                                       ALU.mult, ALU.add if grouped else ALU.mult)\
                            .then_inc(scores_read, 1)

                def row_max(u, parts=range(PARTS)):
                    for part in parts:
                        if normed:
                            dve.wait_ge(bias_added, (it * U + u) * PARTS + part + 1)
                        else:
                            dve.wait_ge(scores_read, it * U + u + 1)
                        nc.vector.tensor_reduce(out=negmax[:, u % 2, part * HP:(part + 1) * HP],
                                                in_=S[:, u % 2, part * HP * KB:(part + 1) * HP * KB, :]
                                                .rearrange("p (h b) t -> p h (b t)", b=KB),
                                                op=ALU.max, axis=AX.X, negate=True).then_inc(max_done, 1)

                def copy_probs(u):
                    for r in DVE_COPIES:
                        dve.wait_ge(pt.full_sem((u, r)), pt.uses_with(it, (u, r)))
                        nc.vector.tensor_copy(PT[:, r, :, :], pt.bank((u, r))[:, :].rearrange("p (i t) -> p i t", i=4))\
                            .then_inc(pt.free_sem((u, r)), 1)

                def normalise(k):
                    dve.wait_ge(exp_done, it * U * HU + (k + 1) * UPS * HU)
                    nc.vector.reciprocal(rinv[:, k, :], rowsum[:, k, :]).then_inc(rinv_done, 1)
                    dve.wait_ge(rinv_done, it * 2 + k + 1)
                    dve.wait_ge(pj.full_sem(("pv", k)), pj.uses_with(it, ("pv", k)))
                    wait_count(dve, stored, it * 32)
                    nc.vector.tensor_tensor(o[:, k, :].rearrange("p (h d) -> p h d", h=NH),
                                            pj.bank(("pv", k))[:, :].rearrange("p (h d) -> p h d", h=NH),
                                            bcast(rinv[:, k, :], [128, NH, HD], 2), ALU.mult)\
                        .then_inc(pj.free_sem(("pv", k)), 1)

                first_of_all = isinstance(it, int) and it == 0
                for u in range(U):
                    if u > 0 and early_transposes(u - 1):
                        copy_probs(u - 1)
                    scale_and_mask(u)
                    if u == 0:
                        if normed and not last:
                            norm_stats(it + 1)
                        if not normed:
                            row_max(0)
                        values(0)
                        if normed and not last:
                            norm_apply(it + 1)
                        for n in range(1, v_items):
                            values(n)
                        if normed:
                            row_max(0)
                        if normed and not last:
                            rows_features(it + 1)
                    else:
                        if normed and last:
                            copy_probs(u - 1)
                            row_max(u)
                        else:
                            if grouped and not early_transposes(u - 1):
                                copy_probs(u - 1)
                            row_max(u)
                            if normed:
                                copy_probs(u - 1)
                        if grouped and u == 1 and not first_of_all:
                            output_stats(it - 1)
                            output_norm(it - 1)
                        if u % UPS == 0:
                            normalise(u // UPS - 1)
                copy_probs(U - 1)
                normalise(SL - 1)
                if grouped and not last:
                    key_blocks(it + 1)
                for k in range(SL):
                    dve.wait_ge(pj.full_sem(("out", k)), pj.uses_with(it, ("out", k)))
                    dve.wait_ge(xres_done, it * 2 + k + 1)
                    if grouped:
                        nc.vector.tensor_tensor(xres[:, k, :], pj.bank(("out", k))[:, :], xres[:, k, :], ALU.add)\
                            .then_inc(pj.free_sem(("out", k)), 1)
                    else:
                        nc.vector.tensor_tensor(o[:, k, :], pj.bank(("out", k))[:, :], xres[:, k, :], ALU.add)\
                            .then_inc(pj.free_sem(("out", k)), 1)

            if normed:
                norm_stats(0)
                norm_apply(0)
                rows_features(0)
            if grouped:
                key_blocks(0)
            run_iterations(dve, body)
            if grouped:
                output_stats(NIT - 1)
                output_norm(NIT - 1)

        @block.tensor
        def _(pe):

            def transpose_rows(it):
                for k in range(SL):
                    wait_count(pe, pj.free_sem(("x", k)), pj.uses_before(it, ("x", k)))
                    if normed:
                        pe.wait_ge(xn_done, it * 2 + k + 1)
                    else:
                        pe.wait_ge(x_loaded[k], it * 16 + 16)
                    rows = xn if normed else x
                    for c in range(C):
                        last = nc.tensor.transpose(pj.bank(("x", k))[:, c * 128:c * 128 + 128],
                                                   rows[:, k, c * 128:c * 128 + 128], ident)
                    last.then_inc(pj.full_sem(("x", k)), 1)

            def project(it):
                def project_features(item, W, f0, n_chunks, moving, width):
                    wait_count(pe, pj.free_sem(item), pj.uses_before(it, item))
                    for i in range(n_chunks):
                        for c in range(C):
                            last = nc.tensor.matmul(pj.bank(item)[:, i * width:(i + 1) * width],
                                                    W[:, c, f0 + i * 128:f0 + i * 128 + 128], moving(c),
                                                    start=c == 0, stop=c == C - 1)
                    last.then_inc(pj.full_sem(item), 1)

                for k in range(SL):
                    pe.wait_ge(pj.free_sem(("x", k)), pj.uses_with(it, ("x", k)))
                if isinstance(it, int) and it == 0:
                    own_weights.wait(pe, 0)
                for n in range(2):
                    project_features(("q", n), Wq, n * 256, 2, lambda c: src_t[:, c, :, NK - T:NK], TT)
                if kind != "self":
                    for k in range(SL):
                        pe.wait_ge(ctx_loaded[k], it * 16 + 16)
                if isinstance(it, int) and it == 0:
                    own_weights.wait(pe, 1)
                if latent:
                    for n in range(4):
                        project_features(("k", n), Wk, n * 128, 1, lambda c: src_t[:, c, :, :], SL * NK)
                elif grouped:
                    for k in range(SL):
                        project_features(("k", k), Wk, 0, 1, lambda c: ctx_sb[:, c, k, :], T)
                else:
                    kv = src_t if kind == "self" else ctx_sb
                    for n in range(2):
                        project_features(("k", n), Wk, n * 256, 2, lambda c: kv[:, c, :, :], TT)

            def body(it, last=False):
                def begin(item):
                    wait_count(pe, pj.free_sem(item), pj.uses_before(it, item))

                def project_values():
                    kv = ctx_sb if kind in ("cross", "group") else src_t
                    for n in range(v_items):
                        begin(("v", n))
                        k, kb = n // KB, n % KB
                        for c in range(C):
                            product = nc.tensor.matmul(pj.bank(("v", n))[:, 0:vw], kv[:, c, k, kb * 128:kb * 128 + 128],
                                                    Wv[:, c, :], start=c == 0, stop=c == C - 1)
                        product.then_inc(pj.full_sem(("v", n)), 1)

                def scores(u):
                    k = u // UPS
                    for item in pj.latest([("q", 0), ("q", 1)] + [("k", i) for i in range(k_items)]):
                        pe.wait_ge(pj.free_sem(item), pj.uses_with(it, item))
                    if grouped:
                        pe.wait_ge(diag_done, it * 2 + k + 1)
                    wait_count(pe, scores_read, it * U + u)
                    if grouped:
                        for r in range(4):
                            j, half = 2 * (u % 2) + r // 2, r % 2
                            product = nc.tensor.matmul(sc[:, r, :], q_t[:, j, k * T:k * T + T],
                                                    k_diag[:, k, 4 * half:4 * half + 4, :], start=True, stop=True)
                    else:
                        for i in range(4 // KB):
                            for r in range(4):
                                m = i + (4 // KB) * (u % UPS)
                                product = nc.tensor.matmul(sc[:, r, i * NK:(i + 1) * NK],
                                                        q_t[32 * r:32 * r + 32, m, k * T:k * T + T],
                                                        k_t[32 * r:32 * r + 32, m, k * NK:(k + 1) * NK],
                                                        start=True, stop=True)
                    product.then_inc(scores_ready, 1)

                def transpose_probs(u, r):
                    wait_count(pe, pt.free_sem((u, r)), pt.uses_before(it, (u, r)))
                    pe.wait_ge(exp_done, it * U * HU + u * HU + (r + 1) * HU // 4)
                    for i in range(4):
                        product = nc.tensor.transpose(pt.bank((u, r))[:, i * 128:i * 128 + 128],
                                                   S[:, u % 2, 4 * r + i, :], ident)
                    product.then_inc(pt.full_sem((u, r)), 1)

                def weigh_values(u, r):
                    k = u // UPS
                    pe.wait_ge(pt.free_sem((u, r)), pt.uses_with(it, (u, r)))
                    if r == 0:
                        if u % UPS == 0:
                            begin(("pv", k))
                        if u == 0:
                            for item in pj.latest([("v", n) for n in range(v_items)]):
                                if pj.index(item) != pj.index(("pv", 0)):
                                    pe.wait_ge(pj.free_sem(item), pj.uses_with(it, item))
                    for i, (h, kb) in enumerate(blocks(u)[4 * r:4 * r + 4]):
                        f = (h // 4) * HD if grouped else h * HD
                        product = nc.tensor.matmul(pj.bank(("pv", k))[:, h * HD:(h + 1) * HD], PT[:, r, i, :],
                                                v[:, k, kb, f:f + HD], start=kb == 0, stop=kb == KB - 1)
                    if u % UPS == UPS - 1 and r == 3:
                        product.then_inc(pj.full_sem(("pv", k)), 1)

                def transpose_output(k):
                    begin(("ot", k))
                    pe.wait_ge(pj.free_sem(("pv", k)), pj.uses_with(it, ("pv", k)))
                    for c in range(C):
                        product = nc.tensor.transpose(pj.bank(("ot", k))[:, c * 128:c * 128 + 128],
                                                   o[:, k, c * 128:c * 128 + 128], ident)
                    product.then_inc(pj.full_sem(("ot", k)), 1)

                scores(0)
                if isinstance(it, int) and it == 0:
                    own_weights.wait(pe, 2)
                    own_weights.wait(pe, 3)
                project_values()
                for u in range(U):
                    if normed and u == 0 and not last:
                        transpose_rows(it + 1)
                    if early_transposes(u):
                        transpose_probs(u, 0)
                        transpose_probs(u, 1)
                    if u + 1 < U:
                        scores(u + 1)
                    if u + 2 == U and early_ot:
                        transpose_output(0)
                        if not last:
                            transpose_rows(it + 1)
                    if u + 2 == U and not last:
                        project(it + 1)
                    if not early_transposes(u):
                        transpose_probs(u, 0)
                        transpose_probs(u, 1)
                    for r in (2, 3):
                        weigh_values(u, r - 2)
                        transpose_probs(u, r)
                    weigh_values(u, 2)
                    weigh_values(u, 3)
                if not early_ot:
                    transpose_output(0)
                transpose_output(1)
                for k in range(SL):
                    begin(("out", k))
                    pe.wait_ge(pj.free_sem(("ot", k)), pj.uses_with(it, ("ot", k)))
                    for c in range(C):
                        product = nc.tensor.matmul(pj.bank(("out", k))[:, :], o_t[:, k, c, :], Wo[:, c, :],
                                                start=c == 0, stop=c == C - 1)
                    product.then_inc(pj.full_sem(("out", k)), 1)

            transpose_rows(0)
            project(0)
            run_iterations(pe, body)


def mlp_phase(nc, cfg, const, x_in, x_out, x_res, weights, own_weights, next_weights):
    name, rms = cfg["name"], cfg["rms"]
    W1, W2 = weights
    ident, minus_half, vec, row = const["ident"], const["minus_half"], const["vec"], const["row"]
    with ExitStack() as stack:
        def sb(n, shape):
            return stack.enter_context(nc.sbuf_tensor(f"{name}_{n}", shape, F32))

        sem = Semaphores(nc, name, stack)

        x = sb("x", [128, SL, D])
        xr = sb("x_res", [128, SL, D]) if rms else x
        xres = sb("xres", [128, SL, D])
        xn = sb("xn", [128, SL, D])
        y = sb("y", [128, SL, D])
        stats = sb("stats", [128, SL, 10])
        rstd = sb("rstd", [128, SL, 1])
        touched = sb("touched", [128, 1])
        src_t = sb("src_t", [128, C, SL, T])
        h_t = sb("h_t", [128, HC, TT])
        banks = [stack.enter_context(nc.psum_tensor(f"{name}_bank{i}", [128, BANK], F32)) for i in range(8)]
        HI = HC // 2
        ph = Ring(f"{name}_hidden", sem, banks[:4], [("h", n) for n in range(HI)])
        px = Ring(f"{name}_rows", sem, banks[4:6], [("x", k) for k in range(SL)])
        po = Ring(f"{name}_out", sem, banks[6:], [("out", k) for k in range(SL)])
        x_loaded = [sem(f"x_loaded{k}") for k in range(SL)]
        r_loaded = [sem(f"r_loaded{k}") for k in range(SL)]
        stored = sem("stored")
        norm_sems = (sem("stat_done"), sem("aggr_done"), sem("var_done"))
        rstd_done, xn_done, xres_done = sem("rstd_done"), sem("xn_done"), sem("xres_done")
        stack.callback(sem.clear)
        block = stack.enter_context(nc.Block())

        @block.sync
        def _(sp):
            def load(it, after=None):
                seq = sequences(sp, it)
                for k in range(SL):
                    if after is not None:
                        sp.wait_ge(xn_done, after * 2 + 2)
                        sp.wait_ge(xres_done, after * 2 + 2)
                    sp.dma_start(x[:, k, :], x_in[seq[k]]).then_inc(x_loaded[k], 16)
                    if rms:
                        sp.dma_start(xr[:, k, :], x_res[seq[k]]).then_inc(r_loaded[k], 16)

            def store(it):
                seq = sequences(sp, it)
                for k in range(SL):
                    sp.wait_ge(po.free_sem(("out", k)), po.uses_with(it, ("out", k)))
                    sp.dma_start(x_out[seq[k]], y[:, k, :]).then_inc(stored, 16)

            load(0)
            load(1, after=0)
            store(0)
            with sp.Fori(1, NIT - 1) as it:
                load(it + 1, after=it)
                store(it)
            store(NIT - 1)
            sp.wait_ge(stored, 16 * B)

        @block.gpsimd
        def _(pool):
            def norm_scale(it):
                rstd_on_pool(nc, pool, stats, rstd, minus_half, norm_sems[2], rstd_done, it)

            def body(it, last=False):
                for k in range(SL):
                    pool.wait_ge((r_loaded if rms else x_loaded)[k], it * 16 + 16)
                    if not isinstance(it, int) or it > 0:
                        pool.wait_ge(po.free_sem(("out", k)), po.uses_with(it - 1, ("out", k)))
                    nc.gpsimd.tensor_tensor(xres[:, k, :], xr[:, k, :], row(cfg["b2"]), ALU.add)\
                        .then_inc(xres_done, 1)
                if not last:
                    norm_scale(it + 1)

            norm_scale(0)
            run_iterations(pool, body)

        @block.scalar
        def _(act):
            if next_weights:
                next_weights.start(act)

            def rows_features(it):
                for k in range(SL):
                    act.wait_ge(px.full_sem(("x", k)), px.uses_with(it, ("x", k)))
                    for c in range(C):
                        last = nc.scalar.activation(src_t[:, c, k, :], px.bank(("x", k))[:, c * 128:c * 128 + 128],
                                                    ACT.Identity, scale=vec(cfg["ln_s"], c),
                                                    bias=0.0 if rms else vec(cfg["ln_b"], c))
                    last.then_inc(px.free_sem(("x", k)), 1)

            def body(it, last=False):
                for n in range(HI):
                    act.wait_ge(ph.full_sem(("h", n)), ph.uses_with(it, ("h", n)))
                    for i in range(2):
                        hidden = nc.scalar.activation(h_t[:, 2 * n + i, :], ph.bank(("h", n))[:, i * TT:(i + 1) * TT],
                                                      ACT.Gelu_apprx_tanh, bias=vec(cfg["b1"], 2 * n + i))
                    hidden.then_inc(ph.free_sem(("h", n)), 1)
                if not last:
                    rows_features(it + 1)

            rows_features(0)
            run_iterations(act, body)

        @block.vector
        def _(dve):
            def normalise(it):
                for k in range(SL):
                    dve.wait_ge(x_loaded[k], it * 16 + 16)
                row_stats(nc, dve, [x[:, k, :] for k in range(SL)], stats, touched, norm_sems, it, cfg["eps"],
                          mean_square=rms)
                dve.wait_ge(rstd_done, it + 1)
                for k in range(SL):
                    if not isinstance(it, int) or it > 0:
                        dve.wait_ge(px.full_sem(("x", k)), px.uses_with(it - 1, ("x", k)))
                    if rms:
                        nc.vector.tensor_scalar(xn[:, k, :], x[:, k, :], rstd[:, k, :], None, ALU.mult)\
                            .then_inc(xn_done, 1)
                    else:
                        nc.vector.tensor_scalar(xn[:, k, :], x[:, k, :], stats[:, k, 6:7], rstd[:, k, :],
                                                ALU.subtract, ALU.mult).then_inc(xn_done, 1)

            def body(it, last=False):
                if not last:
                    normalise(it + 1)
                for k in range(SL):
                    dve.wait_ge(po.full_sem(("out", k)), po.uses_with(it, ("out", k)))
                    dve.wait_ge(xres_done, it * 2 + k + 1)
                    wait_count(dve, stored, it * 32)
                    nc.vector.tensor_tensor(y[:, k, :], po.bank(("out", k))[:, :], xres[:, k, :], ALU.add)\
                        .then_inc(po.free_sem(("out", k)), 1)

            normalise(0)
            run_iterations(dve, body)

        @block.tensor
        def _(pe):
            own_weights.wait(pe)

            def transpose_rows(it):
                for k in range(SL):
                    item = ("x", k)
                    wait_count(pe, px.free_sem(item), px.uses_before(it, item))
                    pe.wait_ge(xn_done, it * 2 + k + 1)
                    for c in range(C):
                        last = nc.tensor.transpose(px.bank(item)[:, c * 128:c * 128 + 128],
                                                   xn[:, k, c * 128:c * 128 + 128], ident)
                    last.then_inc(px.full_sem(item), 1)

            def body(it, last=False):
                for k in range(SL):
                    pe.wait_ge(px.free_sem(("x", k)), px.uses_with(it, ("x", k)))
                for n in range(HI):
                    item = ("h", n)
                    wait_count(pe, ph.free_sem(item), ph.uses_before(it, item))
                    for i in range(2):
                        f = (2 * n + i) * 128
                        for c in range(C):
                            product = nc.tensor.matmul(ph.bank(item)[:, i * TT:(i + 1) * TT], W1[:, c, f:f + 128],
                                                       src_t[:, c, :, :], start=c == 0, stop=c == C - 1)
                    product.then_inc(ph.full_sem(item), 1)
                if not last:
                    transpose_rows(it + 1)
                for k in range(SL):
                    item = ("out", k)
                    wait_count(pe, po.free_sem(item), po.uses_before(it, item))
                    for c in range(HC):
                        if k == 0 and c % 2 == 0:
                            pe.wait_ge(ph.free_sem(("h", c // 2)), ph.uses_with(it, ("h", c // 2)))
                        product = nc.tensor.matmul(po.bank(item)[:, :], h_t[:, c, k * T:k * T + T], W2[:, c, :],
                                                   start=c == 0, stop=c == HC - 1)
                    product.then_inc(po.full_sem(item), 1)

            transpose_rows(0)
            run_iterations(pe, body)


def recurrence_phase(nc, const, x_in, x_out, ctx, state_t, weights, own_weights, next_weights):
    W, maa_w1, maa_w2a, maa_w2b, td_w1, td_w2 = weights
    ident, minus_half, vec, row = const["ident"], const["minus_half"], const["vec"], const["row"]
    MIX_AT = {1: 0, 0: 1, 2: 2, 3: 3, 4: 4}
    JH = HS // 2
    UNITS = [(m, jh) for m in range(C) for jh in range(2)]
    NU = len(UNITS)

    with ExitStack() as stack:
        def sb(n, shape, dt=F32):
            return stack.enter_context(nc.sbuf_tensor(f"rec_{n}", shape, dt))

        def ps(n, shape):
            return stack.enter_context(nc.psum_tensor(f"rec_{n}", shape, F32))

        sem = Semaphores(nc, "rec", stack)

        x = sb("x", [128, D])
        xn = sb("xn", [128, D])
        stats = sb("stats", [128, 10])
        rstd = sb("rstd", [128, 1])
        touched = sb("touched", [128, 1])
        st1 = sb("st1", [128, C])
        xa_t = sb("xa_t", [128, C, T + 1])
        sx_t = sb("sx_t", [128, C, T])
        base = sb("base", [128, C, T])
        t_a = sb("t_a", [128, T])
        t_b = sb("t_b", [DM, T])
        mixtmp = sb("mixtmp", [128, C, T])
        xm = [sb(f"xm{i}", [128, C, T]) for i in range(2)]
        d_t = sb("d_t", [DD, T])
        ruk = sb("ruk", [128, C, T])
        gate = sb("gate", [128, D])
        e_t = sb("e_t", [128, SL, C, T])
        r_t = sb("r_t", [128, SL, C, T])
        k_t = sb("k_t", [128, SL, C, T])
        v_t = sb("v_t", [128, SL, C, T])
        v_tok = sb("v_tok", [128, SL, D])
        g2 = sb("g2", [128, SL, D])
        c_sb = sb("c_sb", [128, SL, NHR])
        s0 = sb("s0", [128, SL, C, HS])
        decay = [sb(f"decay{i}", [128, JH, T]) for i in range(2)]
        A = sb("A", [128, JH, T])
        S = [sb(f"S{i}", [128, JH, T]) for i in range(2)]
        sel = sb("sel", [128, HS, 128])
        xr = sb("xr", [128, D])
        st0 = sb("st0", [128, C])
        stats2 = sb("stats2", [128, 10])
        rstd2 = sb("rstd2", [128, 1])
        touched2 = sb("touched2", [128, 1])
        small = sb("small", [128, 4, NHR])
        og = sb("og", [128, D])
        tmp = sb("tmp", [128, D])
        og_t = sb("og_t", [128, C, T])
        x1 = sb("x1", [128, D])
        xb_t = sb("xb_t", [128, C, T + 1])
        sx2_t = sb("sx2_t", [128, C, T])
        fk_in = sb("fk_in", [128, C, T])
        fr_in = sb("fr_in", [128, C, T])
        y = sb("y", [128, D])

        vb = ps("vb", [128, JH, T])
        rec_out = ps("rec_out", [128, BANK])
        front_order = ["x", "mx", "mix1", "mix0", "d", "z", "k", "mix2", "mix3", "v", "mix4", "r"]
        back_order = ["ogt", "o", "x2", "fk", "fr", "fv"]
        pf = Ring("rec_front", sem, [ps(f"front{i}", [128, BANK]) for i in range(2)],
                  [(w, k) for k in range(SL) for w in front_order])
        pm = Ring("rec_middle", sem, [ps("middle", [128, BANK])],
                  [(w, k) for k in range(SL) for w in ("g", "vt", "c")])
        pb = Ring("rec_back", sem, [ps(f"back{i}", [128, BANK]) for i in range(2)],
                  [(w, k) for k in range(SL) for w in back_order])

        x_loaded = sem("x_loaded")
        st1_loaded = sem("st1_loaded")
        s0_loaded = [sem(f"s0_loaded{k}") for k in range(SL)]
        xr_loaded = sem("xr_loaded")
        st0_loaded = sem("st0_loaded")
        stored = sem("stored")
        sel_loaded = sem("sel_loaded")
        zero_done = sem("zero_done")
        front_norm = (sem("stat_done"), sem("aggr_done"), sem("var_done"))
        back_norm = (sem("stat2_done"), sem("aggr2_done"), sem("var2_done"))
        rstd_done, rstd2_done = sem("rstd_done"), sem("rstd2_done")
        xn_done, xn2_done = sem("xn_done"), sem("xn2_done")
        first_done = sem("first_done")
        first2_done = sem("first2_done")
        sx_done, sx2_done = sem("sx_done"), sem("sx2_done")
        base_done = sem("base_done")
        tanh_done = sem("tanh_done")
        xm_done = sem("xm_done")
        gate_tanh = sem("gate_tanh")
        ruk_done = sem("ruk_done")
        decay_done = sem("decay_done")
        a_done = sem("a_done")
        a_first = sem("a_first")
        vb_full = sem("vb_full")
        scan_done = sem("scan_done")
        prod_done = sem("prod_done")
        reduced = sem("reduced")
        gn_steps = sem("gn_steps")
        gn_red = sem("gn_red")
        gn_rstd = sem("gn_rstd")
        gn_aff = sem("gn_aff")
        og_done = sem("og_done")
        ffn_done = sem("ffn_done")
        kk_done = sem("kk_done")
        y_done = sem("y_done")
        stack.callback(sem.clear)
        block = stack.enter_context(nc.Block())

        class Sequence:

            def __init__(self, it, k):
                self.it, self.k, self.n = it, k, it * SL + k

        def run_steps(engine, step):
            first, second = 0, 1
            step(Sequence(0, first), None, None)
            step(Sequence(0, second), Sequence(0, first), None)
            with engine.Fori(0, NIT - 1) as it:
                step(Sequence(it + 1, first), Sequence(it, second), Sequence(it, first))
                step(Sequence(it + 1, second), Sequence(it + 1, first), Sequence(it, second))
            step(None, Sequence(NIT - 1, second), Sequence(NIT - 1, first))
            step(None, None, Sequence(NIT - 1, second))

        def full(engine, ring, s, item):
            engine.wait_ge(ring.full_sem((item, s.k)), ring.uses_with(s.it, (item, s.k)))

        def freed(engine, ring, s, items):
            ring.wait_free(engine, s.it, read=[(item, s.k) for item in items])

        @block.sync
        def _(sp):
            sp.dma_start(sel[:, :, :].rearrange("p j q -> p (j q)"), const["sel_dram"]).then_inc(sel_loaded, 16)

            def load_front(s):
                seq = sp_index(s)
                wait_count(sp, xn_done, s.n)
                sp.dma_start(x[:, :], x_in[seq]).then_inc(x_loaded, 16)
                wait_count(sp, first_done, s.n)
                sp.dma_start(st1[:, :], state_t[seq][:, 1, :]).then_inc(st1_loaded, 16)

            def load_middle(s):
                seq = sp_index(s)
                wait_count(sp, a_first, (s.n - 1) * NU)
                sp.dma_start(s0[:, s.k, :, :], ctx[seq]).then_inc(s0_loaded[s.k], 16)

            def load_back(s, before):
                seq = sp_index(s)
                if before is not None:
                    freed(sp, pb, before, ["o"])
                sp.dma_start(xr[:, :], x_in[seq]).then_inc(xr_loaded, 16)
                wait_count(sp, first2_done, s.n)
                sp.dma_start(st0[:, :], state_t[seq][:, 0, :]).then_inc(st0_loaded, 16)

            def sp_index(s):
                return s.n if isinstance(s.n, int) else sp.snap(s.n)

            def store(s):
                seq = sp_index(s)
                sp.wait_ge(y_done, s.n + 1)
                sp.dma_start(x_out[seq], y[:, :]).then_inc(stored, 16)

            def step(front, middle, back):
                if front is not None:
                    load_middle(front)
                    after = Sequence(front.it, 1) if front.k == 0 else Sequence(front.it + 1, 0)
                    if not (isinstance(after.n, int) and after.n >= B):
                        load_front(after)
                if middle is not None:
                    load_back(middle, back)
                if back is not None:
                    store(back)

            load_front(Sequence(0, 0))
            step(Sequence(0, 0), None, None)
            step(Sequence(0, 1), Sequence(0, 0), None)
            with sp.Fori(0, NIT - 2) as it:
                step(Sequence(it + 1, 0), Sequence(it, 1), Sequence(it, 0))
                step(Sequence(it + 1, 1), Sequence(it + 1, 0), Sequence(it, 1))
            step(Sequence(NIT - 1, 0), Sequence(NIT - 2, 1), Sequence(NIT - 2, 0))
            step(Sequence(NIT - 1, 1), Sequence(NIT - 1, 0), Sequence(NIT - 2, 1))
            step(None, Sequence(NIT - 1, 1), Sequence(NIT - 1, 0))
            step(None, None, Sequence(NIT - 1, 1))
            sp.wait_ge(stored, 16 * B)

        @block.gpsimd
        def _(pool):
            def rsqrt(s, tile, out, var_done, out_done):
                pool.wait_ge(var_done, s.n + 1)
                nc.gpsimd.tensor_tensor(out[:, 0:1], tile[:, 9:10], minus_half[:, 0:1], ALU.pow).then_inc(out_done, 1)

            def add_rows(s, f):
                at = MIX_AT[f]
                freed(pool, pf, s, [f"mix{f}"])
                last_use = {2: "d", 3: "k", 4: "v"}.get(at)
                if last_use:
                    full(pool, pf, s, last_use)
                elif at == 0:
                    wait_count(pool, pm.full[0], (s.n - 1) * 3 + 1)
                nc.gpsimd.tensor_tensor(xm[at % 2][:, :, :], mixtmp[:, :, :], xa_t[:, :, 1:T + 1], ALU.add)\
                    .then_inc(xm_done, 1)

            def multiply_states(s, u):
                pool.wait_ge(scan_done, s.n * NU + u + 1)
                nc.gpsimd.tensor_tensor(S[u % 2][:, :, :], S[u % 2][:, :, :],
                                        bcast(r_t[:, s.k, UNITS[u][0], :], [128, JH, T], 1), ALU.mult)\
                    .then_inc(prod_done, 1)

            def head_rsqrt(s):
                pool.wait_ge(gn_steps, s.n * 8 + 6)
                nc.gpsimd.tensor_tensor(small[:, 3, :], small[:, 2, :], minus_half[:, 0:NHR], ALU.pow)\
                    .then_inc(gn_rstd, 1)

            def square(s):
                freed(pool, pb, s, ["fk"])
                nc.gpsimd.tensor_tensor(fk_in[:, :, :], fk_in[:, :, :], fk_in[:, :, :], ALU.mult).then_inc(kk_done, 1)

            def step(front, middle, back):
                if front:
                    rsqrt(front, stats, rstd, front_norm[2], rstd_done)
                if middle:
                    multiply_states(middle, 0)
                    multiply_states(middle, 1)
                if back:
                    head_rsqrt(back)
                if front:
                    add_rows(front, 1)
                if middle:
                    multiply_states(middle, 2)
                    multiply_states(middle, 3)
                if front:
                    add_rows(front, 0)
                if middle:
                    multiply_states(middle, 4)
                if back:
                    rsqrt(back, stats2, rstd2, back_norm[2], rstd2_done)
                if front:
                    add_rows(front, 2)
                if middle:
                    multiply_states(middle, 5)
                    multiply_states(middle, 6)
                if front:
                    add_rows(front, 3)
                if back:
                    square(back)
                if front:
                    add_rows(front, 4)
                if middle:
                    multiply_states(middle, 7)

            run_steps(pool, step)

        @block.scalar
        def _(act):
            if next_weights:
                next_weights.start(act)

            def make_decay(s, m):
                wait_count(act, scan_done, s.n * NU + 2 * m - 2)
                if m == 0:
                    freed(act, pf, s, ["z"])
                nc.scalar.activation(decay[m % 2][:, :, 1:T], bcast(e_t[:, s.k, m, 0:T - 1], [128, JH, T - 1], 1),
                                     ACT.Exp, scale=-1.0).then_inc(decay_done, 1)

            def shifted(s, ring, item, dst, w, b, column, loaded, column_done, before, count):
                act.wait_ge(loaded, s.n * 16 + 16)
                wait_count(act, before, count)
                nc.scalar.copy(dst[:, :, 0:1], column[:, :].unsqueeze(2)).then_inc(column_done, 1)
                full(act, ring, s, item)
                bank = ring.bank((item, s.k))
                for c in range(C):
                    last = nc.scalar.activation(dst[:, c, 1:T + 1], bank[:, c * 128:c * 128 + 128],
                                                ACT.Identity, scale=vec(w, c), bias=vec(b, c))
                last.then_inc(ring.free_sem((item, s.k)), 1)

            def copy(s, ring, item, dst, func=ACT.Copy, scale=1.0, shape=None):
                full(act, ring, s, item)
                src = ring.bank((item, s.k))[:, :]
                if shape == "chunks":
                    src = src.rearrange("p (c t) -> p c t", c=C)
                nc.scalar.activation(dst, src, func, scale=scale).then_inc(ring.free_sem((item, s.k)), 1)

            def low_rank_tanh(s):
                full(act, pf, s, "mx")
                bank = pf.bank(("mx", s.k))
                nc.scalar.activation(t_a[:, :], bank[:, 0:T], ACT.Tanh).then_inc(tanh_done, 1)
                nc.scalar.activation(t_b[:, :], bank[0:DM, T:2 * T], ACT.Tanh).then_inc(pf.free_sem(("mx", s.k)), 1)

            def decay_tanh(s):
                full(act, pf, s, "d")
                nc.scalar.activation(d_t[:, :], pf.bank(("d", s.k))[0:DD, 0:T], ACT.Tanh)\
                    .then_inc(pf.free_sem(("d", s.k)), 1)

            def decay_exp(s):
                full(act, pf, s, "z")
                for c in range(C):
                    last = nc.scalar.activation(e_t[:, s.k, c, :], pf.bank(("z", s.k))[:, c * 128:c * 128 + 128],
                                                ACT.Exp, bias=vec("time_decay", c))
                last.then_inc(pf.free_sem(("z", s.k)), 1)

            def rows_front(s):
                shifted(s, pf, "x", xa_t, "r_ln1_w", "r_ln1_b", st1, st1_loaded, first_done, xm_done, s.n * 5)

            def keys(s):
                wait_count(act, prod_done, (s.n - 1) * NU)
                copy(s, pf, "k", k_t[:, s.k, :, :], shape="chunks")

            def values(s):
                copy(s, pf, "v", v_t[:, s.k, :, :], shape="chunks")

            def receptance(s):
                copy(s, pf, "r", r_t[:, s.k, :, :], shape="chunks")

            def gate_tanh_of(s):
                full(act, pm, s, "g")
                nc.scalar.activation(gate[:, :], pm.bank(("g", s.k))[:, :], ACT.Tanh, scale=0.5)\
                    .then_inc(gate_tanh, 1)

            def value_rows(s):
                wait_count(act, og_done, s.n - 1)
                copy(s, pm, "vt", v_tok[:, s.k, :])

            def bonus(s):
                full(act, pm, s, "c")
                nc.scalar.copy(c_sb[:, s.k, :], pm.bank(("c", s.k))[:, 0:NHR])\
                    .then_inc(pm.free_sem(("c", s.k)), 1)

            def gated_features(s):
                copy(s, pb, "ogt", og_t[:, :, :], shape="chunks")

            def rows_back(s):
                shifted(s, pb, "x2", xb_t, "r_ln2_w", "r_ln2_b", st0, st0_loaded, first2_done, ffn_done, s.n * 2)

            def relu(s):
                copy(s, pb, "fk", fk_in[:, :, :], ACT.Relu, shape="chunks")

            def sigmoid_tanh(s):
                copy(s, pb, "fr", og[:, :], ACT.Tanh, scale=0.5)

            def step(front, middle, back):
                if middle:
                    make_decay(middle, 0)
                if front:
                    rows_front(front)
                if middle:
                    gate_tanh_of(middle)
                    make_decay(middle, 1)
                if front:
                    low_rank_tanh(front)
                if middle:
                    value_rows(middle)
                if front:
                    decay_tanh(front)
                if back:
                    gated_features(back)
                if front:
                    decay_exp(front)
                if middle:
                    make_decay(middle, 2)
                if front:
                    keys(front)
                if middle:
                    make_decay(middle, 3)
                if back:
                    rows_back(back)
                    relu(back)
                if middle:
                    bonus(middle)
                if front:
                    values(front)
                    receptance(front)
                if back:
                    sigmoid_tanh(back)

            run_steps(act, step)

        @block.vector
        def _(dve):
            def shift_mix(out, shift, rows, coef, sem_out):
                for c in range(C):
                    last = nc.vector.scalar_tensor_tensor(out[:, c, :], shift[:, c, :], vec(coef, c),
                                                          rows[:, c, 1:T + 1], ALU.mult, ALU.add)
                last.then_inc(sem_out, 1)

            def norm_stats(s, rows, tile, dummy, sems):
                stat_done, aggr_done, var_done = sems
                nc.vector.bn_stats(tile[:, 0:6], rows[:, :]).then_inc(stat_done, 1)
                dve.wait_ge(stat_done, s.n + 1)
                nc.vector.tensor_copy(dummy[:, 0:1], tile[:, 0:1])
                nc.vector.bn_aggr(tile[:, 6:8], tile[:, 0:6]).then_inc(aggr_done, 1)
                dve.wait_ge(aggr_done, s.n + 1)
                nc.vector.tensor_scalar(tile[:, 9:10], tile[:, 7:8], 1e-5, None, ALU.add).then_inc(var_done, 1)

            def norm_apply(s, out, rows, tile, scale, scale_done, out_done):
                dve.wait_ge(scale_done, s.n + 1)
                nc.vector.tensor_scalar(out[:, :], rows[:, :], tile[:, 6:7], scale[:, 0:1],
                                        ALU.subtract, ALU.mult).then_inc(out_done, 1)

            def normalise_front(s):
                dve.wait_ge(x_loaded, s.n * 16 + 16)
                norm_stats(s, x, stats, touched, front_norm)
                norm_apply(s, xn, x, stats, rstd, rstd_done, xn_done)

            def shift_front(s):
                freed(dve, pf, s, ["x"])
                dve.wait_ge(first_done, s.n + 1)
                nc.vector.tensor_tensor(sx_t[:, :, :], xa_t[:, :, 0:T], xa_t[:, :, 1:T + 1], ALU.subtract)\
                    .then_inc(sx_done, 1)
                dve.wait_ge(sx_done, s.n + 1)
                shift_mix(base, sx_t, xa_t, "maa_x", base_done)

            def mix(s, f):
                full(dve, pf, s, f"mix{f}")
                wait_count(dve, xm_done, s.n * 5 + MIX_AT[f])
                bank = pf.bank((f"mix{f}", s.k))
                for c in range(C):
                    last = nc.vector.scalar_tensor_tensor(mixtmp[:, c, :], bank[:, c * 128:c * 128 + 128],
                                                          vec("maa_stack", 4 * f + c), sx_t[:, c, :],
                                                          ALU.add, ALU.mult)
                last.then_inc(pf.free_sem((f"mix{f}", s.k)), 1)

            def bonus_weights(s):
                freed(dve, pf, s, ["k", "r"])
                wait_count(dve, pm.free[0], s.n * 3)
                for c in range(C):
                    last = nc.vector.scalar_tensor_tensor(ruk[:, c, :], k_t[:, s.k, c, :], vec("u", c),
                                                          r_t[:, s.k, c, :], ALU.mult, ALU.mult)
                last.then_inc(ruk_done, 1)

            def make_gate(s):
                dve.wait_ge(gate_tanh, s.n + 1)
                nc.vector.scalar_tensor_tensor(g2[:, s.k, :], gate[:, :], 1.0, pm.bank(("g", s.k))[:, :],
                                               ALU.add, ALU.mult).then_inc(pm.free_sem(("g", s.k)), 1)

            def recur(s, u):
                m, jh = UNITS[u]
                dve.wait_ge(vb_full, s.n * NU + u + 1)
                if u == 0:
                    dve.wait_ge(s0_loaded[s.k], s.it * 16 + 16)
                wait_count(dve, scan_done, s.n * NU + u)
                nc.vector.tensor_tensor(A[:, :, 1:T], vb[:, :, 0:T - 1],
                                        bcast(k_t[:, s.k, m, 0:T - 1], [128, JH, T - 1], 1), ALU.mult)\
                    .then_inc(a_done, 1)
                nc.vector.tensor_copy(A[:, :, 0:1], s0[:, s.k, m, jh * JH:(jh + 1) * JH].unsqueeze(2))\
                    .then_inc(a_first, 1)
                dve.wait_ge(a_done, s.n * NU + u + 1)
                dve.wait_ge(a_first, s.n * NU + u + 1)
                dve.wait_ge(decay_done, s.n * C + m + 1)
                wait_count(dve, reduced, s.n * NU + u - 1)
                nc.vector.tensor_tensor_scan(S[u % 2][:, :, :].rearrange("p j t -> p (j t)"),
                                             decay[m % 2][:, :, :].rearrange("p j t -> p (j t)"),
                                             A[:, :, :].rearrange("p j t -> p (j t)"), 0.0,
                                             ALU.mult, ALU.add).then_inc(scan_done, 1)

            heads = "p (h j) -> p h j"

            def head_mean(s):
                at = s.n * 8
                freed(dve, pm, s, ["c", "vt"])
                nc.vector.tensor_tensor(tmp[:, :].rearrange(heads, h=NHR), v_tok[:, s.k, :].rearrange(heads, h=NHR),
                                        bcast(c_sb[:, s.k, :], [128, NHR, HS], 2), ALU.mult).then_inc(gn_steps, 1)
                dve.wait_ge(gn_steps, at + 1)
                dve.wait_ge(reduced, s.n * NU + NU)
                nc.vector.tensor_tensor(og[:, :].rearrange("p (m h j) -> p m h j", m=C, h=HPT),
                                        rec_out[:, :].rearrange("p (m j h) -> p m h j", m=C, j=HS),
                                        tmp[:, :].rearrange("p (m h j) -> p m h j", m=C, h=HPT), ALU.add)\
                    .then_inc(gn_steps, 1)
                dve.wait_ge(gn_steps, at + 2)
                nc.vector.tensor_reduce(out=small[:, 0, :], in_=og[:, :].rearrange(heads, h=NHR),
                                        op=ALU.add, axis=AX.X).then_inc(gn_steps, 1)
                dve.wait_ge(gn_steps, at + 3)
                nc.vector.scalar_tensor_tensor(og[:, :].rearrange(heads, h=NHR),
                                               bcast(small[:, 0, :], [128, NHR, HS], 2), -1.0 / HS,
                                               og[:, :].rearrange(heads, h=NHR), ALU.mult, ALU.add)\
                    .then_inc(gn_steps, 1)

            def head_variance(s):
                at = s.n * 8
                dve.wait_ge(gn_steps, at + 4)
                nc.vector.tensor_tensor(tmp[:, :], og[:, :], og[:, :], ALU.mult).then_inc(gn_steps, 1)
                dve.wait_ge(gn_steps, at + 5)
                nc.vector.tensor_reduce(out=small[:, 1, :], in_=tmp[:, :].rearrange(heads, h=NHR),
                                        op=ALU.add, axis=AX.X).then_inc(gn_red, 1)
                dve.wait_ge(gn_red, s.n + 1)
                nc.vector.tensor_scalar(small[:, 2, :], small[:, 1, :], 1.0 / HS, 1e-5, ALU.mult, ALU.add)\
                    .then_inc(gn_steps, 1)

            def head_norm(s):
                at = s.n * 8
                dve.wait_ge(gn_rstd, s.n + 1)
                nc.vector.tensor_tensor(tmp[:, :].rearrange(heads, h=NHR), og[:, :].rearrange(heads, h=NHR),
                                        bcast(small[:, 3, :], [128, NHR, HS], 2), ALU.mult).then_inc(gn_steps, 1)
                dve.wait_ge(gn_steps, at + 7)
                nc.vector.tensor_tensor(tmp[:, :], tmp[:, :], row("gn_w"), ALU.mult).then_inc(gn_steps, 1)
                dve.wait_ge(gn_steps, at + 8)
                nc.vector.tensor_tensor(tmp[:, :], tmp[:, :], row("gn_b"), ALU.add).then_inc(gn_aff, 1)
                dve.wait_ge(gn_aff, s.n + 1)
                freed(dve, pm, s, ["g"])
                nc.vector.scalar_tensor_tensor(og[:, :], tmp[:, :], 0.5, g2[:, s.k, :], ALU.mult, ALU.mult)\
                    .then_inc(og_done, 1)

            def residual(s):
                full(dve, pb, s, "o")
                dve.wait_ge(xr_loaded, s.n * 16 + 16)
                nc.vector.tensor_tensor(x1[:, :], pb.bank(("o", s.k))[:, :], xr[:, :], ALU.add)\
                    .then_inc(pb.free_sem(("o", s.k)), 1)
                freed(dve, pb, s, ["o"])
                norm_stats(s, x1, stats2, touched2, back_norm)

            def normalise_back(s):
                norm_apply(s, tmp, x1, stats2, rstd2, rstd2_done, xn2_done)

            def shift_back(s):
                freed(dve, pb, s, ["x2"])
                dve.wait_ge(first2_done, s.n + 1)
                nc.vector.tensor_tensor(sx2_t[:, :, :], xb_t[:, :, 0:T], xb_t[:, :, 1:T + 1], ALU.subtract)\
                    .then_inc(sx2_done, 1)
                dve.wait_ge(sx2_done, s.n + 1)
                shift_mix(fk_in, sx2_t, xb_t, "ffn_k", ffn_done)
                shift_mix(fr_in, sx2_t, xb_t, "ffn_r", ffn_done)

            def output(s):
                full(dve, pb, s, "fv")
                freed(dve, pb, s, ["fr"])
                nc.vector.scalar_tensor_tensor(og[:, :], og[:, :], 1.0, pb.bank(("fv", s.k))[:, :], ALU.add, ALU.mult)\
                    .then_inc(pb.free_sem(("fv", s.k)), 1)
                freed(dve, pb, s, ["fv"])
                wait_count(dve, stored, s.n * 16)
                nc.vector.scalar_tensor_tensor(y[:, :], og[:, :], 0.5, x1[:, :], ALU.mult, ALU.add).then_inc(y_done, 1)

            def step(front, middle, back):
                if front:
                    normalise_front(front)
                if middle:
                    recur(middle, 0)
                if front:
                    shift_front(front)
                if back:
                    head_mean(back)
                if middle:
                    make_gate(middle)
                    recur(middle, 1)
                if back:
                    head_variance(back)
                if middle:
                    recur(middle, 2)
                if front:
                    mix(front, 1)
                if back:
                    head_norm(back)
                if middle:
                    recur(middle, 3)
                if front:
                    mix(front, 0)
                if middle:
                    recur(middle, 4)
                if back:
                    residual(back)
                if front:
                    mix(front, 2)
                if middle:
                    recur(middle, 5)
                if front:
                    mix(front, 3)
                if middle:
                    recur(middle, 6)
                if back:
                    normalise_back(back)
                    shift_back(back)
                if front:
                    mix(front, 4)
                if middle:
                    recur(middle, 7)
                if front:
                    bonus_weights(front)
                if back:
                    output(back)

            for tile in decay:
                nc.vector.memset(tile[:, :, 0:1], 0.0).then_inc(zero_done, 1)
            for tile in S:
                nc.vector.memset(tile[:, :, :], 0.0).then_inc(zero_done, 1)
            dve.wait_ge(zero_done, 4)
            run_steps(dve, step)

        @block.tensor
        def _(pe):
            own_weights.wait(pe)
            pe.wait_ge(sel_loaded, 16)

            def begin(ring, s, item, read=()):
                ring.wait_free(pe, s.it, (item, s.k), [(other, s.k) for other in read])

            def done(ring, s, item, last):
                last.then_inc(ring.full_sem((item, s.k)), 1)

            def transpose(ring, s, item, src):
                for c in range(C):
                    last = nc.tensor.transpose(ring.bank((item, s.k))[:, c * 128:c * 128 + 128], src(c), ident)
                done(ring, s, item, last)

            def features(ring, s, item, Wm, src):
                for f in range(C):
                    for c in range(C):
                        last = nc.tensor.matmul(ring.bank((item, s.k))[:, f * T:(f + 1) * T],
                                                Wm[:, c, f * 128:f * 128 + 128], src[:, c, :],
                                                start=c == 0, stop=c == C - 1)
                done(ring, s, item, last)

            def rows(ring, s, item, Wm, src):
                for c in range(C):
                    last = nc.tensor.matmul(ring.bank((item, s.k))[:, :], src[:, c, :], Wm[:, c, :],
                                            start=c == 0, stop=c == C - 1)
                done(ring, s, item, last)

            def low_rank(s):
                begin(pf, s, "mx")
                pe.wait_ge(base_done, s.n + 1)
                bank = pf.bank(("mx", s.k))
                for lo, hi, at in ((0, 128, 0), (128, 160, T)):
                    for c in range(C):
                        last = nc.tensor.matmul(bank[0:hi - lo, at:at + T], maa_w1[:, c, lo:hi], base[:, c, :],
                                                start=c == 0, stop=c == C - 1)
                done(pf, s, "mx", last)

            def mix(s, f):
                item = f"mix{f}"
                begin(pf, s, item, ["mx"])
                pe.wait_ge(tanh_done, s.n + 1)
                w2, p0, tt = (maa_w2a, 32 * f, t_a) if f < 4 else (maa_w2b, 0, t_b)
                for c in range(C):
                    last = nc.tensor.matmul(pf.bank((item, s.k))[:, c * 128:c * 128 + 128],
                                            w2[p0:p0 + DM, c * 128:c * 128 + 128], tt[p0:p0 + DM, :],
                                            start=True, stop=True)
                done(pf, s, item, last)

            def mixed(s, f):
                pe.wait_ge(xm_done, s.n * 5 + MIX_AT[f] + 1)
                return xm[MIX_AT[f] % 2]

            def spread_v(s, u):
                m, jh = UNITS[u]
                freed(pe, pf, s, ["v"])
                wait_count(pe, a_done, s.n * NU + u)
                for j in range(JH):
                    last = nc.tensor.matmul(vb[:, j, :], sel[:, jh * JH + j, :], v_t[:, s.k, m, :],
                                            start=True, stop=True)
                last.then_inc(vb_full, 1)

            def sum_heads(s, u):
                m, jh = UNITS[u]
                pe.wait_ge(prod_done, s.n * NU + u + 1)
                if u == 0:
                    wait_count(pe, gn_steps, s.n * 8 - 6)
                for j in range(JH):
                    col = m * 128 + (jh * JH + j) * HPT
                    last = nc.tensor.matmul(rec_out[:, col:col + HPT], S[u % 2][:, j, :],
                                            const["head_mask"], start=True, stop=True)
                last.then_inc(reduced, 1)

            def rows_t(s):
                begin(pf, s, "x")
                pe.wait_ge(xn_done, s.n + 1)
                transpose(pf, s, "x", lambda c: xn[:, c * 128:c * 128 + 128])

            def decay_low(s):
                begin(pf, s, "d")
                src = mixed(s, 1)
                for c in range(C):
                    last = nc.tensor.matmul(pf.bank(("d", s.k))[0:DD, 0:T], td_w1[:, c, :], src[:, c, :],
                                            start=c == 0, stop=c == C - 1)
                done(pf, s, "d", last)

            def decay_high(s):
                begin(pf, s, "z", ["d"])
                for c in range(C):
                    last = nc.tensor.matmul(pf.bank(("z", s.k))[:, c * T:(c + 1) * T],
                                            td_w2[0:DD, c * 128:c * 128 + 128], d_t[:, :], start=True, stop=True)
                done(pf, s, "z", last)

            def project(s, w, f):
                begin(pf, s, w)
                features(pf, s, w, W[w], mixed(s, f))

            def gate_rows(s):
                begin(pm, s, "g")
                rows(pm, s, "g", W["g"], mixed(s, 4))

            def values_t(s):
                begin(pm, s, "vt")
                transpose(pm, s, "vt", lambda c: v_t[:, s.k, c, :])

            def bonus_sums(s):
                begin(pm, s, "c")
                pe.wait_ge(ruk_done, s.n + 1)
                for m in range(C):
                    last = nc.tensor.matmul(pm.bank(("c", s.k))[:, m * HPT:(m + 1) * HPT], ruk[:, m, :],
                                            const["head_mask"], start=True, stop=True)
                done(pm, s, "c", last)

            def gated_t(s):
                begin(pb, s, "ogt")
                pe.wait_ge(og_done, s.n + 1)
                transpose(pb, s, "ogt", lambda c: og[:, c * 128:c * 128 + 128])

            def out_rows(s):
                begin(pb, s, "o", ["ogt"])
                rows(pb, s, "o", W["o"], og_t)

            def normed_t(s):
                begin(pb, s, "x2")
                pe.wait_ge(xn2_done, s.n + 1)
                transpose(pb, s, "x2", lambda c: tmp[:, c * 128:c * 128 + 128])

            def ffn_keys(s):
                begin(pb, s, "fk")
                pe.wait_ge(ffn_done, s.n * 2 + 1)
                features(pb, s, "fk", W["fk"], fk_in)

            def ffn_gate(s):
                begin(pb, s, "fr")
                pe.wait_ge(ffn_done, s.n * 2 + 2)
                rows(pb, s, "fr", W["fr"], fr_in)

            def ffn_values(s):
                begin(pb, s, "fv")
                pe.wait_ge(kk_done, s.n + 1)
                rows(pb, s, "fv", W["fv"], fk_in)

            def step(front, middle, back):
                if middle:
                    spread_v(middle, 0)
                if back:
                    sum_heads(back, NU - 1)
                if front:
                    rows_t(front)
                if middle:
                    gate_rows(middle)
                    spread_v(middle, 1)
                    values_t(middle)
                if front:
                    low_rank(front)
                if middle:
                    spread_v(middle, 2)
                    sum_heads(middle, 0)
                if front:
                    mix(front, 1)
                if middle:
                    sum_heads(middle, 1)
                    bonus_sums(middle)
                    spread_v(middle, 3)
                if front:
                    mix(front, 0)
                if back:
                    gated_t(back)
                if front:
                    decay_low(front)
                if middle:
                    sum_heads(middle, 2)
                if front:
                    decay_high(front)
                if middle:
                    spread_v(middle, 4)
                if back:
                    out_rows(back)
                if front:
                    project(front, "k", 0)
                    mix(front, 2)
                if middle:
                    spread_v(middle, 5)
                    sum_heads(middle, 3)
                    spread_v(middle, 6)
                if front:
                    mix(front, 3)
                if middle:
                    sum_heads(middle, 4)
                if front:
                    project(front, "v", 2)
                if back:
                    normed_t(back)
                if front:
                    mix(front, 4)
                if middle:
                    spread_v(middle, 7)
                    sum_heads(middle, 5)
                if back:
                    ffn_keys(back)
                if front:
                    project(front, "r", 3)
                if back:
                    ffn_gate(back)
                    ffn_values(back)
                if middle:
                    sum_heads(middle, 6)

            run_steps(pe, step)


class WeightLoad:

    def __init__(self, sem, name, pairs, late=()):
        self.loads = [(sem(f"weights_{name}{n}"), dst, src, n in late) for n, (dst, src) in enumerate(pairs)]

    def start(self, engine, late=False):
        for loaded, dst, src, is_late in self.loads:
            if is_late == late:
                engine.dma_start(dst, src).then_inc(loaded, 16)

    def wait(self, engine, which=None):
        for loaded, *_ in self.loads if which is None else [self.loads[which]]:
            engine.wait_ge(loaded, 16)


def build(nc, a, out):
    with ExitStack() as stack:
        def sb(name, shape, dt=F32):
            return stack.enter_context(nc.sbuf_tensor(name, shape, dt))

        def sem(name):
            return stack.enter_context(nc.semaphore(name))

        rows_between = [nc.dram_tensor(f"rows_{n}", (B, T, D), F32, kind="Internal").ap() for n in "ABCDEF"]
        offsets, width = {}, 0
        for name, n in VECTORS:
            offsets[name] = width
            width += n
        vectors = sb("vectors", [128, width])
        rows = sb("rows", [128, len(ROWS), D])
        ident = sb("ident", [128, 128])
        head_mask = sb("head_mask", [128, HPT])
        minus_half = sb("minus_half", [128, NHR])
        region_a = sb("region_a", [128, 8 * C * D + C * (NMIX * DM + DD) + 3 * D])

        const = {
            "ident": ident[:, :], "minus_half": minus_half, "head_mask": head_mask[:, :],
            "vec": lambda name, c: vectors[:, offsets[name] + c:offsets[name] + c + 1],
            "row": lambda name: rows[:, ROWS.index(name), :],
            "sel_dram": a["sel"],
        }

        def view(region, parts):
            at, out = 0, []
            for n, m in parts:
                out.append(region[:, at:at + n * m].rearrange("p (n m) -> p n m", n=n))
                at += n * m
            return out

        def load(name, region, parts, sources):
            views = view(region, parts)
            return views, WeightLoad(sem, name, list(zip(views, sources)))

        square = [(C, D)] * 4
        mlp = [(C, HID), (HC, D)]
        rec_names = ["k", "v", "r", "g", "o", "fk", "fr", "fv"]
        A_w = view(region_a, square)
        A_load = WeightLoad(sem, "A", list(zip(A_w, [a[f"A_w{i}"] for i in "qkvo"])), late=range(4))
        C_w, C_load = load("C", region_a, mlp, [a["C_w1"], a["C_w2"]])
        E_w = view(region_a, [(C, D)] * 8 + [(C, NMIX * DM), (C, DD), (1, D), (1, D), (1, D)])
        E_sources = [a[f"E_w{n}"] for n in rec_names] + [a["maa_w1"], a["td_w1"]]
        maa_w2a, maa_w2b, td_w2 = E_w[10][:, 0, :], E_w[11][0:DM, 0, :], E_w[12][0:DD, 0, :]
        E_load = WeightLoad(sem, "E", list(zip(E_w[:10], E_sources)) + [
            (maa_w2a, a["maa_w2"][0:128, :]), (maa_w2b, a["maa_w2"][128:160, :]), (td_w2, a["td_w2"])])
        G_w, G_load = load("G", region_a, mlp, [a["G_w1"], a["G_w2"]])
        rows_load = WeightLoad(sem, "rows", [(rows[:, :, :].rearrange("p n m -> p (n m)"),
                                              a["rows"].to_broadcast([128, len(ROWS) * D]))])
        const["rows_load"] = rows_load
        setup = sem("setup")
        memset_done = sem("memset_done")

        with nc.Block() as block:
            @block.sync
            def _(sp):
                pairs = [(vectors[:, :], a["vectors"]), (ident[:, :], a["ident"]), (head_mask[:, :], a["head_mask"])]
                for dst, src in pairs:
                    sp.dma_start(dst, src).then_inc(setup, 16)
                sp.wait_ge(setup, 16 * len(pairs))

            @block.gpsimd
            def _(pool):
                nc.gpsimd.memset(minus_half[:, :], -0.5).then_inc(memset_done, 1)

        SELF = dict(kind="self", scale=32 ** -0.5, eps=1e-5, ln_s="ln1_s", ln_b="ln1_b", bq="b_q0", bk="b_k0",
                    bv="b_v0", bo="b_ao")
        CROSS = dict(kind="cross", scale=32 ** -0.5, eps=1e-5, ln_s="ln2_s", ln_b="ln2_b", bq="b_q1", bk="b_k1",
                     bv="b_v1", bo="b_co")
        GROUP = dict(kind="group", scale=16 ** -0.5, eps=1e-6, bq="g_bq", bk="g_bk", bv="g_bv", bo="g_bo")
        LATENT = dict(kind="latent", scale=1.0 / 32, bq="p_bq", bk="p_bk", bv="p_bv", bo="p_bo")
        ctx_t = a["ctx_t"]
        rA, rB, rC, rD, rE, rF = rows_between
        with nc.sbuf_tensor("region_b", [128, 4 * C * D], F32) as region_b:
            B_w, B_load = load("B", region_b, square, [a[f"B_w{i}"] for i in "qkvo"])
            D_w, D_load = load("D", region_b, [(C, D), (C, 128), (C, 128), (C, D)], [a[f"D_w{i}"] for i in "qkvo"])
            attention_phase(nc, SELF, const, a["x"], rA, ctx_t, a["mask_self"], A_w, A_load, B_load)
            attention_phase(nc, CROSS, const, rA, rB, ctx_t, a["mask_cross"], B_w, B_load, C_load)
            mlp_phase(nc, dict(name="mlp", rms=False, eps=1e-5, ln_s="ln3_s", ln_b="ln3_b", b1="b1", b2="b2"),
                      const, rB, rC, None, C_w, C_load, D_load)
            attention_phase(nc, GROUP, const, rC, rD, ctx_t, a["mask_group"], D_w, D_load, E_load)
        with nc.sbuf_tensor("F_query_key", [128, 2 * C * D], F32) as F_query_key:
            F_w, F_load = load("F", F_query_key, square[:2], [a["F_wq"], a["F_wk"]])
            W = dict(zip(rec_names, E_w))
            recurrence_phase(nc, const, rD, rE, a["s0"], a["state_t"],
                             (W, E_w[8], maa_w2a, maa_w2b, E_w[9], td_w2), E_load, F_load)
            with nc.sbuf_tensor("F_value_out", [128, 2 * C * D], F32) as F_value_out:
                late_w = view(F_value_out, square[2:])
                F_load.loads += WeightLoad(sem, "F_late", list(zip(late_w, [a["F_wv"], a["F_wo"]])), late=(0, 1)).loads
                attention_phase(nc, LATENT, const, rE, rF, ctx_t, a["key_mask"], F_w + late_w, F_load,
                                G_load)
        mlp_phase(nc, dict(name="pmlp", rms=True, eps=1e-6, ln_s="p_norm", b1="p_b1", b2="p_b2"),
                  const, rF, out, rE, G_w, G_load, None)


def layout(i):
    g = {k: np.asarray(v) for k, v in i.items()}

    def w(m):
        return m.reshape(-1, 128, m.shape[1]).transpose(1, 0, 2)

    def cols(v):
        return v.reshape(-1, 128).T

    L0, L1, L2, L3 = (f"L{n}_xattn_" for n in range(4))
    qkv, kv = g[L0 + "w_qkv"], g[L0 + "w_kv"]
    bqkv, bkv = g[L0 + "b_qkv"], g[L0 + "b_kv"]
    pkv, pbkv = g[L3 + "kv_w"], g[L3 + "kv_b"]
    ctx = g["ctx_2048"]
    gq = g[L1 + "Wq"].reshape(D, 8, 4, 16).transpose(0, 2, 1, 3).reshape(D, D)
    gbq = g[L1 + "bq"].reshape(8, 4, 16).transpose(1, 0, 2).reshape(D)
    gbv = np.broadcast_to(g[L1 + "bv"].reshape(8, 1, 16), (8, 4, 16)).reshape(D)
    vec = {
        "ln1_s": g[L0 + "ln1_s"], "ln1_b": g[L0 + "ln1_b"], "b_q0": bqkv[:D], "b_k0": bqkv[D:2 * D], "b_v0": bqkv[2 * D:],
        "ln2_s": g[L0 + "ln2_s"], "ln2_b": g[L0 + "ln2_b"], "b_q1": g[L0 + "b_q"], "b_k1": bkv[:D], "b_v1": bkv[D:],
        "ln3_s": g[L0 + "ln3_s"], "ln3_b": g[L0 + "ln3_b"], "b1": g[L0 + "b1"],
        "g_bq": gbq, "g_bk": g[L1 + "bk"], "g_bv": gbv,
        "r_ln1_w": g[L2 + "ln1_w"], "r_ln1_b": g[L2 + "ln1_b"], "r_ln2_w": g[L2 + "ln2_w"], "r_ln2_b": g[L2 + "ln2_b"],
        "maa_x": g[L2 + "maa_x"], "maa_stack": g[L2 + "maa_stack"].reshape(-1), "time_decay": g[L2 + "time_decay"],
        "u": g[L2 + "u"].reshape(-1), "ffn_k": g[L2 + "ffn_maa_k"], "ffn_r": g[L2 + "ffn_maa_r"],
        "p_bq": g[L3 + "q_b"], "p_bk": pbkv[0::2], "p_bv": pbkv[1::2], "p_norm": g[L3 + "postnorm_w"],
        "p_b1": g[L3 + "mlp_b1"],
    }
    row = {"b_ao": g[L0 + "b_ao"], "b_co": g[L0 + "b_co"], "b2": g[L0 + "b2"], "g_bo": g[L1 + "bo"],
           "g_gamma": g[L1 + "gamma"], "g_beta": g[L1 + "beta"], "gn_w": g[L2 + "gn_w"], "gn_b": g[L2 + "gn_b"],
           "p_bo": g[L3 + "out_b"], "p_b2": g[L3 + "mlp_b2"]}
    p = np.arange(128)
    sel = (p[:, None, None] == (p[None, None, :] // HS) * HS + np.arange(HS)[None, :, None]).astype(np.float32)
    a = {
        "x": g["x"], "ctx_t": ctx.reshape(B, T, C, 128).transpose(0, 3, 2, 1),
        "state_t": ctx[:, 0:2, :].reshape(B, 2, C, 128).transpose(0, 3, 1, 2),
        "s0": ctx[:, 2:2 + HS, :].reshape(B, C, 128, HS).transpose(0, 2, 1, 3),
        "mask_self": g["mask_1x1xSxS2_fc1"].reshape(1, T, T), "mask_cross": g["mask_Bx1xSxS2_ff1"].reshape(B, T, T),
        "mask_group": g["mask_Bx1xSxS2_ff0"].reshape(B, T, T), "key_mask": g["mask_BxS2_ik0"].reshape(B, 1, T),
        "vectors": np.concatenate([cols(vec[n]) for n, _ in VECTORS], axis=1),
        "rows": np.concatenate([row[n] for n in ROWS]).reshape(1, -1),
        "ident": np.eye(128, dtype=np.float32),
        "head_mask": (p[:, None] // HS == np.arange(HPT)[None, :]).astype(np.float32),
        "sel": sel.reshape(128, HS * 128),
        "A_wq": w(qkv[:, :D]), "A_wk": w(qkv[:, D:2 * D]), "A_wv": w(qkv[:, 2 * D:]), "A_wo": w(g[L0 + "w_ao"]),
        "B_wq": w(g[L0 + "w_q"]), "B_wk": w(kv[:, :D]), "B_wv": w(kv[:, D:]), "B_wo": w(g[L0 + "w_co"]),
        "C_w1": w(g[L0 + "w1"]), "C_w2": w(g[L0 + "w2"]),
        "D_wq": w(gq), "D_wk": w(g[L1 + "Wk"]), "D_wv": w(g[L1 + "Wv"]), "D_wo": w(g[L1 + "Wo"]),
        "maa_w1": w(g[L2 + "maa_w1"]), "maa_w2": g[L2 + "maa_w2"].reshape(NMIX * DM, D),
        "td_w1": w(g[L2 + "td_w1"]), "td_w2": g[L2 + "td_w2"],
        "F_wq": w(g[L3 + "q_w"]), "F_wk": w(pkv[:, 0::2]), "F_wv": w(pkv[:, 1::2]), "F_wo": w(g[L3 + "out_w"]),
        "G_w1": w(g[L3 + "mlp_w1"]), "G_w2": w(g[L3 + "mlp_w2"]),
    }
    for name, key in (("k", "Wk"), ("v", "Wv"), ("r", "Wr"), ("g", "Wg"), ("o", "Wo"),
                      ("fk", "Wfk"), ("fr", "Wfr"), ("fv", "Wfv")):
        a["E_w" + name] = w(g[L2 + key].T)
    return {k: np.ascontiguousarray(v) for k, v in a.items()}


def kernel(**inputs):
    import concourse.bacc as bacc
    from concourse.bass_utils import run_bass_kernel_spmd

    nc = bacc.Bacc("TRN2", target_bir_lowering=False, num_devices=1)
    arrays = layout(inputs)
    aps = {k: nc.dram_tensor(f"in_{k}", v.shape, mybir.dt.from_np(v.dtype), kind="ExternalInput").ap()
           for k, v in arrays.items()}
    out = nc.dram_tensor("out", (B, T, D), F32, kind="ExternalOutput").ap()
    build(nc, aps, out)
    result = run_bass_kernel_spmd(nc, [{f"in_{k}": v for k, v in arrays.items()}], core_ids=[0])
    return result.results[0]["out"]
```
